# Optimizing a Trainium2 kernel written in Bass

```python
import numpy as np
import jax
import jax.numpy as jnp

def _softmax(x, axis=-1):
    return jax.nn.softmax(x, axis=axis)

def _gelu(x):
    return jax.nn.gelu(x, approximate=True)

def _silu(x):
    return jax.nn.silu(x)

def _sigmoid(x):
    return jax.nn.sigmoid(x)

def _layernorm(x, axis=-1, eps=1e-05):
    m = jnp.mean(x, axis=axis, keepdims=True)
    v = jnp.var(x, axis=axis, keepdims=True)
    return (x - m) / jnp.sqrt(v + eps)

def _scatter_add(tgt, idx, src, axis=0):
    return tgt.at[idx].add(src)

def _segment_sum(src, seg, n):
    return jax.ops.segment_sum(src, seg, n)
kernel_name = 'mk_vit_tower_d4_tok_img1024_r4_341d21'

def setup_inputs(seed: int=0):
    np.random.seed(seed)
    _w = jnp.asarray

    def _rec_inputs():
        import jax
        import jax.numpy as jnp
        _rk = jax.random.key(seed)
        x = -0.00016672 + 0.999947 * jax.random.normal(jax.random.fold_in(_rk, 1), (16, 3, 96, 96), jnp.float32)
        return x
    x = _rec_inputs()

    def _L0_tok_setup():
        import jax, jax.numpy as jnp
        import numpy as np
        EPS = 1e-05

        def _layernorm(x, w, b):
            mu = jnp.mean(x, axis=-1, keepdims=True)
            var = jnp.mean(jnp.square(x - mu), axis=-1, keepdims=True)
            return (x - mu) * jax.lax.rsqrt(var + EPS) * w + b
        key = jax.random.key(seed)
        ks = jax.random.split(key, 8)
        B, C, H, W = (64, 3, 96, 96)
        P, D = (16, 256)
        patch_dim = C * P * P
        num_patches = H // P * (W // P)
        x = jax.random.normal(ks[0], (B, C, H, W), dtype=jnp.float32)
        ln1_w = jnp.ones((patch_dim,), jnp.float32)
        ln1_b = jnp.zeros((patch_dim,), jnp.float32)
        lin_w = jax.random.normal(ks[1], (patch_dim, D), jnp.float32) / np.sqrt(patch_dim)
        lin_b = jnp.zeros((D,), jnp.float32)
        ln2_w = jnp.ones((D,), jnp.float32)
        ln2_b = jnp.zeros((D,), jnp.float32)
        pos_embedding = jax.random.normal(ks[2], (1, num_patches + 1, D), jnp.float32)
        cls_token = jax.random.normal(ks[3], (1, 1, D), jnp.float32)
        return dict(x=x, ln1_w=ln1_w, ln1_b=ln1_b, lin_w=lin_w, lin_b=lin_b, ln2_w=ln2_w, ln2_b=ln2_b, pos_embedding=pos_embedding, cls_token=cls_token)
    _L0_tok_all = _L0_tok_setup()
    _L0_tok_in = {k: v for k, v in _L0_tok_all.items() if k in ('ln1_w', 'ln1_b', 'lin_w', 'lin_b', 'ln2_w', 'ln2_b', 'pos_embedding', 'cls_token')}
    del _L0_tok_all

    def _L0_attn_setup():
        import jax, jax.numpy as jnp
        import numpy as np
        N_HEADS = 16
        MAX_LEN = 256
        key = jax.random.key(seed)
        ks = jax.random.split(key, 6)
        B, T, C = (4, 256, 256)
        scale = 0.02
        return {'x': jax.random.normal(ks[0], (B, T, C), dtype=jnp.float32), 'qkv_w': jax.random.normal(ks[1], (3 * C, C), dtype=jnp.float32) * scale, 'qkv_b': jax.random.normal(ks[2], (3 * C,), dtype=jnp.float32) * scale, 'proj_w': jax.random.normal(ks[3], (C, C), dtype=jnp.float32) * scale, 'proj_b': jax.random.normal(ks[4], (C,), dtype=jnp.float32) * scale, 'rel_pos_emb': jax.random.normal(ks[5], (2 * MAX_LEN - 1, C), dtype=jnp.float32) * scale}
    _L0_attn_all = _L0_attn_setup()
    _L0_attn_in = {k: v for k, v in _L0_attn_all.items() if k in ('qkv_w', 'qkv_b', 'proj_w', 'proj_b', 'rel_pos_emb')}
    del _L0_attn_all

    def _L0_ffn_setup():
        import jax, jax.numpy as jnp
        import numpy as np
        D, F, E, K = (256, 688, 8, 2)
        key = jax.random.key(seed)
        k0, k1, k2, k3, k4 = jax.random.split(key, 5)
        s = 0.02
        x = jax.random.normal(k0, (2, 128, D), jnp.float32)
        Ws = jax.random.normal(k1, (D, E), jnp.float32) * s
        bs = jnp.zeros((E,), jnp.float32)
        Wg = jax.random.normal(k2, (E, D, F), jnp.float32) * s
        Wu = jax.random.normal(k3, (E, D, F), jnp.float32) * s
        Wd = jax.random.normal(k4, (E, F, D), jnp.float32) * s
        return {'x': x, 'Ws': Ws, 'bs': bs, 'Wg': Wg, 'Wu': Wu, 'Wd': Wd}
    _L0_ffn_all = _L0_ffn_setup()
    _L0_ffn_in = {k: v for k, v in _L0_ffn_all.items() if k in ('Ws', 'bs', 'Wg', 'Wu', 'Wd')}
    del _L0_ffn_all

    def _L1_attn_setup():
        import jax, jax.numpy as jnp
        import numpy as np
        import math
        EMBED_DIM = 256
        NUM_HEADS = 16
        HEAD_DIM = EMBED_DIM // NUM_HEADS // 2
        DEPTH = 12
        LAMBDA_INIT = 0.8 - 0.6 * math.exp(-0.3 * DEPTH)
        RMS_EPS = 1e-05
        key = jax.random.key(seed)
        ks = jax.random.split(key, 10)
        B, S, E = (2, 256, EMBED_DIM)
        w_std = 0.02
        x = jax.random.normal(ks[0], (B, S, E), dtype=jnp.float32)
        Wq = jax.random.normal(ks[1], (E, E), dtype=jnp.float32) * w_std
        Wk = jax.random.normal(ks[2], (E, E), dtype=jnp.float32) * w_std
        Wv = jax.random.normal(ks[3], (E, E), dtype=jnp.float32) * w_std
        Wo = jax.random.normal(ks[4], (E, E), dtype=jnp.float32) * w_std
        lq1 = jax.random.normal(ks[5], (HEAD_DIM,), dtype=jnp.float32) * 0.1
        lk1 = jax.random.normal(ks[6], (HEAD_DIM,), dtype=jnp.float32) * 0.1
        lq2 = jax.random.normal(ks[7], (HEAD_DIM,), dtype=jnp.float32) * 0.1
        lk2 = jax.random.normal(ks[8], (HEAD_DIM,), dtype=jnp.float32) * 0.1
        rms_w = jnp.ones((2 * HEAD_DIM,), dtype=jnp.float32)
        return {'x': x, 'Wq': Wq, 'Wk': Wk, 'Wv': Wv, 'Wo': Wo, 'lq1': lq1, 'lk1': lk1, 'lq2': lq2, 'lk2': lk2, 'rms_w': rms_w}
    _L1_attn_all = _L1_attn_setup()
    _L1_attn_in = {k: v for k, v in _L1_attn_all.items() if k in ('Wq', 'Wk', 'Wv', 'Wo', 'lq1', 'lk1', 'lq2', 'lk2', 'rms_w')}
    del _L1_attn_all

    def _L1_ffn_setup():
        import jax, jax.numpy as jnp
        import numpy as np
        from jax import lax
        H = 256
        I = 256
        E = 16
        TOP_K = 4

        def _swiglu(x, wg, wd, wu):
            return jax.nn.silu(x @ wg.T) * (x @ wu.T) @ wd.T
        key = jax.random.key(seed)
        ks = jax.random.split(key, 9)
        std_gate = 0.02 / E ** 0.5
        return {'hidden_states': jax.random.normal(ks[0], (1, 512, H), jnp.float32), 'gate_w': jax.random.normal(ks[1], (E, H), jnp.float32) * std_gate, 'expert_bias': jnp.zeros((E,), jnp.float32), 'w1': jax.random.normal(ks[2], (E, I, H), jnp.float32) * 0.02, 'w2': jax.random.normal(ks[3], (E, H, I), jnp.float32) * 0.02, 'w3': jax.random.normal(ks[4], (E, I, H), jnp.float32) * 0.02, 'sw1': jax.random.normal(ks[5], (I, H), jnp.float32) * 0.02, 'sw2': jax.random.normal(ks[6], (H, I), jnp.float32) * 0.02, 'sw3': jax.random.normal(ks[7], (I, H), jnp.float32) * 0.02}
    _L1_ffn_all = _L1_ffn_setup()
    _L1_ffn_in = {k: v for k, v in _L1_ffn_all.items() if k in ('gate_w', 'expert_bias', 'w1', 'w2', 'w3', 'sw1', 'sw2', 'sw3')}
    del _L1_ffn_all

    def _L2_attn_setup():
        import jax, jax.numpy as jnp
        import numpy as np
        B, T, C, H, D = (4, 512, 256, 16, 64)
        key = jax.random.key(seed)
        ks = jax.random.split(key, 8)
        s = 0.02
        return {'x': jax.random.normal(ks[0], (B, T, C), jnp.float32), 'Wq': jax.random.normal(ks[1], (C, H * D), jnp.float32) * s, 'Wk': jax.random.normal(ks[2], (C, H * D), jnp.float32) * s, 'Wv': jax.random.normal(ks[3], (C, H * D), jnp.float32) * s, 'Wo': jax.random.normal(ks[4], (H * D, C), jnp.float32) * s, 'null_k': jax.random.normal(ks[5], (1, H, 1, D), jnp.float32) * s, 'null_v': jnp.zeros((1, H, 1, D), jnp.float32), 'logit_scale': jnp.zeros((H,), jnp.float32)}
    _L2_attn_all = _L2_attn_setup()
    _L2_attn_in = {k: v for k, v in _L2_attn_all.items() if k in ('Wq', 'Wk', 'Wv', 'Wo', 'null_k', 'null_v', 'logit_scale')}
    del _L2_attn_all

    def _L2_ffn_setup():
        import jax, jax.numpy as jnp
        import numpy as np
        E, K, H, F = (64, 6, 256, 128)
        SHARED_F = 512
        B, S = (1, 512)
        T = B * S
        CAP = 2 * ((T * K + E - 1) // E)
        key = jax.random.key(seed)
        ks = jax.random.split(key, 6)
        s = 0.05
        return {'hidden_states': jax.random.normal(ks[0], (B, S, H), jnp.float32), 'router_weight': jax.random.normal(ks[1], (E, H), jnp.float32) * s, 'expert_bias': jnp.zeros((E,), jnp.float32), 'w1': jax.random.normal(ks[2], (E, H, F), jnp.float32) * s, 'w2': jax.random.normal(ks[3], (E, F, H), jnp.float32) * s, 'sw1': jax.random.normal(ks[4], (SHARED_F, H), jnp.float32) * s, 'sw2': jax.random.normal(ks[5], (H, SHARED_F), jnp.float32) * s}
    _L2_ffn_all = _L2_ffn_setup()
    _L2_ffn_in = {k: v for k, v in _L2_ffn_all.items() if k in ('router_weight', 'expert_bias', 'w1', 'w2', 'sw1', 'sw2')}
    del _L2_ffn_all

    def _L3_attn_setup():
        import jax, jax.numpy as jnp
        import numpy as np
        D_MODEL = 256
        NHEAD = 16
        HEAD_DIM = D_MODEL // NHEAD
        LN_EPS = 1e-05

        def _ema_scan(lam, v):
            a = jnp.broadcast_to(lam, v.shape)

            def combine(e1, e2):
                a1, b1 = e1
                a2, b2 = e2
                return (a1 * a2, a2 * b1 + b2)
            _, state = jax.lax.associative_scan(combine, (a, v), axis=1)
            return state
        key = jax.random.key(seed)
        ks = jax.random.split(key, 6)
        B, S = (4, 1024)
        x = jax.random.normal(ks[0], (B, S, D_MODEL), dtype=jnp.float32)
        scale = 0.02
        Wq = jax.random.normal(ks[1], (D_MODEL, D_MODEL), dtype=jnp.float32) * scale
        Wv = jax.random.normal(ks[2], (D_MODEL, D_MODEL), dtype=jnp.float32) * scale
        Wo = jax.random.normal(ks[3], (D_MODEL, D_MODEL), dtype=jnp.float32) * scale
        Wg = jax.random.normal(ks[4], (D_MODEL, D_MODEL), dtype=jnp.float32) * scale
        beta = jnp.full((NHEAD,), -0.2, dtype=jnp.float32)
        ln_gamma = jnp.ones((D_MODEL,), dtype=jnp.float32)
        ln_beta = jnp.zeros((D_MODEL,), dtype=jnp.float32)
        return {'x': x, 'Wq': Wq, 'Wv': Wv, 'Wo': Wo, 'Wg': Wg, 'beta': beta, 'ln_gamma': ln_gamma, 'ln_beta': ln_beta}
    _L3_attn_all = _L3_attn_setup()
    _L3_attn_in = {k: v for k, v in _L3_attn_all.items() if k in ('Wq', 'Wv', 'Wo', 'Wg', 'beta', 'ln_gamma', 'ln_beta')}
    del _L3_attn_all

    def _L3_ffn_setup():
        import jax, jax.numpy as jnp
        import numpy as np
        DIM = 256
        INTER = 352
        N_EXPERTS = 16
        TOPK = 2
        N_SHARED = 2
        SHARED_INTER = N_SHARED * INTER
        ROUTE_SCALE = 1.0
        key = jax.random.key(seed)
        ks = jax.random.split(key, 16)
        s = 0.02
        return {'x': jax.random.normal(ks[0], (2, 512, DIM), dtype=jnp.float32), 'gate_w': jax.random.normal(ks[1], (DIM, N_EXPERTS), dtype=jnp.float32) * s, 'gate_b': jnp.zeros((N_EXPERTS,), dtype=jnp.float32), 'w1': jax.random.normal(ks[2], (N_EXPERTS, DIM, INTER), dtype=jnp.float32) * s, 'b1': jnp.zeros((N_EXPERTS, INTER), dtype=jnp.float32), 'w3': jax.random.normal(ks[3], (N_EXPERTS, DIM, INTER), dtype=jnp.float32) * s, 'b3': jnp.zeros((N_EXPERTS, INTER), dtype=jnp.float32), 'w2': jax.random.normal(ks[4], (N_EXPERTS, INTER, DIM), dtype=jnp.float32) * s, 'b2': jnp.zeros((N_EXPERTS, DIM), dtype=jnp.float32), 'sw1': jax.random.normal(ks[5], (DIM, SHARED_INTER), dtype=jnp.float32) * s, 'sb1': jax.random.normal(ks[6], (SHARED_INTER,), dtype=jnp.float32) * s, 'sw3': jax.random.normal(ks[7], (DIM, SHARED_INTER), dtype=jnp.float32) * s, 'sb3': jax.random.normal(ks[8], (SHARED_INTER,), dtype=jnp.float32) * s, 'sw2': jax.random.normal(ks[9], (SHARED_INTER, DIM), dtype=jnp.float32) * s, 'sb2': jax.random.normal(ks[10], (DIM,), dtype=jnp.float32) * s}
    _L3_ffn_all = _L3_ffn_setup()
    _L3_ffn_in = {k: v for k, v in _L3_ffn_all.items() if k in ('gate_w', 'gate_b', 'w1', 'b1', 'w3', 'b3', 'w2', 'b2', 'sw1', 'sb1', 'sw3', 'sb3', 'sw2', 'sb2')}
    del _L3_ffn_all
    return {'x': x, 'L0_tok_ln1_w': _L0_tok_in['ln1_w'], 'L0_tok_ln1_b': _L0_tok_in['ln1_b'], 'L0_tok_lin_w': _L0_tok_in['lin_w'], 'L0_tok_lin_b': _L0_tok_in['lin_b'], 'L0_tok_ln2_w': _L0_tok_in['ln2_w'], 'L0_tok_ln2_b': _L0_tok_in['ln2_b'], 'L0_tok_pos_embedding': _L0_tok_in['pos_embedding'], 'L0_tok_cls_token': _L0_tok_in['cls_token'], 'L0_attn_qkv_w': _L0_attn_in['qkv_w'], 'L0_attn_qkv_b': _L0_attn_in['qkv_b'], 'L0_attn_proj_w': _L0_attn_in['proj_w'], 'L0_attn_proj_b': _L0_attn_in['proj_b'], 'L0_attn_rel_pos_emb': _L0_attn_in['rel_pos_emb'], 'L0_ffn_Ws': _L0_ffn_in['Ws'], 'L0_ffn_bs': _L0_ffn_in['bs'], 'L0_ffn_Wg': _L0_ffn_in['Wg'], 'L0_ffn_Wu': _L0_ffn_in['Wu'], 'L0_ffn_Wd': _L0_ffn_in['Wd'], 'L1_attn_Wq': _L1_attn_in['Wq'], 'L1_attn_Wk': _L1_attn_in['Wk'], 'L1_attn_Wv': _L1_attn_in['Wv'], 'L1_attn_Wo': _L1_attn_in['Wo'], 'L1_attn_lq1': _L1_attn_in['lq1'], 'L1_attn_lk1': _L1_attn_in['lk1'], 'L1_attn_lq2': _L1_attn_in['lq2'], 'L1_attn_lk2': _L1_attn_in['lk2'], 'L1_attn_rms_w': _L1_attn_in['rms_w'], 'L1_ffn_gate_w': _L1_ffn_in['gate_w'], 'L1_ffn_expert_bias': _L1_ffn_in['expert_bias'], 'L1_ffn_w1': _L1_ffn_in['w1'], 'L1_ffn_w2': _L1_ffn_in['w2'], 'L1_ffn_w3': _L1_ffn_in['w3'], 'L1_ffn_sw1': _L1_ffn_in['sw1'], 'L1_ffn_sw2': _L1_ffn_in['sw2'], 'L1_ffn_sw3': _L1_ffn_in['sw3'], 'L2_attn_Wq': _L2_attn_in['Wq'], 'L2_attn_Wk': _L2_attn_in['Wk'], 'L2_attn_Wv': _L2_attn_in['Wv'], 'L2_attn_Wo': _L2_attn_in['Wo'], 'L2_attn_null_k': _L2_attn_in['null_k'], 'L2_attn_null_v': _L2_attn_in['null_v'], 'L2_attn_logit_scale': _L2_attn_in['logit_scale'], 'L2_ffn_router_weight': _L2_ffn_in['router_weight'], 'L2_ffn_expert_bias': _L2_ffn_in['expert_bias'], 'L2_ffn_w1': _L2_ffn_in['w1'], 'L2_ffn_w2': _L2_ffn_in['w2'], 'L2_ffn_sw1': _L2_ffn_in['sw1'], 'L2_ffn_sw2': _L2_ffn_in['sw2'], 'L3_attn_Wq': _L3_attn_in['Wq'], 'L3_attn_Wv': _L3_attn_in['Wv'], 'L3_attn_Wo': _L3_attn_in['Wo'], 'L3_attn_Wg': _L3_attn_in['Wg'], 'L3_attn_beta': _L3_attn_in['beta'], 'L3_attn_ln_gamma': _L3_attn_in['ln_gamma'], 'L3_attn_ln_beta': _L3_attn_in['ln_beta'], 'L3_ffn_gate_w': _L3_ffn_in['gate_w'], 'L3_ffn_gate_b': _L3_ffn_in['gate_b'], 'L3_ffn_w1': _L3_ffn_in['w1'], 'L3_ffn_b1': _L3_ffn_in['b1'], 'L3_ffn_w3': _L3_ffn_in['w3'], 'L3_ffn_b3': _L3_ffn_in['b3'], 'L3_ffn_w2': _L3_ffn_in['w2'], 'L3_ffn_b2': _L3_ffn_in['b2'], 'L3_ffn_sw1': _L3_ffn_in['sw1'], 'L3_ffn_sb1': _L3_ffn_in['sb1'], 'L3_ffn_sw3': _L3_ffn_in['sw3'], 'L3_ffn_sb3': _L3_ffn_in['sb3'], 'L3_ffn_sw2': _L3_ffn_in['sw2'], 'L3_ffn_sb2': _L3_ffn_in['sb2']}

def reference(x, L0_tok_ln1_w, L0_tok_ln1_b, L0_tok_lin_w, L0_tok_lin_b, L0_tok_ln2_w, L0_tok_ln2_b, L0_tok_pos_embedding, L0_tok_cls_token, L0_attn_qkv_w, L0_attn_qkv_b, L0_attn_proj_w, L0_attn_proj_b, L0_attn_rel_pos_emb, L0_ffn_Ws, L0_ffn_bs, L0_ffn_Wg, L0_ffn_Wu, L0_ffn_Wd, L1_attn_Wq, L1_attn_Wk, L1_attn_Wv, L1_attn_Wo, L1_attn_lq1, L1_attn_lk1, L1_attn_lq2, L1_attn_lk2, L1_attn_rms_w, L1_ffn_gate_w, L1_ffn_expert_bias, L1_ffn_w1, L1_ffn_w2, L1_ffn_w3, L1_ffn_sw1, L1_ffn_sw2, L1_ffn_sw3, L2_attn_Wq, L2_attn_Wk, L2_attn_Wv, L2_attn_Wo, L2_attn_null_k, L2_attn_null_v, L2_attn_logit_scale, L2_ffn_router_weight, L2_ffn_expert_bias, L2_ffn_w1, L2_ffn_w2, L2_ffn_sw1, L2_ffn_sw2, L3_attn_Wq, L3_attn_Wv, L3_attn_Wo, L3_attn_Wg, L3_attn_beta, L3_attn_ln_gamma, L3_attn_ln_beta, L3_ffn_gate_w, L3_ffn_gate_b, L3_ffn_w1, L3_ffn_b1, L3_ffn_w3, L3_ffn_b3, L3_ffn_w2, L3_ffn_b2, L3_ffn_sw1, L3_ffn_sb1, L3_ffn_sw3, L3_ffn_sb3, L3_ffn_sw2, L3_ffn_sb2):
    import jax
    import jax.numpy as jnp

    def _L0_tok_ref(x, ln1_w, ln1_b, lin_w, lin_b, ln2_w, ln2_b, pos_embedding, cls_token):
        import jax, jax.numpy as jnp
        import numpy as np
        EPS = 1e-05

        def _layernorm(x, w, b):
            mu = jnp.mean(x, axis=-1, keepdims=True)
            var = jnp.mean(jnp.square(x - mu), axis=-1, keepdims=True)
            return (x - mu) * jax.lax.rsqrt(var + EPS) * w + b
        B, C, H, W = x.shape
        P = 16
        h, w = (H // P, W // P)
        patches = x.reshape(B, C, h, P, w, P)
        patches = patches.transpose(0, 2, 4, 3, 5, 1)
        patches = patches.reshape(B, h * w, P * P * C)
        y = _layernorm(patches, ln1_w, ln1_b)
        y = jnp.einsum('bnp,pd->bnd', y, lin_w) + lin_b
        y = _layernorm(y, ln2_w, ln2_b)
        cls = jnp.broadcast_to(cls_token, (B, 1, y.shape[-1]))
        y = jnp.concatenate([cls, y], axis=1)
        n = h * w
        y = y + pos_embedding[:, :n + 1]
        return y

    def _L0_attn_ref(x, qkv_w, qkv_b, proj_w, proj_b, rel_pos_emb):
        import jax, jax.numpy as jnp
        import numpy as np
        N_HEADS = 16
        MAX_LEN = 256
        B, T, C = x.shape
        H = N_HEADS
        D = C // H
        qkv = (x @ qkv_w.T + qkv_b).reshape(B, T, 3, H, D)
        qkv = jnp.transpose(qkv, (2, 0, 3, 1, 4))
        q, k, v = (qkv[0], qkv[1], qkv[2])
        att = jnp.einsum('bhtd,bhsd->bhts', q, k) / np.sqrt(D).astype(np.float32)
        table = rel_pos_emb.reshape(2 * MAX_LEN - 1, H, D).sum(axis=-1)
        pos = jnp.arange(T)
        rel_idx = pos[:, None] - pos[None, :] + (MAX_LEN - 1)
        bias = jnp.transpose(table[rel_idx], (2, 0, 1))
        att = att + bias[None]
        causal = pos[None, :] > pos[:, None]
        att = jnp.where(causal[None, None], -jnp.inf, att)
        att = jax.nn.softmax(att, axis=-1)
        out = jnp.einsum('bhts,bhsd->bhtd', att, v)
        out = jnp.transpose(out, (0, 2, 1, 3)).reshape(B, T, C)
        return out @ proj_w.T + proj_b

    def _L0_ffn_ref(x, Ws, bs, Wg, Wu, Wd):
        import jax, jax.numpy as jnp
        import numpy as np
        D, F, E, K = (256, 688, 8, 2)
        b, n, d = x.shape
        xt = x.reshape(-1, d)
        logits = xt @ Ws + bs
        topk_w, topk_idx = jax.lax.top_k(logits, K)
        topk_w = jax.nn.softmax(topk_w, axis=-1)
        combine = jnp.sum(jax.nn.one_hot(topk_idx, E, dtype=xt.dtype) * topk_w[..., None], axis=1)
        g = jnp.einsum('td,edf->tef', xt, Wg)
        u = jnp.einsum('td,edf->tef', xt, Wu)
        h = jax.nn.silu(g) * u
        y = jnp.einsum('tef,efd->ted', h, Wd)
        out = jnp.einsum('ted,te->td', y, combine)
        return out.reshape(b, n, d)

    def _L1_attn_ref(x, Wq, Wk, Wv, Wo, lq1, lk1, lq2, lk2, rms_w):
        import jax, jax.numpy as jnp
        import numpy as np
        import math
        EMBED_DIM = 256
        NUM_HEADS = 16
        HEAD_DIM = EMBED_DIM // NUM_HEADS // 2
        DEPTH = 12
        LAMBDA_INIT = 0.8 - 0.6 * math.exp(-0.3 * DEPTH)
        RMS_EPS = 1e-05
        B, S, E = x.shape
        H, d = (NUM_HEADS, HEAD_DIM)
        scaling = d ** (-0.5)
        q = (x @ Wq).reshape(B, S, 2 * H, d).transpose(0, 2, 1, 3) * scaling
        k = (x @ Wk).reshape(B, S, 2 * H, d).transpose(0, 2, 1, 3)
        v = (x @ Wv).reshape(B, S, H, 2 * d).transpose(0, 2, 1, 3)
        scores = jnp.einsum('bhqd,bhkd->bhqk', q, k)
        causal_mask = jnp.triu(jnp.ones((S, S), dtype=bool), 1)
        scores = jnp.where(causal_mask, -jnp.inf, scores)
        probs = jax.nn.softmax(scores, axis=-1)
        lam = jnp.exp(jnp.sum(lq1 * lk1)) - jnp.exp(jnp.sum(lq2 * lk2)) + LAMBDA_INIT
        probs = probs.reshape(B, H, 2, S, S)
        attn_weights = probs[:, :, 0] - lam * probs[:, :, 1]
        attn = jnp.einsum('bhqk,bhkd->bhqd', attn_weights, v)
        attn = attn * jax.lax.rsqrt(jnp.mean(attn * attn, axis=-1, keepdims=True) + RMS_EPS) * rms_w
        attn = attn * (1.0 - LAMBDA_INIT)
        out = attn.transpose(0, 2, 1, 3).reshape(B, S, H * 2 * d) @ Wo
        return out

    def _L1_ffn_ref(hidden_states, gate_w, expert_bias, w1, w2, w3, sw1, sw2, sw3):
        import jax, jax.numpy as jnp
        import numpy as np
        from jax import lax
        H = 256
        I = 256
        E = 16
        TOP_K = 4

        def _swiglu(x, wg, wd, wu):
            return jax.nn.silu(x @ wg.T) * (x @ wu.T) @ wd.T
        B, S, Hd = hidden_states.shape
        x = hidden_states.reshape(-1, Hd)
        T = x.shape[0]
        router_logits = x @ gate_w.T
        biased = router_logits + expert_bias
        _, sel = lax.top_k(biased, TOP_K)
        raw = jnp.take_along_axis(router_logits, sel, axis=-1)
        rw = jax.nn.softmax(raw.astype(jnp.float32), axis=-1).astype(x.dtype)
        g = jnp.zeros((T, E), x.dtype).at[jnp.arange(T)[:, None], sel].add(rw)
        routed = jnp.zeros_like(x)
        for e in range(E):
            routed = routed + g[:, e:e + 1] * _swiglu(x, w1[e], w2[e], w3[e])
        shared = _swiglu(x, sw1, sw2, sw3)
        out = (shared + routed).reshape(B, S, Hd)
        return out

    def _L2_attn_ref(x, Wq, Wk, Wv, Wo, null_k, null_v, logit_scale):
        import jax, jax.numpy as jnp
        import numpy as np
        B, T, C, H, D = (4, 512, 256, 16, 64)
        Bx, Tx, Cx = x.shape
        q = (x @ Wq).reshape(Bx, Tx, H, D).transpose(0, 2, 1, 3)
        k = (x @ Wk).reshape(Bx, Tx, H, D).transpose(0, 2, 1, 3)
        v = (x @ Wv).reshape(Bx, Tx, H, D).transpose(0, 2, 1, 3)
        k = jnp.concatenate([k, jnp.broadcast_to(null_k, (Bx, H, 1, D))], axis=2)
        v = jnp.concatenate([v, jnp.broadcast_to(null_v, (Bx, H, 1, D))], axis=2)
        scale = jnp.exp(logit_scale).reshape(1, H, 1, 1) / jnp.sqrt(jnp.asarray(D, x.dtype))
        att = jnp.einsum('bhtd,bhsd->bhts', q, k) * scale
        causal = jnp.tril(jnp.ones((Tx, Tx), bool))
        causal = jnp.concatenate([causal, jnp.ones((Tx, 1), bool)], axis=1)[None, None]
        att = jnp.where(causal, att, jnp.finfo(att.dtype).min)
        w = jax.nn.softmax(att, axis=-1)
        y = jnp.einsum('bhts,bhsd->bhtd', w, v)
        y = y.transpose(0, 2, 1, 3).reshape(Bx, Tx, H * D)
        return y @ Wo

    def _L2_ffn_ref(hidden_states, router_weight, expert_bias, w1, w2, sw1, sw2):
        import jax, jax.numpy as jnp
        import numpy as np
        E, K, H, F = (64, 6, 256, 128)
        SHARED_F = 512
        B, S = (1, 512)
        T = B * S
        CAP = 2 * ((T * K + E - 1) // E)
        b, s, h = hidden_states.shape
        x = hidden_states.reshape(-1, h)
        t = x.shape[0]
        logits = x @ router_weight.T
        scores = jax.nn.sigmoid(logits)
        _, top_idx = jax.lax.top_k(scores + expert_bias[None, :], K)
        top_scores = jnp.take_along_axis(scores, top_idx, axis=1)
        probs = top_scores / (jnp.sum(top_scores, axis=-1, keepdims=True) + 1e-20)
        flat_e = top_idx.reshape(-1)
        order = jnp.argsort(flat_e)
        sorted_e = flat_e[order]
        token_of = order // K
        counts = jnp.bincount(flat_e, length=E)
        offsets = jnp.cumsum(counts) - counts
        pos = jnp.arange(t * K) - offsets[sorted_e]
        valid = pos < CAP
        slot = jnp.where(valid, sorted_e * CAP + pos, E * CAP)
        xs = jnp.zeros((E * CAP + 1, h), x.dtype).at[slot].set(x[token_of])
        xs = xs[:-1].reshape(E, CAP, h)
        hmid = jax.nn.gelu(jnp.einsum('ech,ehf->ecf', xs, w1), approximate=True)
        y = jnp.einsum('ecf,efh->ech', hmid, w2).reshape(E * CAP, h)
        pair_w = jnp.where(valid, probs.reshape(-1)[order], 0.0)
        y_pair = y[jnp.minimum(slot, E * CAP - 1)] * pair_w[:, None]
        out = jnp.zeros((t, h), x.dtype).at[token_of].add(y_pair)
        shared = jax.nn.gelu(x @ sw1.T, approximate=True) @ sw2.T
        return (out + shared).reshape(b, s, h)

    def _L3_attn_ref(x, Wq, Wv, Wo, Wg, beta, ln_gamma, ln_beta):
        import jax, jax.numpy as jnp
        import numpy as np
        D_MODEL = 256
        NHEAD = 16
        HEAD_DIM = D_MODEL // NHEAD
        LN_EPS = 1e-05

        def _ema_scan(lam, v):
            a = jnp.broadcast_to(lam, v.shape)

            def combine(e1, e2):
                a1, b1 = e1
                a2, b2 = e2
                return (a1 * a2, a2 * b1 + b2)
            _, state = jax.lax.associative_scan(combine, (a, v), axis=1)
            return state
        B, S, _ = x.shape
        q = (x @ Wq.T).reshape(B, S, NHEAD, HEAD_DIM)
        v = (x @ Wv.T).reshape(B, S, NHEAD, HEAD_DIM)
        lam = jax.nn.sigmoid(beta).reshape(1, 1, NHEAD, 1).astype(v.dtype)
        state = _ema_scan(lam, v)
        y = (q * state).reshape(B, S, D_MODEL)
        mu = jnp.mean(y, axis=-1, keepdims=True)
        var = jnp.mean(jnp.square(y - mu), axis=-1, keepdims=True)
        y = (y - mu) * jax.lax.rsqrt(var + LN_EPS) * ln_gamma + ln_beta
        gate = jax.nn.silu(x @ Wg.T)
        y = y * gate
        return y @ Wo.T

    def _L3_ffn_ref(x, gate_w, gate_b, w1, b1, w3, b3, w2, b2, sw1, sb1, sw3, sb3, sw2, sb2):
        import jax, jax.numpy as jnp
        import numpy as np
        DIM = 256
        INTER = 352
        N_EXPERTS = 16
        TOPK = 2
        N_SHARED = 2
        SHARED_INTER = N_SHARED * INTER
        ROUTE_SCALE = 1.0
        shape = x.shape
        xf = x.reshape(-1, DIM)
        logits = xf @ gate_w + gate_b
        scores = jax.nn.softmax(logits.astype(jnp.float32), axis=-1)
        top_vals, top_idx = jax.lax.top_k(scores, TOPK)
        weights = (top_vals * ROUTE_SCALE).astype(x.dtype)
        cw = (jax.nn.one_hot(top_idx, N_EXPERTS, dtype=x.dtype) * weights[..., None]).sum(axis=1)
        h = jnp.einsum('td,edh->teh', xf, w1) + b1
        g = jnp.einsum('td,edh->teh', xf, w3) + b3
        a = jax.nn.silu(h) * g
        y = jnp.einsum('teh,ehd,te->td', a, w2, cw) + cw @ b2
        z = jax.nn.silu(xf @ sw1 + sb1) * (xf @ sw3 + sb3) @ sw2 + sb2
        return (y + z).reshape(shape)
    h = _L0_tok_ref(x, L0_tok_ln1_w, L0_tok_ln1_b, L0_tok_lin_w, L0_tok_lin_b, L0_tok_ln2_w, L0_tok_ln2_b, L0_tok_pos_embedding, L0_tok_cls_token)
    h = h + _L0_attn_ref(_layernorm(h, axis=-1), L0_attn_qkv_w, L0_attn_qkv_b, L0_attn_proj_w, L0_attn_proj_b, L0_attn_rel_pos_emb)
    h = h + _L0_ffn_ref(_layernorm(h, axis=-1), L0_ffn_Ws, L0_ffn_bs, L0_ffn_Wg, L0_ffn_Wu, L0_ffn_Wd)
    h = h + _L1_attn_ref(_layernorm(h, axis=-1), L1_attn_Wq, L1_attn_Wk, L1_attn_Wv, L1_attn_Wo, L1_attn_lq1, L1_attn_lk1, L1_attn_lq2, L1_attn_lk2, L1_attn_rms_w)
    h = h + _L1_ffn_ref(_layernorm(h, axis=-1), L1_ffn_gate_w, L1_ffn_expert_bias, L1_ffn_w1, L1_ffn_w2, L1_ffn_w3, L1_ffn_sw1, L1_ffn_sw2, L1_ffn_sw3)
    h = h + _L2_attn_ref(_layernorm(h, axis=-1), L2_attn_Wq, L2_attn_Wk, L2_attn_Wv, L2_attn_Wo, L2_attn_null_k, L2_attn_null_v, L2_attn_logit_scale)
    h = h + _L2_ffn_ref(_layernorm(h, axis=-1), L2_ffn_router_weight, L2_ffn_expert_bias, L2_ffn_w1, L2_ffn_w2, L2_ffn_sw1, L2_ffn_sw2)
    h = h + _L3_attn_ref(_layernorm(h, axis=-1), L3_attn_Wq, L3_attn_Wv, L3_attn_Wo, L3_attn_Wg, L3_attn_beta, L3_attn_ln_gamma, L3_attn_ln_beta)
    h = h + _L3_ffn_ref(_layernorm(h, axis=-1), L3_ffn_gate_w, L3_ffn_gate_b, L3_ffn_w1, L3_ffn_b1, L3_ffn_w3, L3_ffn_b3, L3_ffn_w2, L3_ffn_b2, L3_ffn_sw1, L3_ffn_sb1, L3_ffn_sw3, L3_ffn_sb3, L3_ffn_sw2, L3_ffn_sb2)
    return h

_drawn_inputs = setup_inputs


def setup_inputs(seed=0):
    import zlib

    import numpy as np

    out = dict(_drawn_inputs(seed))
    spreads = {'L0_tok_ln1_w': (1.0, 0.2),
     'L0_tok_ln1_b': (0.0, 0.1),
     'L0_tok_lin_b': (0.0, 0.1),
     'L0_tok_ln2_w': (1.0, 0.2),
     'L0_tok_ln2_b': (0.0, 0.1),
     'L0_ffn_bs': (0.0, 0.8),
     'L1_attn_rms_w': (1.0, 0.6),
     'L1_ffn_expert_bias': (0.0, 0.8),
     'L2_attn_null_v': (0.0, 0.697),
     'L2_attn_logit_scale': (0.0, 0.8),
     'L2_ffn_expert_bias': (0.0, 0.1),
     'L3_attn_beta': (-0.20000000298023224, 0.6),
     'L3_attn_ln_gamma': (1.0, 0.6),
     'L3_attn_ln_beta': (0.0, 2.0),
     'L3_ffn_gate_b': (0.0, 0.8),
     'L3_ffn_b1': (0.0, 0.8),
     'L3_ffn_b3': (0.0, 0.8),
     'L3_ffn_b2': (0.0, 0.8)}
    factors = {'L0_attn_qkv_b': 7.356,
     'L0_attn_proj_b': 3.244,
     'L0_attn_rel_pos_emb': 8.0,
     'L0_ffn_Ws': 3.919,
     'L0_ffn_Wg': 3.529,
     'L0_ffn_Wu': 3.502,
     'L0_ffn_Wd': 3.469,
     'L1_attn_lq1': 8.0,
     'L1_attn_lk1': 8.0,
     'L1_attn_lq2': 7.289,
     'L1_attn_lk2': 6.779,
     'L1_ffn_gate_w': 7.992,
     'L1_ffn_w1': 7.789,
     'L1_ffn_w2': 6.906,
     'L1_ffn_w3': 6.751,
     'L1_ffn_sw1': 4.077,
     'L1_ffn_sw2': 4.06,
     'L1_ffn_sw3': 3.98,
     'L2_attn_Wq': 8.0,
     'L2_attn_Wk': 8.0,
     'L2_attn_null_k': 64.0,
     'L3_ffn_gate_w': 6.56,
     'L3_ffn_w1': 8.0,
     'L3_ffn_w3': 8.0,
     'L3_ffn_w2': 8.0,
     'L3_ffn_sw1': 3.191,
     'L3_ffn_sb1': 28.118,
     'L3_ffn_sw3': 3.137,
     'L3_ffn_sb3': 27.914,
     'L3_ffn_sw2': 3.139,
     'L3_ffn_sb2': 28.102}
    for name, (base, spread) in spreads.items():
        noise = np.random.default_rng([zlib.crc32(name.encode()), seed]).standard_normal(out[name].shape)
        drawn = base * np.exp(spread * noise) if base else spread * noise
        out[name] = jnp.asarray(drawn.astype(out[name].dtype))
    for name, factor in factors.items():
        out[name] = (out[name] * factor).astype(out[name].dtype)
    return out
```

```python
from contextlib import ExitStack

import numpy as np

import concourse.bass as bass
from concourse import mybir

ALU = mybir.AluOpType
ACT = mybir.ActivationFunctionType
AX = mybir.AxisListType
F32 = mybir.dt.float32
F32R = mybir.dt.float32r


P = 128
B, T, D = 16, 37, 256
N = B * T
HN = N // 2
NPAD = 640
TT = NPAD // P
PB = B * (T - 1)
HP = PB // 2
PD = 768
PK = PD // P
KD = D // P
H = 16
EPS = 1e-5
BANK = 512
MASKED = -1.0e30
SENTINEL = -3.0e38
TAKEN = -2.0e38
LAMBDA_INIT = 0.8 - 0.6 * float(np.exp(-0.3 * 12))
RING = 4

CAPACITY = 2 * ((512 * 6 + 63) // 64)


class AttentionPlan:

    def __init__(self, dv, keys, subs, before):
        self.dv, self.keys, self.subs = dv, keys, subs
        self.chunks = H * dv // P
        self.hpc = P // dv
        self.rounds = 2 * self.chunks // 4
        self.steps = [(p, i) for p in range(B // 2) for i in range(subs)]
        self.at = sum(len(a.steps) for a in before)
        self.pairs_at = len(before) * B // 2


ATT = []
for dv_, keys_, subs_ in ((16, T, 1), (16, T, 2), (64, T + 1, 1)):
    ATT.append(AttentionPlan(dv_, keys_, subs_, list(ATT)))


class ExpertPlan:

    def __init__(self, e, k, f, shared, glu, bias, before):
        self.e, self.k, self.f, self.shared, self.glu, self.bias = e, k, f, shared, glu, bias
        self.shared_chunks = -(-shared // P)
        self.per_expert = f // P
        self.tail_rows = P // e if f % P else 0
        self.tails = (f % P) * e // P
        self.whole = self.shared_chunks + self.per_expert * e
        self.chunks = self.whole + self.tails
        self.width = (6 if glu else 4) * P + (2 if bias else 0)
        self.col = sum(m.e for m in before)
        self.segments = [(0, RING, False)]
        for start, end, final in ((RING, self.whole, not self.tails), (self.whole, self.chunks, True)):
            looped = max(0, end - start - (1 if final else 0)) // RING * RING
            if looped:
                self.segments.append((start, looped, True))
            if end - start - looped > 0:
                self.segments.append((start + looped, end - start - looped, False))
        self.up_cols = (4 if glu else 2) * P
        self.split_cols = self.up_cols + 2 * P
        self.lag = 2
        self.at = sum(2 * m.chunks for m in before)
        self.chunks_at = sum(m.chunks for m in before)
        self.at_glu = sum(2 * m.chunks for m in before if m.glu)
        self.gates_at = [sum(-(-(m.whole - s) // RING) for m in before) for s in range(RING)]
        self.weights_at = [sum(-(-(m.chunks - s) // RING) for m in before) for s in range(RING)]


MOE = []
for fields_ in ((8, 2, 688, 0, True, False), (16, 4, 256, 256, True, False),
                (64, 6, 128, 512, False, False), (16, 2, 352, 704, True, True)):
    MOE.append(ExpertPlan(*fields_, list(MOE)))
E_ALL = sum(m.e for m in MOE)
W_MAX = max(m.width for m in MOE)


class NormPlan:

    def __init__(self, n, src, out, after, cols=N, kc=KD, ones="mean_d", w=None, b=None):
        self.n, self.src, self.out, self.after, self.cols = n, src, out, after, cols
        self.kc, self.ones, self.w, self.b = kc, ones, w, b
        self.hc = cols // 2


def packed(fields):
    at, out = 0, {}
    for name, width in fields:
        out[name] = (at, width)
        at += width
    return out, at


CONSTS, CONSTS_W = packed([
    ("ident", P), ("mean_d", P), ("mean_pd", P), ("head16", 8), ("head64", 2), ("sub", 2),
    ("stack37", H), ("stack38", H), ("causal37", T), ("causal38", T + 1)])
VECS, VECS_W = packed([
    ("ln1_w", 6), ("ln1_b", 6), ("lin_b", 2), ("ln2_w", 2), ("ln2_b", 2), ("cls", 2), ("pos", 2 * T),
    ("q_b", 2), ("k_b", 2), ("v_b", 2), ("proj_b", 2), ("lambdas", 32), ("rms_w", 1),
    ("null_k", 8), ("null_v", 8), ("logit_scale", 8), ("beta", 2), ("gamma", 2), ("ln_beta", 2),
    ("sb2", 2), ("router_b", E_ALL)])
WEIGHTS_LO, WEIGHTS_LO_W = packed([("lin", PK * D), ("qkv0", KD * 3 * D), ("o0", KD * D),
                                   ("qkv1", KD * 3 * D), ("o1", KD * D)])
WEIGHTS_2, WEIGHTS_2_W = packed([("qkv2", KD * 3 * 1024), ("o2", 8 * D)])
WEIGHTS_3, WEIGHTS_3_W = packed([("qkv3", KD * 3 * D), ("o3", KD * D)])


def vit_tower(nc, ins, out, last_stage=99):
    ctx = ExitStack()
    with ctx:
        sems = {}

        def sem(name):
            if name not in sems:
                sems[name] = ctx.enter_context(nc.semaphore(name))
            return sems[name]

        def sb(name, shape):
            return ctx.enter_context(nc.sbuf_tensor(name, shape, F32))

        def over(name, shape, at):
            return nc.alloc_sbuf_tensor_at(name, shape, F32R, offset=arena_at + at)

        def spread(ap, axis, n):
            ap = ap.unsqueeze(axis)
            shape = list(ap.shape)
            shape[axis] = n
            return ap.broadcast_to(shape)

        ps = ctx.enter_context(nc.psum_tensor("ps", [P, 8, BANK], F32))

        consts = sb("consts", [P, CONSTS_W])
        vecs = sb("vecs", [P, VECS_W])
        weights = sb("weights", [P, max(WEIGHTS_LO_W, WEIGHTS_2_W, WEIGHTS_3_W)])
        router_w = sb("router_w", [P, KD, E_ALL])
        b2 = sb("b2", [H, D])
        h = sb("h", [P, KD, N])
        xn = sb("xn", [P, KD, NPAD])
        rstd = sb("rstd", [P, 2, HN])
        arena_at = nc.sbuf_base
        arena = sb("arena", [P, 8 * 2 * B * (T + 1)])
        x_hi, x_lo = (over(n, [P, KD, N], 4 * KD * N * i) for i, n in enumerate(("x_hi", "x_lo")))
        hid_hi, hid_lo = (over(n, [P, 2, HN], 4 * (2 * KD * N + 2 * HN * i))
                          for i, n in enumerate(("hid_hi", "hid_lo")))
        w_hi, w_lo = (over(n, [P, RING, 6 * P], 4 * (2 * KD * N + 4 * HN + RING * 6 * P * i))
                      for i, n in enumerate(("w_hi", "w_lo")))
        q_raw = sb("q_raw", [P, 8 * NPAD])
        v_raw = sb("v_raw", [P, 8 * B * (T + 1)])
        k_ring = sb("k_ring", [P, 2, B * (T + 1)])
        v_stack = sb("v_stack", [P, 4, H * 65])
        scores = sb("scores", [P, 2, H * (T + 1)])
        probs = sb("probs", [P, 2, H * 64])
        row_max = sb("row_max", [P, 2, H])
        probs_t = sb("probs_t", [P, 8 * 2 * T + 27])
        sums_r = sb("sums_r", [P, 2, H])
        att_out = sb("att_out", [P, H * 64])
        att_tmp = sb("att_tmp", [P, H * 16])
        bias0 = sb("bias0", [P, H, T])
        small = sb("small", [P, 96])
        w_ring = sb("w_ring", [P, RING, W_MAX])
        g_ring = sb("g_ring", [P, RING, N])
        g_tail = sb("g_tail", [P, N])
        router = {n: sb(f"r_{n}", [P, TT, 72]) for n in ("raw", "logit", "hit", "gate")}
        top8 = sb("top8", [P, TT, 8])
        r_small = sb("r_small", [P, 3, TT])
        gates_t = sb("gates_t", [P, NPAD])
        chosen_t = sb("chosen_t", [P, NPAD])

        def const(name):
            at, w = CONSTS[name]
            return consts[:, at:at + w]

        def vec(name, i=0, n=1):
            at = VECS[name][0] + i
            return vecs[:, at:at + n]

        def region(fields, name, k):
            at, w = fields[name]
            return weights[:, at:at + w].rearrange("p (k n) -> p k n", k=k)

        att_w = {0: (region(WEIGHTS_LO, "qkv0", KD), region(WEIGHTS_LO, "o0", KD)),
                 1: (region(WEIGHTS_LO, "qkv1", KD), region(WEIGHTS_LO, "o1", KD)),
                 2: (region(WEIGHTS_2, "qkv2", KD), region(WEIGHTS_2, "o2", 8)),
                 3: (region(WEIGHTS_3, "qkv3", KD), region(WEIGHTS_3, "o3", KD))}
        lin_w = region(WEIGHTS_LO, "lin", PK)
        ident = const("ident")

        patches = arena[:, 0:PK * PB].rearrange("p (k n) -> p k n", k=PK)
        embed = arena[:, PK * PB:PK * PB + KD * PB].rearrange("p (k n) -> p k n", k=KD)
        rel = arena[:, 0:H * T * 16].rearrange("p (a d) -> p a d", d=16)
        mixed = arena[:, 0:KD * N].rearrange("p (k n) -> p k n", k=KD)
        v_flat = arena[:, KD * N:2 * KD * N].rearrange("p (k n) -> p k n", k=KD)
        decay = arena[:, 2 * KD * N:3 * KD * N].rearrange("p (k n) -> p k n", k=KD)
        state = arena[:, 3 * KD * N:4 * KD * N].rearrange("p (k n) -> p k n", k=KD)
        gate3 = arena[:, 4 * KD * N:5 * KD * N].rearrange("p (k n) -> p k n", k=KD)
        normed3 = arena[:, 5 * KD * N:6 * KD * N].rearrange("p (k n) -> p k n", k=KD)
        q_all = q_raw[:, :].rearrange("p (m n) -> p m n", m=8)
        act_g = scores[:, 0:2, 0:HN]
        gated_u = scores[:, 0:2, HN:2 * HN]
        hidden = probs[:, 0:2, 0:HN]

        def v_view(a):
            return v_raw[:, 0:a.chunks * B * a.keys].rearrange("p (m b s) -> p m b s", m=a.chunks, b=B)

        def k_view(a, slot):
            return k_ring[:, slot, 0:B * a.keys].rearrange("p (b s) -> p b s", b=B)

        def kblk_view(a):
            return arena[:, 0:H * B * a.keys].rearrange("p (m j b s) -> p m j b s", m=a.chunks, j=a.hpc, b=B)

        def stack_view(a, slot):
            return v_stack[:, slot, 0:H * (a.dv + 1)].rearrange("p (h d) -> p h d", h=H)

        def stack_parts(a, p, r, odd):
            S, slot = a.keys, 2 * (p % 2)
            rows = slice(64 * odd, 64 * odd + S)
            if a.chunks == 2:
                src = ps[0:S, 4, :].rearrange("p (i h e d) -> p i h e d", i=2, e=2, d=a.dv)[:, :, :, odd, :]
                dst = v_stack[:, slot:slot + 2, 0:H * (a.dv + 1)].rearrange("p i (h e d) -> p i h e d", e=2, d=a.dv + 1)
                return src, dst[rows, :, :, odd, 0:a.dv]
            img, half = divmod(r, 2)
            src = ps[0:S, 4, :].rearrange("p (h e d) -> p h e d", e=2, d=a.dv)[:, :, odd, :]
            dst = stack_view(a, slot + img).rearrange("p (h e) d -> p h e d", e=2)
            return src, dst[rows, 4 * half:4 * half + 4, odd, 0:a.dv]

        def stack_mask(a):
            return const("stack37" if a.keys == T else "stack38")

        gate_rows = {l: nc.dram_tensor(f"gate_rows{l}", [m.whole + H, N], F32, kind="Internal").ap()
                     for l, m in enumerate(MOE)}

        def chunk_walk(eng, m, body):
            for first, count, looped in m.segments:
                if looped:
                    with eng.Fori(0, count // RING) as i:
                        for j in range(RING):
                            body(i * RING + (first + j), first + j, i)
                else:
                    for c in range(first, first + count):
                        body(c, c, 0)

        norms = [NormPlan("patch", patches, patches, ("ln_in_patch", 16), PB, PK, "mean_pd", "ln1_w", "ln1_b"),
                 NormPlan("embed", embed, embed, ("embed_done", 4), PB, w="ln2_w", b="ln2_b")]
        for l in range(4):
            norms.append(NormPlan(f"att{l}", h, xn, ("h_embed", 1) if l == 0 else (f"h_moe{l - 1}", 4)))
            if l == 3:
                norms.append(NormPlan("ema", mixed, normed3, ("mixed", 1), w="gamma", b="ln_beta"))
            norms.append(NormPlan(f"moe{l}", h, xn, (f"h_att{l}", 4)))
        for at, s in enumerate(norms):
            s.at = 2 * at
            s.cen = q_raw[:, 0:s.kc * s.cols].rearrange("p (k n) -> p k n", k=s.kc)
            s.sq = v_raw[:, 0:s.kc * s.cols].rearrange("p (k n) -> p k n", k=s.kc)
        norm_of = {s.n: s for s in norms}

        block = ctx.enter_context(nc.Block())

        @block.sync
        def _(sp):
            sp.dma_start(patches, ins["patches"]).then_inc(sem("ln_in_patch"), 16)
            sp.dma_start(consts[:, :], ins["consts"]).then_inc(sem("consts_in"), 16)
            sp.dma_start(vecs[:, :], ins["vecs"]).then_inc(sem("vecs_in"), 16)
            sp.dma_start(weights[:, 0:WEIGHTS_LO_W], ins["weights_lo"]).then_inc(sem("att_w0"), 16)
            sp.dma_start(router_w[:, :, :], ins["router_w"]).then_inc(sem("router_w_in"), 16)
            sp.dma_start(b2[:, :], ins["b2"]).then_inc(sem("router_w_in"), 16)
            sp.wait_ge(sem("rel_cleared"), 1)
            sp.dma_start(rel[0:T], ins["rel"]).then_inc(sem("rel_in"), 16)
            sp.dma_start(rel[64:64 + T], ins["rel"]).then_inc(sem("rel_in"), 16)
            for l, m in enumerate(MOE):
                if last_stage < 2 * l + 2:
                    break
                w_in = ins[f"experts{l}"]

                def load_weights(c, place, i):
                    slot = place % RING
                    sp.dma_start(w_ring[:, slot, 0:m.width], w_in[c]).then_inc(sem(f"w_in{slot}"), 16)

                def load_gate(c, place, i):
                    if place < m.whole:
                        slot = place % RING
                        row = gate_rows[l][bass.ds(c, 1), :].broadcast_to([P, N])
                        sp.dma_start(g_ring[:, slot, :], row).then_inc(sem(f"gate_in{slot}"), 16)

                if l >= 1:
                    sp.wait_ge(sem("down_done"), m.at)
                for c in range(RING):
                    load_weights(c, c, 0)
                sp.wait_ge(sem(f"gates_ready{l}"), 1)
                n_rows = 0
                if m.shared_chunks:
                    for s in range(m.shared_chunks):
                        sp.dma_start(gate_rows[l][s:s + 1, :], chosen_t[0:1, 0:N]).then_inc(sem(f"rows_out{l}"), 16)
                        n_rows += 1
                for f in range(m.per_expert):
                    at = m.shared_chunks + f * m.e
                    sp.dma_start(gate_rows[l][at:at + m.e, :], gates_t[0:m.e, 0:N]).then_inc(sem(f"rows_out{l}"), 16)
                    n_rows += 1
                sp.wait_ge(sem(f"rows_out{l}"), 16 * n_rows)
                for c in range(RING):
                    load_gate(c, c, 0)
                if m.tails:
                    for e in range(m.e):
                        r = m.tail_rows
                        row = gate_rows[l][m.shared_chunks + e:m.shared_chunks + e + 1, :].broadcast_to([r, N])
                        sp.dma_start(g_tail[e * r:(e + 1) * r, :], row).then_inc(sem(f"tail_in{l}"), 16)

                def stream(c, place, i):
                    if place < RING:
                        return
                    sp.wait_ge(sem("down_done"), m.at + i * (2 * RING) + 2 * (place - RING) + 2)
                    load_weights(c, place, i)
                    load_gate(c, place, i)

                chunk_walk(sp, m, stream)
                if l == 1:
                    sp.dma_start(weights[:, 0:WEIGHTS_2_W], ins["weights_2"]).then_inc(sem("att_w2"), 16)
                if l == 2:
                    sp.dma_start(weights[:, 0:WEIGHTS_3_W], ins["weights_3"]).then_inc(sem("att_w3"), 16)
            final = min(last_stage, 8)
            done = "h_embed" if final == 0 else f"h_{'moe' if final % 2 == 0 else 'att'}{(final - 1) // 2}"
            sp.wait_ge(sem(done), 1 if final == 0 else 4)
            sp.dma_start(out, h[:, :, :]).then_inc(sem("out_stored"), 16)
            sp.wait_ge(sem("out_stored"), 16)

        @block.tensor
        def _(pe):
            def norm(s):
                pe.wait_ge(sem(s.after[0]), s.after[1])
                for t in range(2):
                    for k in range(s.kc):
                        mm = pe.matmul(ps[:, 4 + t, 0:s.hc], const(s.ones), s.src[:, k, t * s.hc:(t + 1) * s.hc],
                                       start=(k == 0), stop=(k == s.kc - 1))
                    mm.then_inc(sem("mean"), 1)
                for t in range(2):
                    pe.wait_ge(sem("square"), s.at + t + 1)
                    for k in range(s.kc):
                        mm = pe.matmul(ps[:, 6 + t, 0:s.hc], const(s.ones), s.sq[:, k, t * s.hc:(t + 1) * s.hc],
                                       start=(k == 0), stop=(k == s.kc - 1))
                    mm.then_inc(sem("var"), 1)

            def project(l, w, chunks):
                pe.wait_ge(sem(f"att_w{0 if l == 1 else l}"), 16)
                pe.wait_ge(sem(f"normed_att{l}"), 2)
                j = 0
                for m in range(3 * chunks):
                    for t in range(2):
                        if j >= 8:
                            pe.wait_ge(sem(f"proj_out{l}_{j % 2}"), (j - 8) // 2 + 1)
                        for k in range(KD):
                            mm = pe.matmul(ps[:, j % 8, 0:HN], w[:, k, m * P:(m + 1) * P],
                                           xn[:, k, t * HN:(t + 1) * HN], start=(k == 0), stop=(k == KD - 1))
                        mm.then_inc(sem(f"proj{l}"), 1)
                        j += 1

            def attention(l):
                a = ATT[l]
                w_qkv, w_o = att_w[l]
                project(l, w_qkv, a.chunks)
                kb, vv, S = kblk_view(a), v_view(a), a.keys
                pe.wait_ge(sem("q_pad"), l + 1)
                for par in range(2):
                    pe.wait_ge(sem(f"proj_out{l}_{par}"), 3 * a.chunks)

                pe.wait_ge(sem(f"kblk_chunk_v{l}"), a.chunks)
                pe.wait_ge(sem(f"kblk_chunk_s{l}"), a.chunks)

                def score(s):
                    p, i = a.steps[s]
                    if s >= 1:
                        pe.wait_ge(sem("scored"), a.at + s)
                    for img in range(2):
                        tok = (2 * p + img) * T
                        for m in range(a.chunks):
                            head = m * a.hpc
                            dst = ps[64 * img:64 * img + 64, head // 8,
                                     (head % 8) * S:(head % 8 + a.hpc) * S]
                            mm = pe.matmul(dst, q_all[:, i * a.chunks + m, tok:tok + 64],
                                           kb[:, m, :, 2 * p + img, :], start=(head % 8 == 0),
                                           stop=(head % 8 + a.hpc == 8), skip_group_check=True)
                    mm.then_inc(sem("score"), 1)

                def stack(p):
                    for r in range(a.rounds):
                        if p * a.rounds + r >= 1:
                            pe.wait_ge(sem(f"stacked_even{l}"), p * a.rounds + r)
                            pe.wait_ge(sem(f"stacked_odd{l}"), p * a.rounds + r)
                        for n in range(4):
                            img, m = divmod(4 * r + n, a.chunks)
                            mm = pe.transpose(ps[0:S, 4, n * P:(n + 1) * P], vv[:, m, 2 * p + img, :], ident)
                        mm.then_inc(sem(f"stack{l}"), 1)

                def turn_out(p):
                    if l == 1:
                        pe.wait_ge(sem("att_normed"), p + 1)
                    else:
                        pe.wait_ge(sem("summed"), a.at + p + 1)
                    for m in range(a.chunks):
                        mm = pe.transpose(ps[:, 2 + m // 4, (m % 4) * P:(m % 4 + 1) * P],
                                          att_out[:, m * P:(m + 1) * P], ident)
                    mm.then_inc(sem("turned"), 1)

                def turn_probs(s):
                    p, i = a.steps[s]
                    pe.wait_ge(sem("exped"), a.at + s + 1)
                    if s >= 1:
                        pe.wait_ge(sem("probs_copied"), a.at + s)
                    if i == 0 and p >= 1:
                        pe.wait_ge(sem("out_copied"), a.pairs_at + p)
                    for g in range(8):
                        mm = pe.transpose(ps[:, 2 + g // 4, (g % 4) * P:(g % 4 + 1) * P],
                                          probs[:, s % 2, g * P:(g + 1) * P], ident)
                    mm.then_inc(sem("probs_turned"), 1)

                def values(s):
                    p, i = a.steps[s]
                    pe.wait_ge(sem("probs_copied"), a.at + s + 1)
                    pe.wait_ge(sem(f"stacked_even{l}"), (p + 1) * a.rounds)
                    pe.wait_ge(sem(f"stacked_odd{l}"), (p + 1) * a.rounds)
                    if s >= 1:
                        pe.wait_ge(sem("summed"), a.at + s)
                    d1 = a.dv + 1
                    for img in range(2):
                        st = stack_view(a, 2 * (p % 2) + img)
                        for g in range(8):
                            if l == 2:
                                bank, col = 5 + g // 3, (g % 3) * 2 * d1
                            else:
                                bank, col = 5, g * 2 * d1
                            at = (g * 2 + img) * T
                            mm = pe.matmul(ps[64 * img:64 * img + 64, bank, col:col + 2 * d1], probs_t[:, at:at + 64],
                                           st[:, 2 * g:2 * g + 2, :].rearrange("p h d -> p (h d)"),
                                           start=(col == 0), stop=True, skip_group_check=True)
                    mm.then_inc(sem("valued"), 1)

                last = len(a.steps) - 1
                pe.wait_ge(sem(f"stack_ones{l}"), 1)
                score(0)
                stack(0)
                for s in range(last + 1):
                    p, i = a.steps[s]
                    if s < last:
                        score(s + 1)
                        if a.steps[s + 1][1] == 0:
                            stack(p + 1)
                    if s >= 1 and i == 0:
                        turn_out(p - 1)
                    turn_probs(s)
                    values(s)
                turn_out(B // 2 - 1)
                output(l, w_o, a.chunks, q_all, ("out_copied", a.pairs_at + B // 2))

            def output(l, w_o, chunks, src, after):
                pe.wait_ge(sem(after[0]), after[1])
                for m in range(KD):
                    for t in range(2):
                        for k in range(chunks):
                            mm = pe.matmul(ps[:, 4 + 2 * m + t, 0:HN], w_o[:, k, m * P:(m + 1) * P],
                                           src[:, k, t * HN:(t + 1) * HN], start=(k == 0), stop=(k == chunks - 1))
                        mm.then_inc(sem(f"out_proj{l}"), 1)

            def route(l):
                m = MOE[l]
                pe.wait_ge(sem(f"normed_moe{l}"), 2)
                if l == 0:
                    pe.wait_ge(sem("router_w_in"), 32)
                for t in range(TT):
                    for k in range(KD):
                        mm = pe.matmul(ps[:, 0, t * m.e:(t + 1) * m.e], xn[:, k, t * P:(t + 1) * P],
                                       router_w[:, k, m.col:m.col + m.e], start=(k == 0), stop=(k == KD - 1))
                mm.then_inc(sem(f"logits{l}"), 1)
                pe.wait_ge(sem(f"gated{l}"), 1)
                for n, src in enumerate([router["gate"], router["hit"]][:2 if l == 2 else 1]):
                    for t in range(TT):
                        mm = pe.transpose(ps[0:m.e, 2 * n + t // 4, (t % 4) * P:(t % 4 + 1) * P],
                                          src[:, t, 0:m.e], ident)
                mm.then_inc(sem(f"gates_turned{l}"), 1)

            def experts(l):
                m = MOE[l]
                total = 2 * m.chunks

                def bank_of(place, t):
                    return 4 + 2 * t if m.glu else 4 + 2 * (place % 2) + t

                def split_product(dst, w_at, slot, xh, xl, first, last, **kw):
                    wh, wl = w_hi[:, slot, w_at:w_at + P], w_lo[:, slot, w_at:w_at + P]
                    pe.matmul(dst, wh, xh, start=first, stop=False, **kw)
                    pe.matmul(dst, wh, xl, start=False, stop=False, **kw)
                    return pe.matmul(dst, wl, xh, start=False, stop=last, **kw)

                def up(place, i, t):
                    slot = place % RING
                    if t == 0:
                        pe.wait_ge(sem("w_lo_done"), m.chunks_at + i * RING + place + 1)
                    u = 2 * place + t
                    if m.glu and u >= 2:
                        pe.wait_ge(sem("act_done"), m.at + i * (2 * RING) + u - 1)
                        pe.wait_ge(sem("gated_u"), m.at_glu + i * (2 * RING) + u - 1)
                    elif u >= 4:
                        pe.wait_ge(sem("act_done"), m.at + i * (2 * RING) + u - 3)
                    for n in range(2 if m.glu else 1):
                        for k in range(KD):
                            cols = slice(t * HN, (t + 1) * HN)
                            mm = split_product(ps[:, bank_of(place, t) + n, 0:HN], (n * KD + k) * P, slot,
                                               x_hi[:, k, cols], x_lo[:, k, cols], k == 0, k == KD - 1)
                    mm.then_inc(sem("up_done"), 1)

                def down(place, i, t):
                    slot = place % RING
                    pe.wait_ge(sem("hid_lo_done"), m.at + i * (2 * RING) + 2 * place + t + 1)
                    for d in range(KD):
                        mm = split_product(ps[:, 2 * d + t, 0:HN], m.up_cols + d * P, slot, hid_hi[:, t, :],
                                           hid_lo[:, t, :], place == 0,
                                           2 * place + t >= total - 2 and not m.bias, skip_group_check=True)
                    mm.then_inc(sem("down_done"), 1)

                def down_of(place, t, i):
                    u = 2 * place + t - m.lag
                    if u >= 0:
                        down(u // 2, i, u % 2)

                def body(c, place, i):
                    for t in range(2):
                        up(place, i, t)
                        down_of(place, t, i)

                pe.wait_ge(sem("x_split"), 2 * l + 2)
                chunk_walk(pe, m, body)
                for u in range(total - m.lag, total):
                    down(u // 2, 0, u % 2)
                if m.bias:
                    for d in range(KD):
                        for t in range(2):
                            mm = pe.matmul(ps[:, 2 * d + t, 0:HN], b2[0:m.e, d * P:(d + 1) * P],
                                           gates_t[0:m.e, t * HN:(t + 1) * HN], start=False, stop=True,
                                           skip_group_check=True)
                    mm.then_inc(sem(f"biased{l}"), 1)

            pe.wait_ge(sem("consts_in"), 16)
            norm(norm_of["patch"])
            pe.wait_ge(sem("att_w0"), 16)
            pe.wait_ge(sem("patches_normed"), 2)
            for m in range(KD):
                for t in range(2):
                    for k in range(PK):
                        mm = pe.matmul(ps[:, 2 * m + t, 0:HP], lin_w[:, k, m * P:(m + 1) * P],
                                       patches[:, k, t * HP:(t + 1) * HP], start=(k == 0), stop=(k == PK - 1))
                    mm.then_inc(sem("embedded"), 1)
            norm(norm_of["embed"])
            for l in range(4):
                if last_stage < 2 * l + 1:
                    break
                norm(norm_of[f"att{l}"])
                if l < 3:
                    attention(l)
                else:
                    project(3, att_w[3][0], KD)
                    norm(norm_of["ema"])
                    output(3, att_w[3][1], KD, mixed, ("ema_gated", 1))
                if last_stage < 2 * l + 2:
                    break
                norm(norm_of[f"moe{l}"])
                route(l)
                experts(l)

        @block.scalar
        def _(act):
            def norm(s):
                for t in range(2):
                    act.wait_ge(sem("centred"), s.at + t + 1)
                    cols = slice(t * s.hc, (t + 1) * s.hc)
                    act.activation(s.sq[:, :, cols], s.cen[:, :, cols], ACT.Square).then_inc(sem("square"), 1)
                for t in range(2):
                    act.wait_ge(sem("var_eps"), s.at + t + 1)
                    act.activation(rstd[:, t, 0:s.hc], rstd[:, t, 0:s.hc], ACT.Sqrt).then_inc(sem("std"), 1)

            def from_proj(l, j):
                act.wait_ge(sem(f"proj{l}"), j + 1)

            def attention(l):
                a = ATT[l]
                S = a.keys
                if l == 0:
                    act.wait_ge(sem("q_bias_scaled"), 1)
                for j in range(0, 6 * a.chunks, 2):
                    kind, m = divmod(j // 2, a.chunks)
                    from_proj(l, j)
                    src = ps[:, j % 8, 0:HN]
                    imgs = src.rearrange("p (b s) -> p b s", b=B // 2)
                    done = sem(f"proj_out{l}_0")
                    if kind == 0 and l == 0:
                        act.activation(q_all[:, m, 0:HN], src, ACT.Identity, bias=small[:, m:m + 1],
                                       scale=0.25).then_inc(done, 1)
                    elif kind == 0 and l == 1:
                        if m == 0:
                            act.wait_ge(sem("sub_scaled"), 1)
                        act.activation(q_all[:, m, 0:HN], src, ACT.Identity, scale=small[:, 8:9])
                        act.activation(q_all[:, 2 + m, 0:HN], src, ACT.Identity, scale=small[:, 9:10]).then_inc(done, 1)
                    elif kind == 0:
                        if m == 0:
                            act.wait_ge(sem("logit_scale_ready"), 1)
                        act.activation(q_all[:, m, 0:HN], src, ACT.Identity, scale=small[:, 24 + m:25 + m]).then_inc(done, 1)
                    elif kind == 1:
                        if m >= 2:
                            act.wait_ge(sem(f"kblk_chunk_v{l}"), m - 1)
                            act.wait_ge(sem(f"kblk_chunk_s{l}"), m - 1)
                        bias = vec("k_b", m) if l == 0 else 0.0
                        act.activation(k_view(a, m % 2)[:, 0:B // 2, 0:T], imgs, ACT.Identity, bias=bias).then_inc(done, 1)
                    else:
                        bias = vec("v_b", m) if l == 0 else 0.0
                        act.activation(v_view(a)[:, m, 0:B // 2, 0:T], imgs, ACT.Identity, bias=bias).then_inc(done, 1)
                    if kind == 1:
                        act.wait_ge(sem(f"k_chunk{l}"), m + 1)
                        act.wait_ge(sem(f"proj_out{l}_0"), a.chunks + m + 1)
                        hm = const("head16" if a.dv == 16 else "head64")
                        heads = range(1, a.hpc, 3)
                        for jh in heads:
                            ins_ = act.activation(kblk_view(a)[:, m, jh], k_view(a, m % 2), ACT.Copy, scale=hm[:, jh:jh + 1])
                        ins_.then_inc(sem(f"kblk_chunk_s{l}"), 1)

                def stack_even(p):
                    for r in range(a.rounds):
                        act.wait_ge(sem(f"stack{l}"), p * a.rounds + r + 1)
                        if p >= 2:
                            act.wait_ge(sem("valued"), a.at + (p - 1) * a.subs)
                        src, dst = stack_parts(a, p, r, 0)
                        act.activation(dst, src, ACT.Copy).then_inc(sem(f"stacked_even{l}"), 1)

                last = len(a.steps) - 1
                act.wait_ge(sem(f"stack_ones{l}"), 1)
                stack_even(0)
                for s in range(last + 1):
                    p, i = a.steps[s]
                    act.wait_ge(sem("shifted"), a.at + s + 1)
                    if s >= 2:
                        act.wait_ge(sem("probs_turned"), a.at + s - 1)
                    act.activation(probs[:, s % 2, :].rearrange("p (h k) -> p h k", h=H)[:, :, 0:S],
                                   scores[:, s % 2, 0:H * S].rearrange("p (h s) -> p h s", h=H),
                                   ACT.Exp).then_inc(sem("exped"), 1)
                    if s < last and a.steps[s + 1][1] == 0:
                        stack_even(p + 1)
                    if s >= 1 and i == 0:
                        copy_out(l, a, p - 1)
                    act.wait_ge(sem("probs_turned"), a.at + s + 1)
                    if s >= 1:
                        act.wait_ge(sem("valued"), a.at + s)
                    pt = probs_t[:, 0:16 * T].rearrange("p (g i t) -> p g i t", g=8, i=2)
                    src = ps[:, 2:4, :].rearrange("p b (g i t) -> p (b g) i t", g=4, i=2)
                    ins_ = act.activation(pt, src[:, :, :, 0:T], ACT.Copy)
                    ins_.then_inc(sem("probs_copied"), 1)
                    if l == 1 and i == 1:
                        root_mean_square(p)
                copy_out(l, a, B // 2 - 1)

            def root_mean_square(p):
                act.wait_ge(sem("mean_square"), p + 1)
                act.activation(sums_r[:, 0, :], sums_r[:, 0, :], ACT.Sqrt).then_inc(sem("rms_ready"), 1)

            def copy_out(l, a, p):
                act.wait_ge(sem("turned"), a.pairs_at + p + 1)
                src = ps[:, 2:4, :].rearrange("p b (m i t) -> p (b m) i t", m=4, i=2)[:, 0:a.chunks, :, 0:T]
                dst = q_all[:, 0:a.chunks, 2 * p * T:2 * (p + 1) * T].rearrange("p m (i t) -> p m i t", i=2)
                if l == 1:
                    act.activation(dst, src, ACT.Copy, scale=small[:, 10:11]).then_inc(sem("out_copied"), 1)
                else:
                    act.activation(dst, src, ACT.Copy).then_inc(sem("out_copied"), 1)

            def route(l):
                m = MOE[l]
                if l == 2:
                    act.wait_ge(sem("logits2"), 1)
                    src = ps[:, 0, 0:TT * m.e].rearrange("p (t e) -> p t e", t=TT)
                    act.activation(router["raw"][:, :, 0:m.e], src, ACT.Sigmoid).then_inc(sem("sigmoid2"), 1)
                else:
                    act.wait_ge(sem(f"raw_shifted{l}"), 1)
                    act.activation(router["gate"][:, :, 0:m.e], router["gate"][:, :, 0:m.e], ACT.Exp).then_inc(sem(f"raw_exp{l}"), 1)

            def split_weights(l, place, i):
                m = MOE[l]
                slot = place % RING
                act.wait_ge(sem(f"w_in{slot}"), i * 16 + 16 * (place // RING + 1 + m.weights_at[slot]))
                if place >= RING:
                    act.wait_ge(sem("down_done"), m.at + i * (2 * RING) + 2 * (place - RING) + 2)
                act.activation(w_hi[:, slot, 0:m.split_cols], w_ring[:, slot, 0:m.split_cols],
                               ACT.Copy).then_inc(sem("w_hi_done"), 1)

            def experts(l):
                m = MOE[l]
                func = ACT.Silu if m.glu else ACT.Gelu_apprx_tanh

                def high_part(i, u):
                    unit = m.at + i * (2 * RING) + u
                    act.wait_ge(sem("hidden_done"), unit + 1)
                    if u >= 2:
                        act.wait_ge(sem("down_done"), unit - 1)
                    act.activation(hid_hi[:, u % 2, :], hidden[:, u % 2, :], ACT.Copy).then_inc(sem("hid_hi_done"), 1)

                def body(c, place, i):
                    for t in range(2):
                        u = 2 * place + t
                        unit = m.at + i * (2 * RING) + u
                        act.wait_ge(sem("up_done"), unit + 1)
                        if u >= 2:
                            act.wait_ge(sem("hidden_done"), unit - 1)
                        bias = w_ring[:, place % RING, 6 * P:6 * P + 1] if m.bias else 0.0
                        bank = 4 + 2 * t if m.glu else 4 + 2 * (place % 2) + t
                        act.activation(act_g[:, t, :], ps[:, bank, 0:HN], func, bias=bias).then_inc(sem("act_done"), 1)
                        if u >= 1:
                            high_part(i, u - 1)
                        if t == 0 and place < m.chunks - 1:
                            split_weights(l, place + 1, i)

                chunk_walk(act, m, body)
                high_part(0, 2 * m.chunks - 1)

            act.wait_ge(sem("ln_in_patch"), 16)
            norm(norm_of["patch"])
            norm(norm_of["embed"])
            act.wait_ge(sem("lambda_sums"), 1)
            act.activation(small[:, 12:14], small[:, 14:16], ACT.Exp).then_inc(sem("lambda_exp"), 1)
            act.activation(small[:, 32:40], vec("logit_scale", 0, 8), ACT.Exp).then_inc(sem("logit_exp"), 1)
            act.activation(small[:, 40:42], vec("beta", 0, 2), ACT.Sigmoid).then_inc(sem("decay_ready"), 1)
            for l in range(4):
                if last_stage < 2 * l + 1:
                    break
                norm(norm_of[f"att{l}"])
                if l < 3:
                    attention(l)
                else:
                    for j in range(0, 12, 2):
                        kind, m = divmod(j // 2, KD)
                        from_proj(3, j)
                        dst = (q_all, v_flat, gate3)[kind]
                        act.activation(dst[:, m, 0:HN], ps[:, j % 8, 0:HN],
                                       ACT.Silu if kind == 2 else ACT.Copy).then_inc(sem("proj_out3_0"), 1)
                    for m in range(KD):
                        j = 9 + 2 * m
                        from_proj(3, j)
                        act.activation(gate3[:, m, HN:N], ps[:, j % 8, 0:HN], ACT.Silu).then_inc(sem("gate_out3"), 1)
                    norm(norm_of["ema"])
                if last_stage < 2 * l + 2:
                    break
                norm(norm_of[f"moe{l}"])
                for t in range(2):
                    cols = slice(t * HN, (t + 1) * HN)
                    act.wait_ge(sem(f"normed_moe{l}"), t + 1)
                    act.activation(x_hi[:, :, cols], xn[:, :, cols], ACT.Copy).then_inc(sem("x_hi_done"), 1)
                split_weights(l, 0, 0)
                route(l)
                experts(l)

        @block.gpsimd
        def _(pool):
            pool.memset(xn[:, :, N:NPAD], 0.0).then_inc(sem("xn_pad"), 1)
            pool.memset(probs_t[:, :], 1.0).then_inc(sem("probs_t_pad"), 1)
            pool.memset(att_out[:, :], 0.0).then_inc(sem("att_out_pad"), 1)
            pool.wait_ge(sem("h_embed"), 1)
            pool.memset(arena[:, 0:H * T * 16], 0.0).then_inc(sem("rel_cleared"), 1)
            for l in range(4):
                if last_stage < 2 * l + 1:
                    break
                a = ATT[l] if l < 3 else None
                if a:
                    if l:
                        pool.wait_ge(sem(f"h_moe{l - 1}"), 4)
                    pool.memset(v_stack[:, :, :], 0.0).then_inc(sem(f"att_zeroed{l}"), 1)
                    pool.memset(probs[:, :, :], 0.0).then_inc(sem(f"att_zeroed{l}"), 1)
                for s in range(len(a.steps) if a else 0):
                    S = a.keys
                    pool.wait_ge(sem("maxed"), a.at + s + 1)
                    sc = scores[:, s % 2, 0:H * S].rearrange("p (h s) -> p h s", h=H)
                    pool.tensor_tensor(sc, sc, spread(row_max[:, s % 2, :], 2, S), ALU.subtract).then_inc(sem("shifted"), 1)

        @block.vector
        def _(dve):
            chain = [0]

            def link(ins_):
                chain[0] += 1
                ins_.then_inc(sem("vector_chain"), 1)
                dve.wait_ge(sem("vector_chain"), chain[0])

            def norm(s, done):
                dve.wait_ge(sem(s.after[0]), s.after[1])
                for t in range(2):
                    cols = slice(t * s.hc, (t + 1) * s.hc)
                    dve.wait_ge(sem("mean"), s.at + t + 1)
                    dve.tensor_tensor(s.cen[:, :, cols], s.src[:, :, cols], spread(ps[:, 4 + t, 0:s.hc], 1, s.kc),
                                      ALU.subtract).then_inc(sem("centred"), 1)
                dve.wait_ge(sem("centred"), s.at + 2)
                for t in range(2):
                    cols = slice(t * s.hc, (t + 1) * s.hc)
                    dve.wait_ge(sem("var"), s.at + t + 1)
                    dve.tensor_scalar(rstd[:, t, 0:s.hc], ps[:, 6 + t, 0:s.hc], EPS, None, ALU.add).then_inc(sem("var_eps"), 1)
                for t in range(2):
                    cols = slice(t * s.hc, (t + 1) * s.hc)
                    dve.wait_ge(sem("std"), s.at + t + 1)
                    link(dve.reciprocal(rstd[:, t, 0:s.hc], rstd[:, t, 0:s.hc]))
                    ins_ = dve.tensor_tensor(s.out[:, :, cols], s.cen[:, :, cols], spread(rstd[:, t, 0:s.hc], 1, s.kc), ALU.mult)
                    if s.w:
                        link(ins_)
                        for k in range(s.kc):
                            ins_ = dve.tensor_scalar(s.out[:, k, cols], s.out[:, k, cols], vec(s.w, k), vec(s.b, k),
                                                     ALU.mult, ALU.add)
                    ins_.then_inc(sem(done), 1)

            def attention(l):
                a = ATT[l]
                S = a.keys
                dve.memset(q_all[:, 0:a.subs * a.chunks, N:NPAD], 0.0).then_inc(sem("q_pad"), 1)
                dve.wait_ge(sem(f"att_zeroed{l}"), 2)
                ones = v_stack[:, :, 0:H * (a.dv + 1)].rearrange("p i (h d) -> p i h d", h=H)[:, :, :, a.dv]
                dve.tensor_copy(ones, spread(stack_mask(a), 1, 4)).then_inc(sem(f"stack_ones{l}"), 1)
                if l == 2:
                    for slot in range(2):
                        link(dve.memset(k_ring[:, slot, :], 0.0))
                    for m in range(a.chunks):
                        link(dve.tensor_copy(v_view(a)[:, m, :, T:S], spread(vec("null_v", m), 1, B)))
                    link(dve.tensor_scalar(small[:, 24:32], small[:, 32:40], 0.125, None, ALU.mult))
                    dve.tensor_copy(small[:, 92:93], small[:, 24:25]).then_inc(sem("logit_scale_ready"), 1)
                for j in range(1, 6 * a.chunks, 2):
                    kind, m = divmod(j // 2, a.chunks)
                    dve.wait_ge(sem(f"proj{l}"), j + 1)
                    src = ps[:, j % 8, 0:HN]
                    imgs = src.rearrange("p (b s) -> p b s", b=B // 2)
                    done = sem(f"proj_out{l}_1")
                    if kind == 0 and l == 0:
                        dve.tensor_scalar(q_all[:, m, HN:N], src, vec("q_b", m), 0.25, ALU.add, ALU.mult).then_inc(done, 1)
                    elif kind == 0 and l == 1:
                        for i in range(2):
                            ins_ = dve.tensor_scalar(q_all[:, 2 * i + m, HN:N], src, small[:, 8 + i:9 + i], None, ALU.mult)
                        ins_.then_inc(done, 1)
                    elif kind == 0:
                        dve.tensor_scalar(q_all[:, m, HN:N], src, small[:, 24 + m:25 + m], None, ALU.mult).then_inc(done, 1)
                    elif kind == 1:
                        if m >= 2:
                            dve.wait_ge(sem(f"kblk_chunk_v{l}"), m - 1)
                            dve.wait_ge(sem(f"kblk_chunk_s{l}"), m - 1)
                        dst = k_view(a, m % 2)[:, B // 2:B, 0:T]
                        if l == 0:
                            dve.tensor_scalar(dst, imgs, vec("k_b", m), None, ALU.add).then_inc(done, 1)
                        else:
                            dve.tensor_copy(dst, imgs).then_inc(done, 1)
                        if l == 2:
                            link(dve.tensor_copy(k_view(a, m % 2)[:, :, T:S], spread(vec("null_k", m), 1, B)))
                        dve.wait_ge(sem(f"proj_out{l}_1"), a.chunks + m + 1)
                        dve.wait_ge(sem(f"proj_out{l}_0"), a.chunks + m + 1)
                        hm = const("head16" if a.dv == 16 else "head64")
                        first = True
                        for jh in range(a.hpc):
                            if jh % 3 != 1:
                                ins_ = dve.tensor_scalar(kblk_view(a)[:, m, jh], k_view(a, m % 2), hm[:, jh:jh + 1], None, ALU.mult)
                                if first:
                                    ins_.then_inc(sem(f"k_chunk{l}"), 1)
                                    first = False
                                    last_ins = None
                                else:
                                    last_ins = ins_
                        if last_ins is not None:
                            last_ins.then_inc(sem(f"kblk_chunk_v{l}"), 1)
                        else:
                            dve.wait_ge(sem(f"k_chunk{l}"), m + 1)
                            dve.tensor_copy(small[:, 94:95], vec("beta")).then_inc(sem(f"kblk_chunk_v{l}"), 1)
                    else:
                        dst = v_view(a)[:, m, B // 2:B, 0:T]
                        if l == 0:
                            dve.tensor_scalar(dst, imgs, vec("v_b", m), None, ALU.add).then_inc(done, 1)
                        else:
                            dve.tensor_copy(dst, imgs).then_inc(done, 1)


                def scored(s):
                    dve.wait_ge(sem("score"), a.at + s + 1)
                    if s >= 2:
                        dve.wait_ge(sem("exped"), a.at + s - 1)
                    src = ps[:, 0:2, 0:8 * S].rearrange("p b (h s) -> p b h s", h=8)
                    dst = scores[:, s % 2, 0:H * S].rearrange("p (b h s) -> p b h s", b=2, h=8)
                    if l == 0:
                        bias = bias0[:, :, :].rearrange("p (b h) s -> p b h s", b=2)
                    else:
                        bias = spread(spread(const("causal37" if S == T else "causal38"), 1, 8), 1, 2)
                    dve.tensor_tensor(dst, src, bias, ALU.add).then_inc(sem("scored"), 1)
                    dve.wait_ge(sem("scored"), a.at + s + 1)
                    dve.tensor_reduce(row_max[:, s % 2, :], scores[:, s % 2, 0:H * S].rearrange("p (h s) -> p h s", h=H),
                                      AX.X, ALU.max).then_inc(sem("maxed"), 1)

                def stack_odd(p):
                    for r in range(a.rounds):
                        dve.wait_ge(sem(f"stacked_even{l}"), p * a.rounds + r + 1)
                        if p >= 2:
                            dve.wait_ge(sem("valued"), a.at + (p - 1) * a.subs)
                        src, dst = stack_parts(a, p, r, 1)
                        dve.tensor_copy(dst, src).then_inc(sem(f"stacked_odd{l}"), 1)

                def summed(s):
                    p, i = a.steps[s]
                    d1 = a.dv + 1
                    dve.wait_ge(sem("valued"), a.at + s + 1)
                    if i == 0 and p >= 1:
                        dve.wait_ge(sem("turned"), a.pairs_at + p)
                    if l == 2:
                        parts = [(ps[:, 5 + b, 0:n * d1].rearrange("p (h d) -> p h d", h=n), 6 * b, n)
                                 for b, n in enumerate((6, 6, 4))]
                    else:
                        parts = [(ps[:, 5, 0:H * d1].rearrange("p (h d) -> p h d", h=H), 0, H)]
                    for src, h0, n in parts:
                        ins_ = dve.reciprocal(sums_r[:, i, h0:h0 + n], src[:, :, a.dv])
                    link(ins_)
                    if i == 1:
                        link(dve.tensor_scalar(sums_r[:, 1, :], sums_r[:, 1, :], small[:, 11:12], None, ALU.mult))
                    dst = att_tmp[:, :] if i == 1 else att_out[:, 0:H * a.dv]
                    dst = dst.rearrange("p (h d) -> p h d", h=H)
                    for n_, (src, h0, n) in enumerate(parts):
                        ins_ = dve.tensor_tensor(dst[:, h0:h0 + n, :], src[:, :, 0:a.dv],
                                                 spread(sums_r[:, i, h0:h0 + n], 2, a.dv), ALU.mult)
                        if n_ == len(parts) - 1:
                            ins_.then_inc(sem("summed"), 1)
                    if i == 1:
                        dve.wait_ge(sem("summed"), a.at + s + 1)
                        o = att_out[:, 0:H * a.dv]
                        if True:
                            o3 = o.rearrange("p (h d) -> p h d", h=H)
                            link(dve.tensor_tensor(o, o, att_tmp[:, :], ALU.subtract))
                            link(dve.tensor_tensor(att_tmp[:, :], o, o, ALU.mult))
                            link(dve.tensor_reduce(sums_r[:, 0, :], att_tmp[:, :].rearrange("p (h d) -> p h d", h=H), AX.X, ALU.add))
                            dve.tensor_scalar(sums_r[:, 0, :], sums_r[:, 0, :], 1.0 / a.dv, EPS, ALU.mult,
                                              ALU.add).then_inc(sem("mean_square"), 1)
                            dve.wait_ge(sem("rms_ready"), p + 1)
                            link(dve.reciprocal(sums_r[:, 0, :], sums_r[:, 0, :]))
                            dve.tensor_tensor(o3, o3, spread(sums_r[:, 0, :], 2, a.dv), ALU.mult).then_inc(sem("att_normed"), 1)

                last = len(a.steps) - 1
                scored(0)
                stack_odd(0)
                for s in range(last + 1):
                    p, i = a.steps[s]
                    if s >= 1:
                        summed(s - 1)
                    if s < last:
                        scored(s + 1)
                        if a.steps[s + 1][1] == 0:
                            stack_odd(p + 1)
                summed(last)

            def residual(l, bias):
                for m in range(KD):
                    for t in range(2):
                        cols = slice(t * HN, (t + 1) * HN)
                        dve.wait_ge(sem(f"out_proj{l}"), 2 * m + t + 1)
                        src = ps[:, 4 + 2 * m + t, 0:HN]
                        if bias:
                            ins_ = dve.scalar_tensor_tensor(h[:, m, cols], src, vec(bias, m), h[:, m, cols], ALU.add, ALU.add)
                        else:
                            ins_ = dve.tensor_tensor(h[:, m, cols], src, h[:, m, cols], ALU.add)
                        ins_.then_inc(sem(f"h_att{l}"), 1)

            def ema():
                for j in range(1, 8, 2):
                    kind, m = divmod(j // 2, KD)
                    dve.wait_ge(sem("proj3"), j + 1)
                    dve.tensor_copy((q_all, v_flat)[kind][:, m, HN:N], ps[:, j % 8, 0:HN]).then_inc(sem("proj_out3_1"), 1)
                dve.wait_ge(sem("decay_ready"), 1)
                for m in range(KD):
                    link(dve.memset(decay[:, m, :], 1.0))
                    link(dve.tensor_scalar(decay[:, m, :], decay[:, m, :], small[:, 40 + m:41 + m], None, ALU.mult))
                    link(dve.memset(decay[:, m, :].rearrange("p (b t) -> p b t", b=B)[:, :, 0:1], 0.0))
                dve.wait_ge(sem("proj_out3_0"), 4)
                dve.wait_ge(sem("proj_out3_1"), 4)
                for m in range(KD):
                    link(dve.tensor_tensor_scan(state[:, m, :], decay[:, m, :], v_flat[:, m, :], 0.0, ALU.mult, ALU.add))
                dve.tensor_tensor(mixed, q_all[:, 0:KD, 0:N], state, ALU.mult).then_inc(sem("mixed"), 1)
                norm(norm_of["ema"], "normed_ema")
                dve.wait_ge(sem("normed_ema"), 2)
                dve.wait_ge(sem("proj_out3_0"), 6)
                dve.wait_ge(sem("gate_out3"), 2)
                dve.tensor_tensor(mixed, normed3, gate3, ALU.mult).then_inc(sem("ema_gated"), 1)

            def route(l):
                m = MOE[l]
                E, K = m.e, m.k
                raw, logit, hit, gate = (router[n] for n in ("raw", "logit", "hit", "gate"))
                src = ps[:, 0, 0:TT * E].rearrange("p (t e) -> p t e", t=TT)
                bias = spread(vec("router_b", m.col, E), 1, TT)
                dve.wait_ge(sem(f"logits{l}"), 1)
                link(dve.memset(logit[:, :, E:E + 8], SENTINEL))
                if l == 2:
                    dve.wait_ge(sem("sigmoid2"), 1)
                    link(dve.tensor_tensor(logit[:, :, 0:E], raw[:, :, 0:E], bias, ALU.add))
                elif l == 1:
                    link(dve.tensor_copy(raw[:, :, 0:E], src))
                    link(dve.tensor_tensor(logit[:, :, 0:E], raw[:, :, 0:E], bias, ALU.add))
                elif l == 0:
                    link(dve.tensor_tensor(logit[:, :, 0:E], src, bias, ALU.add))
                    link(dve.tensor_copy(raw[:, :, 0:E], logit[:, :, 0:E]))
                else:
                    link(dve.tensor_tensor(raw[:, :, 0:E], src, bias, ALU.add))
                    link(dve.tensor_reduce(r_small[:, 0, :], raw[:, :, 0:E], AX.X, ALU.max))
                    dve.tensor_tensor(gate[:, :, 0:E], raw[:, :, 0:E], spread(r_small[:, 0, :], 2, E),
                                      ALU.subtract).then_inc(sem("raw_shifted3"), 1)
                    dve.wait_ge(sem("raw_exp3"), 1)
                    link(dve.tensor_reduce(r_small[:, 1, :], gate[:, :, 0:E], AX.X, ALU.add))
                    link(dve.reciprocal(r_small[:, 2, :], r_small[:, 1, :]))
                    link(dve.tensor_tensor(raw[:, :, 0:E], gate[:, :, 0:E], spread(r_small[:, 2, :], 2, E), ALU.mult))
                    link(dve.tensor_copy(logit[:, :, 0:E], raw[:, :, 0:E]))
                for t in range(TT):
                    ins_ = dve.max(top8[:, t, :], logit[:, t, 0:E])
                link(ins_)
                link(dve.memset(top8[:, :, K:8], SENTINEL))
                for t in range(TT):
                    ins_ = dve.match_replace(hit[:, t, 0:E + 8], top8[:, t, :], logit[:, t, 0:E + 8], TAKEN)
                link(ins_)
                link(dve.tensor_scalar(hit[:, :, 0:E], hit[:, :, 0:E], TAKEN, None, ALU.is_equal))
                hits = hit[:, :, 0:E]
                if l in (0, 1):
                    link(dve.tensor_scalar(gate[:, :, 0:E], hits, -MASKED, MASKED, ALU.mult, ALU.add))
                    link(dve.tensor_tensor(gate[:, :, 0:E], gate[:, :, 0:E], raw[:, :, 0:E], ALU.add))
                    link(dve.tensor_reduce(r_small[:, 0, :], gate[:, :, 0:E], AX.X, ALU.max))
                    dve.tensor_tensor(gate[:, :, 0:E], gate[:, :, 0:E], spread(r_small[:, 0, :], 2, E),
                                      ALU.subtract).then_inc(sem(f"raw_shifted{l}"), 1)
                    dve.wait_ge(sem(f"raw_exp{l}"), 1)
                elif l == 2:
                    link(dve.tensor_tensor(gate[:, :, 0:E], raw[:, :, 0:E], hits, ALU.mult))
                else:
                    dve.tensor_tensor(gate[:, :, 0:E], raw[:, :, 0:E], hits, ALU.mult).then_inc(sem("gated3"), 1)
                if l != 3:
                    link(dve.tensor_reduce(r_small[:, 1, :], gate[:, :, 0:E], AX.X, ALU.add))
                    if l == 2:
                        link(dve.tensor_scalar(r_small[:, 1, :], r_small[:, 1, :], 1e-20, None, ALU.add))
                    link(dve.reciprocal(r_small[:, 2, :], r_small[:, 1, :]))
                    dve.tensor_tensor(gate[:, :, 0:E], gate[:, :, 0:E], spread(r_small[:, 2, :], 2, E),
                                      ALU.mult).then_inc(sem(f"gated{l}"), 1)
                dve.wait_ge(sem(f"gates_turned{l}"), 1)
                link(dve.tensor_copy(gates_t[0:E, 0:NPAD], ps[0:E, 0:2, :].rearrange("p b n -> p (b n)")[:, 0:NPAD]))
                if l == 2:
                    link(dve.tensor_copy(chosen_t[0:E, 0:NPAD], ps[0:E, 2:4, :].rearrange("p b n -> p (b n)")[:, 0:NPAD]))
                    link(dve.memset(g_tail[0:E, 0:N], 0.0))
                    link(dve.tensor_tensor_scan(g_tail[0:E, 0:N], chosen_t[0:E, 0:N], g_tail[0:E, 0:N], 0.0, ALU.add, ALU.add))
                    link(dve.tensor_scalar(chosen_t[0:E, 0:N], g_tail[0:E, 0:N], float(CAPACITY), None, ALU.is_le))
                    link(dve.tensor_tensor(gates_t[0:E, 0:N], gates_t[0:E, 0:N], chosen_t[0:E, 0:N], ALU.mult))
                dve.memset(chosen_t[0:1, 0:N], 1.0).then_inc(sem(f"gates_ready{l}"), 1)

            def experts(l):
                m = MOE[l]

                def split_weights(place, i):
                    slot = place % RING
                    dve.wait_ge(sem("w_hi_done"), m.chunks_at + i * RING + place + 1)
                    dve.tensor_tensor(w_lo[:, slot, 0:m.split_cols], w_ring[:, slot, 0:m.split_cols],
                                      w_hi[:, slot, 0:m.split_cols].bitcast(F32), ALU.subtract).then_inc(sem("w_lo_done"), 1)

                def low_part(i, u):
                    dve.wait_ge(sem("hid_hi_done"), m.at + i * (2 * RING) + u + 1)
                    dve.tensor_tensor(hid_lo[:, u % 2, :], hidden[:, u % 2, :], hid_hi[:, u % 2, :].bitcast(F32),
                                      ALU.subtract).then_inc(sem("hid_lo_done"), 1)

                def body(c, place, i):
                    slot = place % RING
                    whole = place < m.whole
                    gates = g_ring[:, slot, :] if whole else g_tail[:, :]
                    for t in range(2):
                        u = 2 * place + t
                        unit = m.at + i * (2 * RING) + u
                        cols = slice(t * HN, (t + 1) * HN)
                        if whole and t == 0:
                            dve.wait_ge(sem(f"gate_in{slot}"), i * 16 + 16 * (place // RING + 1 + m.gates_at[slot]))
                        elif place == m.whole and t == 0:
                            dve.wait_ge(sem(f"tail_in{l}"), 16 * m.e)
                        dve.wait_ge(sem("up_done"), unit + 1)
                        if m.glu:
                            if m.bias:
                                ins_ = dve.scalar_tensor_tensor(gated_u[:, t, :], ps[:, 5 + 2 * t, 0:HN],
                                                                w_ring[:, slot, 6 * P + 1:6 * P + 2], gates[:, cols],
                                                                ALU.add, ALU.mult)
                            else:
                                ins_ = dve.tensor_tensor(gated_u[:, t, :], ps[:, 5 + 2 * t, 0:HN], gates[:, cols], ALU.mult)
                            ins_.then_inc(sem("gated_u"), 1)
                            dve.wait_ge(sem("gated_u"), m.at_glu + i * (2 * RING) + u + 1)
                            other = gated_u[:, t, :]
                        else:
                            other = gates[:, cols]
                        dve.wait_ge(sem("act_done"), unit + 1)
                        if u >= 2:
                            dve.wait_ge(sem("hid_lo_done"), unit - 1)
                        dve.tensor_tensor(hidden[:, t, :], act_g[:, t, :], other, ALU.mult).then_inc(sem("hidden_done"), 1)
                        if u >= 1:
                            low_part(i, u - 1)
                        if t == 0 and place < m.chunks - 1:
                            split_weights(place + 1, i)

                split_weights(0, 0)
                chunk_walk(dve, m, body)
                low_part(0, 2 * m.chunks - 1)
                dve.wait_ge(sem("down_done"), m.at + 2 * m.chunks)
                if m.bias:
                    dve.wait_ge(sem(f"biased{l}"), 1)
                for d in range(KD):
                    for t in range(2):
                        cols = slice(t * HN, (t + 1) * HN)
                        src = ps[:, 2 * d + t, 0:HN]
                        if m.bias:
                            ins_ = dve.scalar_tensor_tensor(h[:, d, cols], src, vec("sb2", d), h[:, d, cols], ALU.add, ALU.add)
                        else:
                            ins_ = dve.tensor_tensor(h[:, d, cols], src, h[:, d, cols], ALU.add)
                        ins_.then_inc(sem(f"h_moe{l}"), 1)

            dve.wait_ge(sem("vecs_in"), 16)
            dve.wait_ge(sem("consts_in"), 16)
            link(dve.memset(small[:, :], 0.0))
            lam = vec("lambdas", 0, 32).rearrange("p (a b d) -> p a b d", a=2, b=2)
            link(dve.tensor_tensor(small[:, 16:32].rearrange("p (a d) -> p a d", a=2), lam[:, :, 0, :], lam[:, :, 1, :], ALU.mult))
            dve.tensor_reduce(small[:, 14:16], small[:, 16:32].rearrange("p (a d) -> p a d", a=2), AX.X,
                              ALU.add).then_inc(sem("lambda_sums"), 1)
            dve.tensor_scalar(small[:, 0:2], vec("q_b", 0, 2), 0.25, None, ALU.mult).then_inc(sem("q_bias_scaled"), 1)
            dve.tensor_scalar(small[:, 10:11], vec("rms_w"), 1.0 - LAMBDA_INIT, None, ALU.mult)
            dve.tensor_scalar(small[:, 8:10], const("sub"), float(8) ** -0.5, None, ALU.mult).then_inc(sem("sub_scaled"), 1)
            dve.wait_ge(sem("sub_scaled"), 1)

            norm(norm_of["patch"], "patches_normed")
            for m in range(KD):
                for t in range(2):
                    dve.wait_ge(sem("embedded"), 2 * m + t + 1)
                    dve.tensor_scalar(embed[:, m, t * HP:(t + 1) * HP], ps[:, 2 * m + t, 0:HP], vec("lin_b", m), None,
                                      ALU.add).then_inc(sem("embed_done"), 1)
            norm(norm_of["embed"], "embed_normed")
            dve.wait_ge(sem("embed_normed"), 2)
            pos = vec("pos", 0, 2 * T).rearrange("p (k t) -> p k t", k=KD)
            for m in range(KD):
                hm = h[:, m, :].rearrange("p (b t) -> p b t", b=B)
                dve.tensor_tensor(hm[:, :, 1:T], embed[:, m, :].rearrange("p (b t) -> p b t", b=B),
                                  spread(pos[:, m, 1:T], 1, B), ALU.add)
                link(dve.tensor_tensor(small[:, 4 + m:5 + m], vec("cls", m), pos[:, m, 0:1], ALU.add))
                link(dve.tensor_copy(hm[:, :, 0:1], spread(small[:, 4 + m:5 + m], 1, B)))
            dve.tensor_copy(small[:, 87:88], vec("beta")).then_inc(sem("h_embed"), 1)
            dve.wait_ge(sem("lambda_exp"), 1)
            link(dve.tensor_tensor(small[:, 11:12], small[:, 12:13], small[:, 13:14], ALU.subtract))
            link(dve.tensor_scalar(small[:, 11:12], small[:, 11:12], LAMBDA_INIT, None, ALU.add))
            dve.wait_ge(sem("logit_exp"), 1)
            for n in ("xn_pad", "probs_t_pad", "att_out_pad"):
                dve.wait_ge(sem(n), 1)
            for l in range(4):
                if last_stage < 2 * l + 1:
                    break
                norm(norm_of[f"att{l}"], f"normed_att{l}")
                if l == 0:
                    dve.wait_ge(sem("rel_in"), 32)
                    link(dve.tensor_reduce(bias0[:, :, :].rearrange("p h t -> p (h t)"), rel, AX.X, ALU.add))
                    link(dve.tensor_tensor(bias0[:, :, :], bias0[:, :, :], spread(const("causal37"), 1, H), ALU.add))
                if l < 3:
                    attention(l)
                else:
                    ema()
                residual(l, "proj_b" if l == 0 else None)
                if last_stage < 2 * l + 2:
                    break
                norm(norm_of[f"moe{l}"], f"normed_moe{l}")
                for t in range(2):
                    cols = slice(t * HN, (t + 1) * HN)
                    dve.wait_ge(sem("x_hi_done"), 2 * l + t + 1)
                    dve.tensor_tensor(x_lo[:, :, cols], xn[:, :, cols], x_hi[:, :, cols].bitcast(F32),
                                      ALU.subtract).then_inc(sem("x_split"), 1)
                route(l)
                experts(l)


def lay_out(x):
    f = {k: np.asarray(v) for k, v in x.items()}

    def cols(v):
        return v.reshape(-1, P).T

    def rows(w):
        return w.reshape(-1, P, w.shape[1]).transpose(1, 0, 2).reshape(P, -1)

    out = {}
    img = f["x"].reshape(B, 3, 6, 16, 6, 16).transpose(3, 5, 1, 0, 2, 4).reshape(PD, PB)
    out["patches"] = img.reshape(PK, P, PB).transpose(1, 0, 2)

    p = np.arange(P)
    c = np.zeros((P, CONSTS_W), np.float32)

    def put(arr, fields, name, val):
        at, w = fields[name]
        arr[:, at:at + w] = np.asarray(val).reshape(-1, w)

    tok = p % 64
    put(c, CONSTS, "ident", np.eye(P))
    put(c, CONSTS, "mean_d", np.full((P, P), 1.0 / D))
    put(c, CONSTS, "mean_pd", np.full((P, P), 1.0 / PD))
    put(c, CONSTS, "head16", p[:, None] // 16 == np.arange(8))
    put(c, CONSTS, "head64", p[:, None] // 64 == np.arange(2))
    put(c, CONSTS, "sub", p[:, None] // 8 % 2 == np.arange(2))
    for s in (T, T + 1):
        put(c, CONSTS, f"stack{s}", (p[:, None] // 64 == np.arange(H) % 2) & (tok[:, None] < s))
        keys = np.arange(s)
        hidden = (keys > tok[:, None]) & (tok[:, None] < T) & (keys < T)
        put(c, CONSTS, f"causal{s}", np.where(hidden, MASKED, 0.0))
    out["consts"] = c

    v = np.zeros((P, VECS_W), np.float32)
    for name, src in (("ln1_w", "L0_tok_ln1_w"), ("ln1_b", "L0_tok_ln1_b"), ("lin_b", "L0_tok_lin_b"),
                      ("ln2_w", "L0_tok_ln2_w"), ("ln2_b", "L0_tok_ln2_b"), ("proj_b", "L0_attn_proj_b"),
                      ("gamma", "L3_attn_ln_gamma"), ("ln_beta", "L3_attn_ln_beta"), ("sb2", "L3_ffn_sb2")):
        put(v, VECS, name, cols(f[src]))
    put(v, VECS, "cls", cols(f["L0_tok_cls_token"].reshape(-1)))
    put(v, VECS, "pos", f["L0_tok_pos_embedding"][0, :T].T.reshape(KD, P, T).transpose(1, 0, 2).reshape(P, -1))
    for i, n in enumerate(("q_b", "k_b", "v_b")):
        put(v, VECS, n, cols(f["L0_attn_qkv_b"][i * D:(i + 1) * D]))
    lam = np.concatenate([f[f"L1_attn_{n}"] for n in ("lq1", "lk1", "lq2", "lk2")])
    put(v, VECS, "lambdas", np.tile(lam, (P, 1)))
    put(v, VECS, "rms_w", np.tile(f["L1_attn_rms_w"], 8)[:, None])
    put(v, VECS, "null_k", cols(f["L2_attn_null_k"].reshape(-1)))
    put(v, VECS, "null_v", cols(f["L2_attn_null_v"].reshape(-1)))
    put(v, VECS, "logit_scale", cols(np.repeat(f["L2_attn_logit_scale"], 64)))
    put(v, VECS, "beta", cols(np.repeat(f["L3_attn_beta"], 16)))
    biases = [f["L0_ffn_bs"], f["L1_ffn_expert_bias"], f["L2_ffn_expert_bias"], f["L3_ffn_gate_b"]]
    put(v, VECS, "router_b", np.tile(np.concatenate(biases), (P, 1)))
    out["vecs"] = v

    t = np.arange(T)
    back = (t[:, None] - t[None, :]) + 255
    rel = f["L0_attn_rel_pos_emb"].reshape(511, H, 16)[back]
    out["rel"] = rel.transpose(0, 2, 1, 3).reshape(T, H * T, 16)

    out["weights_lo"] = np.concatenate(
        [rows(f["L0_tok_lin_w"]), rows(f["L0_attn_qkv_w"].T), rows(f["L0_attn_proj_w"].T),
         rows(np.concatenate([f["L1_attn_Wq"], f["L1_attn_Wk"], f["L1_attn_Wv"]], 1)), rows(f["L1_attn_Wo"])], 1)
    out["weights_2"] = np.concatenate(
        [rows(np.concatenate([f["L2_attn_Wq"], f["L2_attn_Wk"], f["L2_attn_Wv"]], 1)), rows(f["L2_attn_Wo"])], 1)
    out["weights_3"] = np.concatenate(
        [rows(np.concatenate([f["L3_attn_Wq"].T, f["L3_attn_Wv"].T, f["L3_attn_Wg"].T], 1)), rows(f["L3_attn_Wo"].T)], 1)
    routers = [f["L0_ffn_Ws"], f["L1_ffn_gate_w"].T, f["L2_ffn_router_weight"].T, f["L3_ffn_gate_w"]]
    out["router_w"] = rows(np.concatenate(routers, 1)).reshape(P, KD, E_ALL)
    out["b2"] = f["L3_ffn_b2"]

    def chunk_rows(m, routed, shared):
        n = routed.shape[2]
        parts = []
        if m.shared:
            s = np.zeros((m.shared_chunks * P, n), np.float32)
            s[:m.shared] = shared
            parts.append(s.reshape(-1, P, n))
        cut = m.per_expert * P
        parts.append(routed[:, :cut].reshape(m.e, m.per_expert, P, n).transpose(1, 0, 2, 3).reshape(-1, P, n))
        if m.tails:
            r = routed[:, cut:].reshape(m.e, m.tails, m.tail_rows, n).transpose(1, 0, 2, 3)
            parts.append(r.reshape(-1, P, n))
        return np.concatenate(parts)

    def pack(l, ups, down, biases=()):
        m = MOE[l]
        cols_ = []
        for routed, shared in ups:
            r = chunk_rows(m, routed, shared)
            cols_.append(r.reshape(-1, P, KD, P).transpose(0, 3, 2, 1).reshape(-1, P, KD * P))
        cols_.append(chunk_rows(m, *down))
        for routed, shared in biases:
            cols_.append(chunk_rows(m, routed[:, :, None], None if shared is None else shared[:, None]))
        return np.concatenate(cols_, 2)

    sw = lambda a: a.transpose(0, 2, 1)
    out["experts0"] = pack(0, [(sw(f["L0_ffn_Wg"]), None), (sw(f["L0_ffn_Wu"]), None)], (f["L0_ffn_Wd"], None))
    out["experts1"] = pack(1, [(f["L1_ffn_w1"], f["L1_ffn_sw1"]), (f["L1_ffn_w3"], f["L1_ffn_sw3"])],
                           (sw(f["L1_ffn_w2"]), f["L1_ffn_sw2"].T))
    out["experts2"] = pack(2, [(sw(f["L2_ffn_w1"]), f["L2_ffn_sw1"])], (f["L2_ffn_w2"], f["L2_ffn_sw2"].T))
    out["experts3"] = pack(3, [(sw(f["L3_ffn_w1"]), f["L3_ffn_sw1"].T), (sw(f["L3_ffn_w3"]), f["L3_ffn_sw3"].T)],
                           (f["L3_ffn_w2"], f["L3_ffn_sw2"]),
                           [(f["L3_ffn_b1"], f["L3_ffn_sb1"]), (f["L3_ffn_b3"], f["L3_ffn_sb3"])])
    return {k: np.ascontiguousarray(a) for k, a in out.items()}


def kernel(**inputs):
    import concourse.bacc as _bacc
    from concourse.bass_utils import run_bass_kernel_spmd as _run

    nc = _bacc.Bacc("TRN2", target_bir_lowering=False, num_devices=1)
    arrays = {f"in_{k}": a for k, a in lay_out(inputs).items()}
    ins = {k[3:]: nc.dram_tensor(k, a.shape, mybir.dt.from_np(a.dtype), kind="ExternalInput").ap()
           for k, a in arrays.items()}
    out = nc.dram_tensor("out_tokens", (P, KD, N), F32, kind="ExternalOutput").ap()
    vit_tower(nc, ins, out)
    r = _run(nc, [arrays], core_ids=[0])
    got = r.results[0]["out_tokens"]
    return np.ascontiguousarray(got.transpose(2, 1, 0).reshape(B, T, D))
```

```python
from contextlib import ExitStack

import numpy as np

import concourse.bass as bass
from concourse import mybir

ALU = mybir.AluOpType
ACT = mybir.ActivationFunctionType
AX = mybir.AxisListType
F32 = mybir.dt.float32
F32R = mybir.dt.float32r


P = 128
B, T, D = 16, 37, 256
N = B * T
HN = N // 2
NPAD = 640
TT = NPAD // P
PB = B * (T - 1)
HP = PB // 2
PD = 768
PK = PD // P
KD = D // P
H = 16
EPS = 1e-5
BANK = 512
MASKED = -1.0e30
SENTINEL = -3.0e38
TAKEN = -2.0e38
LAMBDA_INIT = 0.8 - 0.6 * float(np.exp(-0.3 * 12))
RING = 4

CAPACITY = 2 * ((512 * 6 + 63) // 64)


class AttentionPlan:

    def __init__(self, dv, keys, subs, before):
        self.dv, self.keys, self.subs = dv, keys, subs
        self.chunks = H * dv // P
        self.hpc = P // dv
        self.rounds = 2 * self.chunks // 4
        self.steps = [(p, i) for p in range(B // 2) for i in range(subs)]
        self.group = B // 4 if subs == 2 else 1
        self.groups = B // 2 // self.group
        self.turn_at = [(g + 1) * self.group * subs - 1 for g in range(self.groups - 1)]
        self.out_lag = 2 if subs == 2 else 1
        self.at = sum(len(a.steps) for a in before)
        self.groups_at = sum(a.groups for a in before)


ATT = []
for dv_, keys_, subs_ in ((16, T, 1), (16, T, 2), (64, T + 1, 1)):
    ATT.append(AttentionPlan(dv_, keys_, subs_, list(ATT)))


class ExpertPlan:

    def __init__(self, e, k, f, shared, glu, bias, before):
        self.e, self.k, self.f, self.shared, self.glu, self.bias = e, k, f, shared, glu, bias
        self.shared_chunks = -(-shared // P)
        self.per_expert = f // P
        self.tail_rows = P // e if f % P else 0
        self.tails = (f % P) * e // P
        self.whole = self.shared_chunks + self.per_expert * e
        self.chunks = self.whole + self.tails
        self.width = (6 if glu else 4) * P + (2 if bias else 0)
        self.col = sum(m.e for m in before)
        self.segments = [(0, RING, False)]
        for start, end, final in ((RING, self.whole, not self.tails), (self.whole, self.chunks, True)):
            looped = max(0, end - start - (1 if final else 0)) // RING * RING
            if looped:
                self.segments.append((start, looped, True))
            if end - start - looped > 0:
                self.segments.append((start + looped, end - start - looped, False))
        self.up_cols = (4 if glu else 2) * P
        self.split_cols = self.up_cols + 2 * P
        self.lag = 2
        self.at = sum(2 * m.chunks for m in before)
        self.chunks_at = sum(m.chunks for m in before)
        self.at_glu = sum(2 * m.chunks for m in before if m.glu)
        self.gates_at = [sum(-(-(m.whole - s) // RING) for m in before) for s in range(RING)]
        self.weights_at = [sum(-(-(m.chunks - s) // RING) for m in before) for s in range(RING)]


MOE = []
for fields_ in ((8, 2, 688, 0, True, False), (16, 4, 256, 256, True, False),
                (64, 6, 128, 512, False, False), (16, 2, 352, 704, True, True)):
    MOE.append(ExpertPlan(*fields_, list(MOE)))
E_ALL = sum(m.e for m in MOE)
W_MAX = max(m.width for m in MOE)


class NormPlan:

    def __init__(self, n, src, out, after, cols=N, kc=KD, ones="mean_d", w=None, b=None):
        self.n, self.src, self.out, self.after, self.cols = n, src, out, after, cols
        self.kc, self.ones, self.w, self.b = kc, ones, w, b
        self.hc = cols // 2
        self.tiles = [(t, min(P, cols - t * P)) for t in range(TT)]
        self.pieces = [(0, 0, self.hc, 7, 0), (1, self.hc, 3 * P - self.hc, 7, self.hc),
                       (1, 3 * P, cols - 3 * P, 6, P)]


def packed(fields):
    at, out = 0, {}
    for name, width in fields:
        out[name] = (at, width)
        at += width
    return out, at


CONSTS, CONSTS_W = packed([
    ("ident", P), ("mean_d", P), ("mean_pd", P), ("eps", 8), ("head16", 8), ("head64", 2), ("sub", 2),
    ("stack37", H), ("stack38", H), ("causal37", T), ("causal38", T + 1)])
VECS, VECS_W = packed([
    ("ln1_w", 6), ("ln1_b", 6), ("lin_b", 2), ("ln2_w", 2), ("ln2_b", 2), ("cls", 2), ("pos", 2 * T),
    ("q_b", 2), ("k_b", 2), ("v_b", 2), ("proj_b", 2), ("lambdas", 32), ("rms_w", 1),
    ("null_k", 8), ("null_v", 8), ("logit_scale", 8), ("beta", 2), ("gamma", 2), ("ln_beta", 2),
    ("sb2", 2), ("router_b", E_ALL)])
WEIGHTS_LO, WEIGHTS_LO_W = packed([("lin", PK * D), ("qkv0", KD * 3 * D), ("o0", KD * D),
                                   ("qkv1", KD * 3 * D), ("o1", KD * D)])
WEIGHTS_2, WEIGHTS_2_W = packed([("qkv2", KD * 3 * 1024), ("o2", 8 * D)])
WEIGHTS_3, WEIGHTS_3_W = packed([("qkv3", KD * 3 * D), ("o3", KD * D)])


def vit_tower(nc, ins, out, last_stage=99):
    ctx = ExitStack()
    with ctx:
        sems = {}

        def sem(name):
            if name not in sems:
                sems[name] = ctx.enter_context(nc.semaphore(name))
            return sems[name]

        def sb(name, shape):
            return ctx.enter_context(nc.sbuf_tensor(name, shape, F32))

        def over(name, shape, at):
            return nc.alloc_sbuf_tensor_at(name, shape, F32R, offset=arena_at + at)

        def spread(ap, axis, n):
            ap = ap.unsqueeze(axis)
            shape = list(ap.shape)
            shape[axis] = n
            return ap.broadcast_to(shape)

        ps = ctx.enter_context(nc.psum_tensor("ps", [P, 8, BANK], F32))

        consts = sb("consts", [P, CONSTS_W])
        vecs = sb("vecs", [P, VECS_W])
        weights = sb("weights", [P, max(WEIGHTS_LO_W, WEIGHTS_2_W, WEIGHTS_3_W)])
        router_w = sb("router_w", [P, KD, E_ALL])
        b2 = sb("b2", [H, D])
        h = sb("h", [P, KD, N])
        xn = sb("xn", [P, KD, NPAD])
        arena_at = nc.sbuf_base
        arena = sb("arena", [P, 8 * 2 * B * (T + 1)])
        x_hi, x_lo = (over(n, [P, KD, N], 4 * KD * N * i) for i, n in enumerate(("x_hi", "x_lo")))
        hid_hi, hid_lo = (over(n, [P, 2, HN], 4 * (2 * KD * N + 2 * HN * i))
                          for i, n in enumerate(("hid_hi", "hid_lo")))
        w_hi, w_lo = (over(n, [P, RING, 6 * P], 4 * (2 * KD * N + 4 * HN + RING * 6 * P * i))
                      for i, n in enumerate(("w_hi", "w_lo")))
        q_raw = sb("q_raw", [P, 8 * NPAD])
        v_raw = sb("v_raw", [P, 8 * B * (T + 1)])
        k_ring = sb("k_ring", [P, 2, B * (T + 1)])
        v_stack = sb("v_stack", [P, 4, H * 65])
        scores = sb("scores", [P, 2, H * (T + 1)])
        probs = sb("probs", [P, 2, H * 64])
        row_max = sb("row_max", [P, 2, H])
        probs_t = sb("probs_t", [P, 8 * 2 * T + 27])
        sums_r = sb("sums_r", [P, 2, H])
        att_out = sb("att_out", [P, H * 64])
        att_tmp = sb("att_tmp", [P, H * 16])
        bias0 = sb("bias0", [P, H, T])
        small = sb("small", [P, 96])
        std = sb("std", [P, TT])
        rstd = sb("rstd", [P, TT])
        rms = sb("rms", [P, B // 4 * H])
        act_scratch = sb("act_scratch", [P, 1])
        w_ring = sb("w_ring", [P, RING, W_MAX])
        g_ring = sb("g_ring", [P, RING, N])
        g_tail = sb("g_tail", [P, N])
        router = {n: sb(f"r_{n}", [P, TT, 72]) for n in ("raw", "logit", "hit", "gate")}
        top8 = sb("top8", [P, TT, 8])
        r_small = sb("r_small", [P, 3, TT])
        gates_t = sb("gates_t", [P, NPAD])
        chosen_t = sb("chosen_t", [P, NPAD])

        def const(name):
            at, w = CONSTS[name]
            return consts[:, at:at + w]

        def vec(name, i=0, n=1):
            at = VECS[name][0] + i
            return vecs[:, at:at + n]

        def region(fields, name, k):
            at, w = fields[name]
            return weights[:, at:at + w].rearrange("p (k n) -> p k n", k=k)

        att_w = {0: (region(WEIGHTS_LO, "qkv0", KD), region(WEIGHTS_LO, "o0", KD)),
                 1: (region(WEIGHTS_LO, "qkv1", KD), region(WEIGHTS_LO, "o1", KD)),
                 2: (region(WEIGHTS_2, "qkv2", KD), region(WEIGHTS_2, "o2", 8)),
                 3: (region(WEIGHTS_3, "qkv3", KD), region(WEIGHTS_3, "o3", KD))}
        lin_w = region(WEIGHTS_LO, "lin", PK)
        ident = const("ident")
        eps_col = const("eps")[:, 0:1]

        patches = arena[:, 0:PK * PB].rearrange("p (k n) -> p k n", k=PK)
        embed = arena[:, PK * PB:PK * PB + KD * PB].rearrange("p (k n) -> p k n", k=KD)
        rel = arena[:, 0:H * T * 16].rearrange("p (a d) -> p a d", d=16)
        mixed = arena[:, 0:KD * N].rearrange("p (k n) -> p k n", k=KD)
        v_flat = arena[:, KD * N:2 * KD * N].rearrange("p (k n) -> p k n", k=KD)
        decay = arena[:, 2 * KD * N:3 * KD * N].rearrange("p (k n) -> p k n", k=KD)
        state = arena[:, 3 * KD * N:4 * KD * N].rearrange("p (k n) -> p k n", k=KD)
        gate3 = arena[:, 4 * KD * N:5 * KD * N].rearrange("p (k n) -> p k n", k=KD)
        normed3 = arena[:, 5 * KD * N:6 * KD * N].rearrange("p (k n) -> p k n", k=KD)
        q_all = q_raw[:, :].rearrange("p (m n) -> p m n", m=8)
        act_g = scores[:, 0:2, 0:HN]
        gated_u = scores[:, 0:2, HN:2 * HN]
        hidden = probs[:, 0:2, 0:HN]

        def v_view(a):
            return v_raw[:, 0:a.chunks * B * a.keys].rearrange("p (m b s) -> p m b s", m=a.chunks, b=B)

        def k_view(a, slot):
            return k_ring[:, slot, 0:B * a.keys].rearrange("p (b s) -> p b s", b=B)

        def kblk_view(a):
            return arena[:, 0:H * B * a.keys].rearrange("p (m j b s) -> p m j b s", m=a.chunks, j=a.hpc, b=B)

        v_raw_free = v_raw[:, 2 * B * (T + 1):]

        def stack_view(a, slot):
            return v_stack[:, slot, 0:H * (a.dv + 1)].rearrange("p (h d) -> p h d", h=H)

        def stack_parts(a, p, r, odd):
            S, slot = a.keys, 2 * (p % 2)
            rows = slice(64 * odd, 64 * odd + S)
            if a.chunks == 2:
                src = ps[0:S, 4, :].rearrange("p (i h e d) -> p i h e d", i=2, e=2, d=a.dv)[:, :, :, odd, :]
                dst = v_stack[:, slot:slot + 2, 0:H * (a.dv + 1)].rearrange("p i (h e d) -> p i h e d", e=2, d=a.dv + 1)
                return src, dst[rows, :, :, odd, 0:a.dv]
            img, half = divmod(r, 2)
            src = ps[0:S, 4, :].rearrange("p (h e d) -> p h e d", e=2, d=a.dv)[:, :, odd, :]
            dst = stack_view(a, slot + img).rearrange("p (h e) d -> p h e d", e=2)
            return src, dst[rows, 4 * half:4 * half + 4, odd, 0:a.dv]

        def out_view(l, p):
            if l == 1:
                return g_ring[:, :, :].rearrange("p r n -> p (r n)")[:, p * D:(p + 1) * D]
            return att_out[:, 0:ATT[l].chunks * P]

        out_bank = {0: 7, 1: 6, 2: 2}

        def value_banks(l, s):
            return 5 + s % 2 if l == 0 else 5

        def stack_mask(a):
            return const("stack37" if a.keys == T else "stack38")

        gate_rows = {l: nc.dram_tensor(f"gate_rows{l}", [m.whole + H, N], F32, kind="Internal").ap()
                     for l, m in enumerate(MOE)}

        def chunk_walk(eng, m, body):
            for first, count, looped in m.segments:
                if looped:
                    with eng.Fori(0, count // RING) as i:
                        for j in range(RING):
                            body(i * RING + (first + j), first + j, i)
                else:
                    for c in range(first, first + count):
                        body(c, c, 0)

        norms = [NormPlan("patch", patches, patches, ("ln_in_patch", 16), PB, PK, "mean_pd", "ln1_w", "ln1_b"),
                 NormPlan("embed", embed, embed, ("embed_done", 4), PB, w="ln2_w", b="ln2_b")]
        for l in range(4):
            norms.append(NormPlan(f"att{l}", h, xn, ("h_embed", 1) if l == 0 else (f"h_moe{l - 1}", 4)))
            if l == 3:
                norms.append(NormPlan("ema", mixed, normed3, ("mixed", 1), w="gamma", b="ln_beta"))
            norms.append(NormPlan(f"moe{l}", h, xn, (f"h_att{l}", 4)))
        for at, s in enumerate(norms):
            s.index = at
            s.at = 2 * at
            s.cen = q_raw[:, 0:s.kc * s.cols].rearrange("p (k n) -> p k n", k=s.kc)
            s.sq = v_raw[:, 0:s.kc * s.cols].rearrange("p (k n) -> p k n", k=s.kc)
        norm_of = {s.n: s for s in norms}

        block = ctx.enter_context(nc.Block())

        @block.sync
        def _(sp):
            sp.dma_start(patches, ins["patches"]).then_inc(sem("ln_in_patch"), 16)
            sp.dma_start(consts[:, :], ins["consts"]).then_inc(sem("consts_in"), 16)
            sp.dma_start(vecs[:, :], ins["vecs"]).then_inc(sem("vecs_in"), 16)
            sp.dma_start(weights[:, 0:WEIGHTS_LO_W], ins["weights_lo"]).then_inc(sem("att_w0"), 16)
            sp.dma_start(router_w[:, :, :], ins["router_w"]).then_inc(sem("router_w_in"), 16)
            sp.dma_start(b2[:, :], ins["b2"]).then_inc(sem("router_w_in"), 16)
            sp.wait_ge(sem("rel_cleared"), 1)
            sp.dma_start(rel[0:T], ins["rel"]).then_inc(sem("rel_in"), 16)
            sp.dma_start(rel[64:64 + T], ins["rel"]).then_inc(sem("rel_in"), 16)
            for l, m in enumerate(MOE):
                if last_stage < 2 * l + 2:
                    break
                w_in = ins[f"experts{l}"]

                def load_weights(c, place, i):
                    slot = place % RING
                    sp.dma_start(w_ring[:, slot, 0:m.width], w_in[c]).then_inc(sem(f"w_in{slot}"), 16)

                def load_gate(c, place, i):
                    if place < m.whole:
                        slot = place % RING
                        row = gate_rows[l][bass.ds(c, 1), :].broadcast_to([P, N])
                        sp.dma_start(g_ring[:, slot, :], row).then_inc(sem(f"gate_in{slot}"), 16)

                if l >= 1:
                    sp.wait_ge(sem("down_done"), m.at)
                for c in range(RING):
                    load_weights(c, c, 0)
                sp.wait_ge(sem("gates_ready"), l + 1)
                n_rows = 0
                if m.shared_chunks:
                    for s in range(m.shared_chunks):
                        sp.dma_start(gate_rows[l][s:s + 1, :], chosen_t[0:1, 0:N]).then_inc(sem(f"rows_out{l}"), 16)
                        n_rows += 1
                for f in range(m.per_expert):
                    at = m.shared_chunks + f * m.e
                    sp.dma_start(gate_rows[l][at:at + m.e, :], gates_t[0:m.e, 0:N]).then_inc(sem(f"rows_out{l}"), 16)
                    n_rows += 1
                sp.wait_ge(sem(f"rows_out{l}"), 16 * n_rows)
                for c in range(RING):
                    load_gate(c, c, 0)
                if m.tails:
                    for e in range(m.e):
                        r = m.tail_rows
                        row = gate_rows[l][m.shared_chunks + e:m.shared_chunks + e + 1, :].broadcast_to([r, N])
                        sp.dma_start(g_tail[e * r:(e + 1) * r, :], row).then_inc(sem(f"tail_in{l}"), 16)

                def stream(c, place, i):
                    if place < RING:
                        return
                    sp.wait_ge(sem("down_done"), m.at + i * (2 * RING) + 2 * (place - RING) + 2)
                    load_weights(c, place, i)
                    load_gate(c, place, i)

                chunk_walk(sp, m, stream)
                if l == 1:
                    sp.dma_start(weights[:, 0:WEIGHTS_2_W], ins["weights_2"]).then_inc(sem("att_w2"), 16)
                if l == 2:
                    sp.dma_start(weights[:, 0:WEIGHTS_3_W], ins["weights_3"]).then_inc(sem("att_w3"), 16)
            final = min(last_stage, 8)
            done = "h_embed" if final == 0 else f"h_{'moe' if final % 2 == 0 else 'att'}{(final - 1) // 2}"
            sp.wait_ge(sem(done), 1 if final == 0 else 4)
            sp.dma_start(out, h[:, :, :]).then_inc(sem("out_stored"), 16)
            sp.wait_ge(sem("out_stored"), 16)

        @block.tensor
        def _(pe):
            def norm(s):
                pe.wait_ge(sem(s.after[0]), s.after[1])
                for t in range(2):
                    for k in range(s.kc):
                        mm = pe.matmul(ps[:, 4 + t, 0:s.hc], const(s.ones), s.src[:, k, t * s.hc:(t + 1) * s.hc],
                                       start=(k == 0), stop=(k == s.kc - 1))
                    mm.then_inc(sem("mean"), 1)
                for t, rows in s.tiles:
                    if t in (0, 2):
                        pe.wait_ge(sem("square"), s.at + (1 if t == 0 else 2))
                    for k in range(s.kc):
                        mm = pe.matmul(ps[0:rows, 6, t:t + 1], s.sq[:, k, t * P:t * P + rows], const(s.ones)[:, 0:1],
                                       start=(k == 0), stop=(k == s.kc - 1))
                mm.then_inc(sem("var"), 1)
                pe.wait_ge(sem("rstd_ready"), s.index + 1)
                for t, rows in s.tiles:
                    bank, col = (7, t * P) if t < 3 else (6, (t - 2) * P)
                    mm = pe.matmul(ps[:, bank, col:col + rows], rstd[0:rows, t:t + 1].broadcast_to([rows, P]),
                                   ident[0:rows, 0:rows], start=True, stop=True)
                    if t in (2, TT - 1):
                        mm.then_inc(sem("rstd_spread"), 1)

            def project(l, w, chunks):
                pe.wait_ge(sem(f"att_w{0 if l == 1 else l}"), 16)
                pe.wait_ge(sem(f"normed_att{l}"), 2)
                j = 0
                for m in range(3 * chunks):
                    for t in range(2):
                        if j >= 8:
                            pe.wait_ge(sem(f"proj_out{l}_{j % 2}"), (j - 8) // 2 + 1)
                        for k in range(KD):
                            mm = pe.matmul(ps[:, j % 8, 0:HN], w[:, k, m * P:(m + 1) * P],
                                           xn[:, k, t * HN:(t + 1) * HN], start=(k == 0), stop=(k == KD - 1))
                        mm.then_inc(sem(f"proj{l}"), 1)
                        j += 1

            def attention(l):
                a = ATT[l]
                w_qkv, w_o = att_w[l]
                project(l, w_qkv, a.chunks)
                kb, vv, S = kblk_view(a), v_view(a), a.keys
                pe.wait_ge(sem("q_pad"), l + 1)
                for par in range(2):
                    pe.wait_ge(sem(f"proj_out{l}_{par}"), 3 * a.chunks)

                pe.wait_ge(sem(f"kblk_chunk_v{l}"), a.chunks)
                pe.wait_ge(sem(f"kblk_chunk_s{l}"), a.chunks)

                def score(s):
                    p, i = a.steps[s]
                    if s >= 1:
                        pe.wait_ge(sem("scored"), a.at + s)
                    for img in range(2):
                        tok = (2 * p + img) * T
                        for m in range(a.chunks):
                            head = m * a.hpc
                            dst = ps[64 * img:64 * img + 64, head // 8,
                                     (head % 8) * S:(head % 8 + a.hpc) * S]
                            mm = pe.matmul(dst, q_all[:, i * a.chunks + m, tok:tok + 64],
                                           kb[:, m, :, 2 * p + img, :], start=(head % 8 == 0),
                                           stop=(head % 8 + a.hpc == 8), skip_group_check=True)
                    mm.then_inc(sem("score"), 1)

                def stack(p, r):
                    if p * a.rounds + r >= 1:
                        pe.wait_ge(sem(f"stacked_even{l}"), p * a.rounds + r)
                        pe.wait_ge(sem(f"stacked_odd{l}"), p * a.rounds + r)
                    for n in range(4):
                        img, m = divmod(4 * r + n, a.chunks)
                        mm = pe.transpose(ps[0:S, 4, n * P:(n + 1) * P], vv[:, m, 2 * p + img, :], ident)
                    mm.then_inc(sem(f"stack{l}"), 1)

                def turn_out(g):
                    if l == 1:
                        pe.wait_ge(sem("rms_normed"), g + 1)
                    else:
                        pe.wait_ge(sem("summed"), a.at + g + 1)
                    if g:
                        pe.wait_ge(sem("out_copied"), a.groups_at + g)
                    for n in range(a.group):
                        for m in range(a.chunks):
                            dst = ps[:, out_bank[l] + n // 2 + m // 4, (2 * n % 4 + m % 4) * P:(2 * n % 4 + m % 4 + 1) * P]
                            mm = pe.transpose(dst, out_view(l, g * a.group + n)[:, m * P:(m + 1) * P], ident)
                    mm.then_inc(sem("turned"), 1)

                def turn_probs(s):
                    p, i = a.steps[s]
                    pe.wait_ge(sem("exped"), a.at + s + 1)
                    if s >= 1:
                        pe.wait_ge(sem("probs_copied"), a.at + s)
                    if l == 2 and s >= 2:
                        pe.wait_ge(sem("out_copied"), a.groups_at + s - 1)
                    for g in range(8):
                        mm = pe.transpose(ps[:, 2 + g // 4, (g % 4) * P:(g % 4 + 1) * P],
                                          probs[:, s % 2, g * P:(g + 1) * P], ident)
                    mm.then_inc(sem("probs_turned"), 1)

                def values(s, part):
                    p, i = a.steps[s]
                    if part == 0:
                        pe.wait_ge(sem("probs_copied"), a.at + s + 1)
                        pe.wait_ge(sem(f"stacked_even{l}"), (p + 1) * a.rounds)
                        pe.wait_ge(sem(f"stacked_odd{l}"), (p + 1) * a.rounds)
                        ahead = 2 if l == 0 else 1
                        if s >= ahead:
                            pe.wait_ge(sem("summed"), a.at + s - ahead + 1)
                    d1 = a.dv + 1
                    each = 16 // a.rounds
                    for n in range(part * each, (part + 1) * each):
                        img, g = divmod(n, 8)
                        st = stack_view(a, 2 * (p % 2) + img)
                        if l == 2:
                            bank, col = 5 + g // 3, (g % 3) * 2 * d1
                        else:
                            bank, col = value_banks(l, s), g * 2 * d1
                        at = (g * 2 + img) * T
                        mm = pe.matmul(ps[64 * img:64 * img + 64, bank, col:col + 2 * d1], probs_t[:, at:at + 64],
                                       st[:, 2 * g:2 * g + 2, :].rearrange("p h d -> p (h d)"),
                                       start=(col == 0), stop=True, skip_group_check=True)
                    if part == a.rounds - 1:
                        mm.then_inc(sem("valued"), 1)

                pe.wait_ge(sem("stack_ones"), l + 1)
                score(0)
                for r in range(a.rounds):
                    stack(0, r)
                score(1)
                for s, (p, i) in enumerate(a.steps):
                    turn_probs(s)
                    if s + 2 < len(a.steps):
                        score(s + 2)
                    for r in range(a.rounds):
                        if s + 1 < len(a.steps) and a.steps[s + 1][1] == 0:
                            stack(p + 1, r)
                        values(s, r)
                        if r == 0 and s - a.out_lag in a.turn_at:
                            turn_out(a.turn_at.index(s - a.out_lag))
                turn_out(a.groups - 1)
                output(l, w_o, a.chunks, q_all, ("out_copied", a.groups_at + a.groups))

            def output(l, w_o, chunks, src, after):
                pe.wait_ge(sem(after[0]), after[1])
                for m in range(KD):
                    for t in range(2):
                        for k in range(chunks):
                            mm = pe.matmul(ps[:, 4 + 2 * m + t, 0:HN], w_o[:, k, m * P:(m + 1) * P],
                                           src[:, k, t * HN:(t + 1) * HN], start=(k == 0), stop=(k == chunks - 1))
                        mm.then_inc(sem("out_proj"), 1)

            def route(l):
                m = MOE[l]
                pe.wait_ge(sem(f"normed_moe{l}"), 2)
                if l == 0:
                    pe.wait_ge(sem("router_w_in"), 32)
                for t in range(TT):
                    for k in range(KD):
                        mm = pe.matmul(ps[:, 0, t * m.e:(t + 1) * m.e], xn[:, k, t * P:(t + 1) * P],
                                       router_w[:, k, m.col:m.col + m.e], start=(k == 0), stop=(k == KD - 1))
                mm.then_inc(sem("logits"), 1)
                pe.wait_ge(sem("gated"), l + 1)
                for n, src in enumerate([router["gate"], router["hit"]][:2 if l == 2 else 1]):
                    for t in range(TT):
                        mm = pe.transpose(ps[0:m.e, 2 * n + t // 4, (t % 4) * P:(t % 4 + 1) * P],
                                          src[:, t, 0:m.e], ident)
                mm.then_inc(sem("gates_turned"), 1)

            def experts(l):
                m = MOE[l]
                total = 2 * m.chunks

                def bank_of(place, t):
                    return 4 + 2 * t if m.glu else 4 + 2 * (place % 2) + t

                def split_product(dst, w_at, slot, xh, xl, first, last, **kw):
                    wh, wl = w_hi[:, slot, w_at:w_at + P], w_lo[:, slot, w_at:w_at + P]
                    pe.matmul(dst, wh, xh, start=first, stop=False, **kw)
                    pe.matmul(dst, wh, xl, start=False, stop=False, **kw)
                    return pe.matmul(dst, wl, xh, start=False, stop=last, **kw)

                def up(place, i, t):
                    slot = place % RING
                    if t == 0:
                        pe.wait_ge(sem("w_lo_done"), m.chunks_at + i * RING + place + 1)
                    u = 2 * place + t
                    if m.glu and u >= 2:
                        pe.wait_ge(sem("act_done"), m.at + i * (2 * RING) + u - 1)
                        pe.wait_ge(sem("gated_u"), m.at_glu + i * (2 * RING) + u - 1)
                    elif u >= 4:
                        pe.wait_ge(sem("act_done"), m.at + i * (2 * RING) + u - 3)
                    for n in range(2 if m.glu else 1):
                        for k in range(KD):
                            cols = slice(t * HN, (t + 1) * HN)
                            mm = split_product(ps[:, bank_of(place, t) + n, 0:HN], (n * KD + k) * P, slot,
                                               x_hi[:, k, cols], x_lo[:, k, cols], k == 0, k == KD - 1)
                    mm.then_inc(sem("up_done"), 1)

                def down(place, i, t):
                    slot = place % RING
                    pe.wait_ge(sem("hid_lo_done"), m.at + i * (2 * RING) + 2 * place + t + 1)
                    for d in range(KD):
                        mm = split_product(ps[:, 2 * d + t, 0:HN], m.up_cols + d * P, slot, hid_hi[:, t, :],
                                           hid_lo[:, t, :], place == 0,
                                           2 * place + t >= total - 2 and not m.bias, skip_group_check=True)
                    mm.then_inc(sem("down_done"), 1)

                def down_of(place, t, i):
                    u = 2 * place + t - m.lag
                    if u >= 0:
                        down(u // 2, i, u % 2)

                def body(c, place, i):
                    for t in range(2):
                        up(place, i, t)
                        down_of(place, t, i)

                pe.wait_ge(sem("x_split"), 2 * l + 2)
                chunk_walk(pe, m, body)
                for u in range(total - m.lag, total):
                    down(u // 2, 0, u % 2)
                if m.bias:
                    for d in range(KD):
                        for t in range(2):
                            mm = pe.matmul(ps[:, 2 * d + t, 0:HN], b2[0:m.e, d * P:(d + 1) * P],
                                           gates_t[0:m.e, t * HN:(t + 1) * HN], start=False, stop=True,
                                           skip_group_check=True)
                    mm.then_inc(sem(f"biased{l}"), 1)

            pe.wait_ge(sem("consts_in"), 16)
            norm(norm_of["patch"])
            pe.wait_ge(sem("att_w0"), 16)
            pe.wait_ge(sem("patches_normed"), 2)
            for m in range(KD):
                for t in range(2):
                    for k in range(PK):
                        mm = pe.matmul(ps[:, 2 * m + t, 0:HP], lin_w[:, k, m * P:(m + 1) * P],
                                       patches[:, k, t * HP:(t + 1) * HP], start=(k == 0), stop=(k == PK - 1))
                    mm.then_inc(sem("embedded"), 1)
            norm(norm_of["embed"])
            for l in range(4):
                if last_stage < 2 * l + 1:
                    break
                norm(norm_of[f"att{l}"])
                if l < 3:
                    attention(l)
                else:
                    project(3, att_w[3][0], KD)
                    norm(norm_of["ema"])
                    output(3, att_w[3][1], KD, mixed, ("ema_gated", 1))
                if last_stage < 2 * l + 2:
                    break
                norm(norm_of[f"moe{l}"])
                route(l)
                experts(l)

        @block.scalar
        def _(act):
            loaded = [0]

            def load_table(func):
                if loaded[0]:
                    act.wait_ge(sem("table_loaded"), loaded[0])
                loaded[0] += 1
                act.activation(act_scratch[:, :], ident[:, 0:1], func).then_inc(sem("table_loaded"), 1)

            def norm(s, after=None):
                load_table(ACT.Sqrt)
                for t in range(2):
                    act.wait_ge(sem("centred"), s.at + t + 1)
                    cols = slice(t * s.hc, (t + 1) * s.hc)
                    act.activation(s.sq[:, :, cols], s.cen[:, :, cols], ACT.Square).then_inc(sem("square"), 1)
                act.wait_ge(sem("var"), s.index + 1)
                rows = s.tiles[-1][1]
                act.activation(std[:, 0:TT - 1], ps[:, 6, 0:TT - 1], ACT.Sqrt, bias=eps_col)
                act.activation(std[0:rows, TT - 1:TT], ps[0:rows, 6, TT - 1:TT], ACT.Sqrt,
                               bias=eps_col[0:rows]).then_inc(sem("std"), 1)
                if after is not None:
                    load_table(after)

            def from_proj(l, j):
                act.wait_ge(sem(f"proj{l}"), j + 1)

            def attention(l):
                a = ATT[l]
                S = a.keys
                if l == 0:
                    act.wait_ge(sem("q_bias_scaled"), 1)
                for j in range(0, 6 * a.chunks, 2):
                    kind, m = divmod(j // 2, a.chunks)
                    from_proj(l, j)
                    src = ps[:, j % 8, 0:HN]
                    imgs = src.rearrange("p (b s) -> p b s", b=B // 2)
                    done = sem(f"proj_out{l}_0")
                    if kind == 0 and l == 0:
                        act.activation(q_all[:, m, 0:HN], src, ACT.Identity, bias=small[:, m:m + 1],
                                       scale=0.25).then_inc(done, 1)
                    elif kind == 0 and l == 1:
                        if m == 0:
                            act.wait_ge(sem("sub_scaled"), 1)
                        act.activation(q_all[:, m, 0:HN], src, ACT.Identity, scale=small[:, 8:9])
                        act.activation(q_all[:, 2 + m, 0:HN], src, ACT.Identity, scale=small[:, 9:10]).then_inc(done, 1)
                    elif kind == 0:
                        if m == 0:
                            act.wait_ge(sem("logit_scale_ready"), 1)
                        act.activation(q_all[:, m, 0:HN], src, ACT.Identity, scale=small[:, 24 + m:25 + m]).then_inc(done, 1)
                    elif kind == 1:
                        if m >= 2:
                            act.wait_ge(sem(f"kblk_chunk_v{l}"), m - 1)
                            act.wait_ge(sem(f"kblk_chunk_s{l}"), m - 1)
                        bias = vec("k_b", m) if l == 0 else 0.0
                        act.activation(k_view(a, m % 2)[:, 0:B // 2, 0:T], imgs, ACT.Identity, bias=bias).then_inc(done, 1)
                    else:
                        bias = vec("v_b", m) if l == 0 else 0.0
                        act.activation(v_view(a)[:, m, 0:B // 2, 0:T], imgs, ACT.Identity, bias=bias).then_inc(done, 1)
                    if kind == 1:
                        act.wait_ge(sem(f"k_chunk{l}"), m + 1)
                        act.wait_ge(sem(f"proj_out{l}_0"), a.chunks + m + 1)
                        hm = const("head16" if a.dv == 16 else "head64")
                        heads = range(1, a.hpc, 3)
                        for jh in heads:
                            ins_ = act.activation(kblk_view(a)[:, m, jh], k_view(a, m % 2), ACT.Copy, scale=hm[:, jh:jh + 1])
                        ins_.then_inc(sem(f"kblk_chunk_s{l}"), 1)

                def stack_even(p, rounds):
                    for r in rounds:
                        act.wait_ge(sem(f"stack{l}"), p * a.rounds + r + 1)
                        if p >= 2:
                            act.wait_ge(sem("valued"), a.at + (p - 1) * a.subs)
                        src, dst = stack_parts(a, p, r, 0)
                        act.activation(dst, src, ACT.Copy).then_inc(sem(f"stacked_even{l}"), 1)

                def exponentials(s):
                    act.wait_ge(sem("shifted"), a.at + s + 1)
                    if s >= 2:
                        act.wait_ge(sem("probs_turned"), a.at + s - 1)
                    act.activation(probs[:, s % 2, :].rearrange("p (h k) -> p h k", h=H)[:, :, 0:S],
                                   scores[:, s % 2, 0:H * S].rearrange("p (h s) -> p h s", h=H),
                                   ACT.Exp).then_inc(sem("exped"), 1)

                act.wait_ge(sem("stack_ones"), l + 1)
                stack_even(0, range(a.rounds))
                exponentials(0)
                for s, (p, i) in enumerate(a.steps):
                    if s + 1 < len(a.steps):
                        exponentials(s + 1)
                    stacks = s + 1 < len(a.steps) and a.steps[s + 1][1] == 0
                    if stacks:
                        stack_even(p + 1, range(1))
                    act.wait_ge(sem("probs_turned"), a.at + s + 1)
                    if s >= 1:
                        act.wait_ge(sem("valued"), a.at + s)
                    pt = probs_t[:, 0:16 * T].rearrange("p (g i t) -> p g i t", g=8, i=2)
                    src = ps[:, 2:4, :].rearrange("p b (g i t) -> p (b g) i t", g=4, i=2)
                    act.activation(pt, src[:, :, :, 0:T], ACT.Copy).then_inc(sem("probs_copied"), 1)
                    if l == 1 and s - 1 in a.turn_at:
                        root_mean_square(a.turn_at.index(s - 1))
                    if stacks:
                        stack_even(p + 1, range(1, min(2, a.rounds)))
                    if s - a.out_lag in a.turn_at:
                        copy_out(l, a, a.turn_at.index(s - a.out_lag))
                    if stacks:
                        stack_even(p + 1, range(2, a.rounds))
                if l == 1:
                    load_table(ACT.Sqrt)
                    root_mean_square(a.groups - 1)
                copy_out(l, a, a.groups - 1)

            def root_mean_square(g):
                act.wait_ge(sem("mean_square"), g + 1)
                act.activation(rms[:, :], rms[:, :], ACT.Sqrt).then_inc(sem("rms_ready"), 1)

            def copy_out(l, a, g):
                act.wait_ge(sem("turned"), a.groups_at + g + 1)
                for n in range(a.group):
                    p = g * a.group + n
                    bank = out_bank[l] + n // 2
                    src = ps[:, bank:bank + a.chunks // 4 + 1, :].rearrange("p b (m i t) -> p (b m) i t", m=4, i=2)
                    at = 2 * n % 4
                    src = src[:, at:at + a.chunks, :, 0:T]
                    dst = q_all[:, 0:a.chunks, 2 * p * T:2 * (p + 1) * T].rearrange("p m (i t) -> p m i t", i=2)
                    ins_ = act.activation(dst, src, ACT.Copy, scale=small[:, 10:11] if l == 1 else 1.0)
                ins_.then_inc(sem("out_copied"), 1)

            def route(l):
                m = MOE[l]
                if l == 2:
                    act.wait_ge(sem("logits"), l + 1)
                    src = ps[:, 0, 0:TT * m.e].rearrange("p (t e) -> p t e", t=TT)
                    act.activation(router["raw"][:, :, 0:m.e], src, ACT.Sigmoid).then_inc(sem("sigmoid2"), 1)
                else:
                    act.wait_ge(sem(f"raw_shifted{l}"), 1)
                    act.activation(router["gate"][:, :, 0:m.e], router["gate"][:, :, 0:m.e], ACT.Exp).then_inc(sem(f"raw_exp{l}"), 1)

            def split_weights(l, place, i):
                m = MOE[l]
                slot = place % RING
                act.wait_ge(sem(f"w_in{slot}"), i * 16 + 16 * (place // RING + 1 + m.weights_at[slot]))
                if place >= RING:
                    act.wait_ge(sem("down_done"), m.at + i * (2 * RING) + 2 * (place - RING) + 2)
                act.activation(w_hi[:, slot, 0:m.split_cols], w_ring[:, slot, 0:m.split_cols],
                               ACT.Copy).then_inc(sem("w_hi_done"), 1)

            def experts(l):
                m = MOE[l]
                func = ACT.Silu if m.glu else ACT.Gelu_apprx_tanh

                def high_part(i, u):
                    unit = m.at + i * (2 * RING) + u
                    act.wait_ge(sem("hidden_done"), unit + 1)
                    if u >= 2:
                        act.wait_ge(sem("down_done"), unit - 1)
                    act.activation(hid_hi[:, u % 2, :], hidden[:, u % 2, :], ACT.Copy).then_inc(sem("hid_hi_done"), 1)

                def body(c, place, i):
                    for t in range(2):
                        u = 2 * place + t
                        unit = m.at + i * (2 * RING) + u
                        act.wait_ge(sem("up_done"), unit + 1)
                        if u >= 2:
                            act.wait_ge(sem("hidden_done"), unit - 1)
                        bias = w_ring[:, place % RING, 6 * P:6 * P + 1] if m.bias else 0.0
                        bank = 4 + 2 * t if m.glu else 4 + 2 * (place % 2) + t
                        act.activation(act_g[:, t, :], ps[:, bank, 0:HN], func, bias=bias).then_inc(sem("act_done"), 1)
                        if u >= 1:
                            high_part(i, u - 1)
                        if t == 0 and place < m.chunks - 1:
                            split_weights(l, place + 1, i)

                chunk_walk(act, m, body)
                high_part(0, 2 * m.chunks - 1)

            act.wait_ge(sem("consts_in"), 16)
            norm(norm_of["patch"])
            norm(norm_of["embed"], ACT.Exp)
            act.wait_ge(sem("lambda_sums"), 1)
            act.activation(small[:, 12:14], small[:, 14:16], ACT.Exp).then_inc(sem("lambda_exp"), 1)
            act.activation(small[:, 32:40], vec("logit_scale", 0, 8), ACT.Exp).then_inc(sem("logit_exp"), 1)
            act.activation(small[:, 40:42], vec("beta", 0, 2), ACT.Sigmoid).then_inc(sem("decay_ready"), 1)
            for l in range(4):
                if last_stage < 2 * l + 1:
                    break
                norm(norm_of[f"att{l}"], ACT.Exp if l < 3 else ACT.Silu)
                if l < 3:
                    attention(l)
                else:
                    for j in range(0, 12, 2):
                        kind, m = divmod(j // 2, KD)
                        from_proj(3, j)
                        dst = (q_all, v_flat, gate3)[kind]
                        act.activation(dst[:, m, 0:HN], ps[:, j % 8, 0:HN],
                                       ACT.Silu if kind == 2 else ACT.Copy).then_inc(sem("proj_out3_0"), 1)
                    for m in range(KD):
                        j = 9 + 2 * m
                        from_proj(3, j)
                        act.activation(gate3[:, m, HN:N], ps[:, j % 8, 0:HN], ACT.Silu).then_inc(sem("gate_out3"), 1)
                    norm(norm_of["ema"])
                if last_stage < 2 * l + 2:
                    break
                norm(norm_of[f"moe{l}"], ACT.Sigmoid if l == 2 else ACT.Exp)
                for t in range(2):
                    cols = slice(t * HN, (t + 1) * HN)
                    act.wait_ge(sem(f"normed_moe{l}"), t + 1)
                    act.activation(x_hi[:, :, cols], xn[:, :, cols], ACT.Copy).then_inc(sem("x_hi_done"), 1)
                split_weights(l, 0, 0)
                route(l)
                load_table(ACT.Silu if MOE[l].glu else ACT.Gelu_apprx_tanh)
                experts(l)

        @block.gpsimd
        def _(pool):
            pool.memset(xn[:, :, N:NPAD], 0.0).then_inc(sem("xn_pad"), 1)
            pool.memset(probs_t[:, :], 1.0).then_inc(sem("probs_t_pad"), 1)
            pool.memset(att_out[:, :], 0.0).then_inc(sem("att_out_pad"), 1)
            pool.wait_ge(sem("h_embed"), 1)
            pool.memset(arena[:, 0:H * T * 16], 0.0).then_inc(sem("rel_cleared"), 1)
            for l in range(4):
                if last_stage < 2 * l + 1:
                    break
                a = ATT[l] if l < 3 else None
                if a:
                    if l:
                        pool.wait_ge(sem(f"h_moe{l - 1}"), 4)
                    pool.memset(v_stack[:, :, :], 0.0).then_inc(sem("att_zeroed"), 1)
                    pool.memset(probs[:, :, :], 0.0).then_inc(sem("att_zeroed"), 1)
                for s in range(len(a.steps) if a else 0):
                    S = a.keys
                    pool.wait_ge(sem("maxed"), a.at + s + 1)
                    sc = scores[:, s % 2, 0:H * S].rearrange("p (h s) -> p h s", h=H)
                    pool.tensor_tensor(sc, sc, spread(row_max[:, s % 2, :], 2, S), ALU.subtract).then_inc(sem("shifted"), 1)

        @block.vector
        def _(dve):
            chain = [0]

            def link(ins_):
                chain[0] += 1
                ins_.then_inc(sem("vector_chain"), 1)
                dve.wait_ge(sem("vector_chain"), chain[0])

            def norm(s, done):
                dve.wait_ge(sem(s.after[0]), s.after[1])
                for t in range(2):
                    cols = slice(t * s.hc, (t + 1) * s.hc)
                    dve.wait_ge(sem("mean"), s.at + t + 1)
                    dve.tensor_tensor(s.cen[:, :, cols], s.src[:, :, cols], spread(ps[:, 4 + t, 0:s.hc], 1, s.kc),
                                      ALU.subtract).then_inc(sem("centred"), 1)
                rows = s.tiles[-1][1]
                dve.wait_ge(sem("std"), s.index + 1)
                dve.reciprocal(rstd[:, 0:TT - 1], std[:, 0:TT - 1])
                dve.reciprocal(rstd[0:rows, TT - 1:TT], std[0:rows, TT - 1:TT]).then_inc(sem("rstd_ready"), 1)
                dve.wait_ge(sem("centred"), s.at + 2)
                for t, at, width, bank, col in s.pieces:
                    cols = slice(at, at + width)
                    dve.wait_ge(sem("rstd_spread"), s.at + t + 1)
                    ins_ = dve.tensor_tensor(s.out[:, :, cols], s.cen[:, :, cols],
                                             spread(ps[:, bank, col:col + width], 1, s.kc), ALU.mult)
                    if s.w:
                        link(ins_)
                        for k in range(s.kc):
                            ins_ = dve.tensor_scalar(s.out[:, k, cols], s.out[:, k, cols], vec(s.w, k), vec(s.b, k),
                                                     ALU.mult, ALU.add)
                    if at != s.hc:
                        ins_.then_inc(sem(done), 1)

            def attention(l):
                a = ATT[l]
                S = a.keys
                dve.wait_ge(sem(f"normed_att{l}"), 2)
                dve.memset(q_all[:, 0:a.subs * a.chunks, N:NPAD], 0.0).then_inc(sem("q_pad"), 1)
                dve.wait_ge(sem("att_zeroed"), 2 * l + 2)
                ones = v_stack[:, :, 0:H * (a.dv + 1)].rearrange("p i (h d) -> p i h d", h=H)[:, :, :, a.dv]
                dve.tensor_copy(ones, spread(stack_mask(a), 1, 4)).then_inc(sem("stack_ones"), 1)
                if l == 2:
                    for slot in range(2):
                        link(dve.memset(k_ring[:, slot, :], 0.0))
                    for m in range(a.chunks):
                        link(dve.tensor_copy(v_view(a)[:, m, :, T:S], spread(vec("null_v", m), 1, B)))
                    link(dve.tensor_scalar(small[:, 24:32], small[:, 32:40], 0.125, None, ALU.mult))
                    dve.tensor_copy(small[:, 92:93], small[:, 24:25]).then_inc(sem("logit_scale_ready"), 1)
                for j in range(1, 6 * a.chunks, 2):
                    kind, m = divmod(j // 2, a.chunks)
                    dve.wait_ge(sem(f"proj{l}"), j + 1)
                    src = ps[:, j % 8, 0:HN]
                    imgs = src.rearrange("p (b s) -> p b s", b=B // 2)
                    done = sem(f"proj_out{l}_1")
                    if kind == 0 and l == 0:
                        dve.tensor_scalar(q_all[:, m, HN:N], src, vec("q_b", m), 0.25, ALU.add, ALU.mult).then_inc(done, 1)
                    elif kind == 0 and l == 1:
                        for i in range(2):
                            ins_ = dve.tensor_scalar(q_all[:, 2 * i + m, HN:N], src, small[:, 8 + i:9 + i], None, ALU.mult)
                        ins_.then_inc(done, 1)
                    elif kind == 0:
                        dve.tensor_scalar(q_all[:, m, HN:N], src, small[:, 24 + m:25 + m], None, ALU.mult).then_inc(done, 1)
                    elif kind == 1:
                        if m >= 2:
                            dve.wait_ge(sem(f"kblk_chunk_v{l}"), m - 1)
                            dve.wait_ge(sem(f"kblk_chunk_s{l}"), m - 1)
                        dst = k_view(a, m % 2)[:, B // 2:B, 0:T]
                        if l == 0:
                            dve.tensor_scalar(dst, imgs, vec("k_b", m), None, ALU.add).then_inc(done, 1)
                        else:
                            dve.tensor_copy(dst, imgs).then_inc(done, 1)
                        if l == 2:
                            link(dve.tensor_copy(k_view(a, m % 2)[:, :, T:S], spread(vec("null_k", m), 1, B)))
                        dve.wait_ge(sem(f"proj_out{l}_1"), a.chunks + m + 1)
                        dve.wait_ge(sem(f"proj_out{l}_0"), a.chunks + m + 1)
                        hm = const("head16" if a.dv == 16 else "head64")
                        first = True
                        for jh in range(a.hpc):
                            if jh % 3 != 1:
                                ins_ = dve.tensor_scalar(kblk_view(a)[:, m, jh], k_view(a, m % 2), hm[:, jh:jh + 1], None, ALU.mult)
                                if first:
                                    ins_.then_inc(sem(f"k_chunk{l}"), 1)
                                    first = False
                                    last_ins = None
                                else:
                                    last_ins = ins_
                        if last_ins is not None:
                            last_ins.then_inc(sem(f"kblk_chunk_v{l}"), 1)
                        else:
                            dve.wait_ge(sem(f"k_chunk{l}"), m + 1)
                            dve.tensor_copy(small[:, 94:95], vec("beta")).then_inc(sem(f"kblk_chunk_v{l}"), 1)
                    else:
                        dst = v_view(a)[:, m, B // 2:B, 0:T]
                        if l == 0:
                            dve.tensor_scalar(dst, imgs, vec("v_b", m), None, ALU.add).then_inc(done, 1)
                        else:
                            dve.tensor_copy(dst, imgs).then_inc(done, 1)


                def scored(s):
                    dve.wait_ge(sem("score"), a.at + s + 1)
                    if s >= 2:
                        dve.wait_ge(sem("exped"), a.at + s - 1)
                    src = ps[:, 0:2, 0:8 * S].rearrange("p b (h s) -> p b h s", h=8)
                    dst = scores[:, s % 2, 0:H * S].rearrange("p (b h s) -> p b h s", b=2, h=8)
                    if l == 0:
                        bias = bias0[:, :, :].rearrange("p (b h) s -> p b h s", b=2)
                    else:
                        bias = spread(spread(const("causal37" if S == T else "causal38"), 1, 8), 1, 2)
                    dve.tensor_tensor(dst, src, bias, ALU.add).then_inc(sem("scored"), 1)
                    dve.wait_ge(sem("scored"), a.at + s + 1)
                    dve.tensor_reduce(row_max[:, s % 2, :], scores[:, s % 2, 0:H * S].rearrange("p (h s) -> p h s", h=H),
                                      AX.X, ALU.max).then_inc(sem("maxed"), 1)

                def stack_odd(p):
                    for r in range(a.rounds):
                        dve.wait_ge(sem(f"stacked_even{l}"), p * a.rounds + r + 1)
                        if p >= 2:
                            dve.wait_ge(sem("valued"), a.at + (p - 1) * a.subs)
                        src, dst = stack_parts(a, p, r, 1)
                        dve.tensor_copy(dst, src).then_inc(sem(f"stacked_odd{l}"), 1)

                def summed(s):
                    p, i = a.steps[s]
                    d1 = a.dv + 1
                    dve.wait_ge(sem("valued"), a.at + s + 1)
                    if l != 1 and s >= 1:
                        dve.wait_ge(sem("turned"), a.groups_at + s)
                    if l == 2:
                        parts = [(ps[:, 5 + b, 0:n * d1].rearrange("p (h d) -> p h d", h=n), 6 * b, n)
                                 for b, n in enumerate((6, 6, 4))]
                    else:
                        parts = [(ps[:, value_banks(l, s), 0:H * d1].rearrange("p (h d) -> p h d", h=H), 0, H)]
                    for src, h0, n in parts:
                        ins_ = dve.reciprocal(sums_r[:, i, h0:h0 + n], src[:, :, a.dv])
                    link(ins_)
                    if i == 1:
                        link(dve.tensor_scalar(sums_r[:, 1, :], sums_r[:, 1, :], small[:, 11:12], None, ALU.mult))
                    out_p = out_view(l, p)
                    dst = (att_tmp[:, :] if i == 1 else out_p).rearrange("p (h d) -> p h d", h=H)
                    for n_, (src, h0, n) in enumerate(parts):
                        ins_ = dve.tensor_tensor(dst[:, h0:h0 + n, :], src[:, :, 0:a.dv],
                                                 spread(sums_r[:, i, h0:h0 + n], 2, a.dv), ALU.mult)
                    ins_.then_inc(sem("summed"), 1)
                    if i == 1:
                        dve.wait_ge(sem("summed"), a.at + s + 1)
                        link(dve.tensor_tensor(out_p, out_p, att_tmp[:, :], ALU.subtract))

                def group_view(g):
                    return g_ring[:, :, :].rearrange("p r n -> p (r n)")[:, g * a.group * D:(g + 1) * a.group * D]

                def mean_square(g):
                    o = group_view(g)
                    sq = v_raw_free[:, 0:a.group * D]
                    link(dve.tensor_tensor(sq, o, o, ALU.mult))
                    link(dve.tensor_reduce(rms[:, :], sq.rearrange("p (h d) -> p h d", d=a.dv), AX.X, ALU.add))
                    dve.tensor_scalar(rms[:, :], rms[:, :], 1.0 / a.dv, EPS, ALU.mult, ALU.add).then_inc(sem("mean_square"), 1)

                def rms_norm(g):
                    o = group_view(g).rearrange("p (h d) -> p h d", d=a.dv)
                    dve.wait_ge(sem("rms_ready"), g + 1)
                    link(dve.reciprocal(rms[:, :], rms[:, :]))
                    dve.tensor_tensor(o, o, spread(rms[:, :], 2, a.dv), ALU.mult).then_inc(sem("rms_normed"), 1)

                scored(0)
                stack_odd(0)
                scored(1)
                for s, (p, i) in enumerate(a.steps):
                    if s + 2 < len(a.steps):
                        scored(s + 2)
                    if s + 1 < len(a.steps) and a.steps[s + 1][1] == 0:
                        stack_odd(p + 1)
                    if l == 1 and s - 2 in a.turn_at:
                        rms_norm(a.turn_at.index(s - 2))
                    summed(s)
                    if l == 1 and s in a.turn_at:
                        mean_square(a.turn_at.index(s))
                if l == 1:
                    mean_square(a.groups - 1)
                    rms_norm(a.groups - 1)

            def residual(l, bias):
                for m in range(KD):
                    for t in range(2):
                        cols = slice(t * HN, (t + 1) * HN)
                        dve.wait_ge(sem("out_proj"), 4 * l + 2 * m + t + 1)
                        src = ps[:, 4 + 2 * m + t, 0:HN]
                        if bias:
                            ins_ = dve.scalar_tensor_tensor(h[:, m, cols], src, vec(bias, m), h[:, m, cols], ALU.add, ALU.add)
                        else:
                            ins_ = dve.tensor_tensor(h[:, m, cols], src, h[:, m, cols], ALU.add)
                        ins_.then_inc(sem(f"h_att{l}"), 1)

            def ema():
                for j in range(1, 8, 2):
                    kind, m = divmod(j // 2, KD)
                    dve.wait_ge(sem("proj3"), j + 1)
                    dve.tensor_copy((q_all, v_flat)[kind][:, m, HN:N], ps[:, j % 8, 0:HN]).then_inc(sem("proj_out3_1"), 1)
                dve.wait_ge(sem("decay_ready"), 1)
                for m in range(KD):
                    link(dve.memset(decay[:, m, :], 1.0))
                    link(dve.tensor_scalar(decay[:, m, :], decay[:, m, :], small[:, 40 + m:41 + m], None, ALU.mult))
                    link(dve.memset(decay[:, m, :].rearrange("p (b t) -> p b t", b=B)[:, :, 0:1], 0.0))
                dve.wait_ge(sem("proj_out3_0"), 4)
                dve.wait_ge(sem("proj_out3_1"), 4)
                for m in range(KD):
                    link(dve.tensor_tensor_scan(state[:, m, :], decay[:, m, :], v_flat[:, m, :], 0.0, ALU.mult, ALU.add))
                dve.tensor_tensor(mixed, q_all[:, 0:KD, 0:N], state, ALU.mult).then_inc(sem("mixed"), 1)
                norm(norm_of["ema"], "normed_ema")
                dve.wait_ge(sem("normed_ema"), 2)
                dve.wait_ge(sem("proj_out3_0"), 6)
                dve.wait_ge(sem("gate_out3"), 2)
                dve.tensor_tensor(mixed, normed3, gate3, ALU.mult).then_inc(sem("ema_gated"), 1)

            def route(l):
                m = MOE[l]
                E, K = m.e, m.k
                raw, logit, hit, gate = (router[n] for n in ("raw", "logit", "hit", "gate"))
                src = ps[:, 0, 0:TT * E].rearrange("p (t e) -> p t e", t=TT)
                bias = spread(vec("router_b", m.col, E), 1, TT)
                dve.wait_ge(sem("logits"), l + 1)
                link(dve.memset(logit[:, :, E:E + 8], SENTINEL))
                if l == 2:
                    dve.wait_ge(sem("sigmoid2"), 1)
                    link(dve.tensor_tensor(logit[:, :, 0:E], raw[:, :, 0:E], bias, ALU.add))
                elif l == 1:
                    link(dve.tensor_copy(raw[:, :, 0:E], src))
                    link(dve.tensor_tensor(logit[:, :, 0:E], raw[:, :, 0:E], bias, ALU.add))
                elif l == 0:
                    link(dve.tensor_tensor(logit[:, :, 0:E], src, bias, ALU.add))
                    link(dve.tensor_copy(raw[:, :, 0:E], logit[:, :, 0:E]))
                else:
                    link(dve.tensor_tensor(raw[:, :, 0:E], src, bias, ALU.add))
                    link(dve.tensor_reduce(r_small[:, 0, :], raw[:, :, 0:E], AX.X, ALU.max))
                    dve.tensor_tensor(gate[:, :, 0:E], raw[:, :, 0:E], spread(r_small[:, 0, :], 2, E),
                                      ALU.subtract).then_inc(sem("raw_shifted3"), 1)
                    dve.wait_ge(sem("raw_exp3"), 1)
                    link(dve.tensor_reduce(r_small[:, 1, :], gate[:, :, 0:E], AX.X, ALU.add))
                    link(dve.reciprocal(r_small[:, 2, :], r_small[:, 1, :]))
                    link(dve.tensor_tensor(raw[:, :, 0:E], gate[:, :, 0:E], spread(r_small[:, 2, :], 2, E), ALU.mult))
                    link(dve.tensor_copy(logit[:, :, 0:E], raw[:, :, 0:E]))
                for t in range(TT):
                    ins_ = dve.max(top8[:, t, :], logit[:, t, 0:E])
                link(ins_)
                link(dve.memset(top8[:, :, K:8], SENTINEL))
                for t in range(TT):
                    ins_ = dve.match_replace(hit[:, t, 0:E + 8], top8[:, t, :], logit[:, t, 0:E + 8], TAKEN)
                link(ins_)
                link(dve.tensor_scalar(hit[:, :, 0:E], hit[:, :, 0:E], TAKEN, None, ALU.is_equal))
                hits = hit[:, :, 0:E]
                if l in (0, 1):
                    link(dve.tensor_scalar(gate[:, :, 0:E], hits, -MASKED, MASKED, ALU.mult, ALU.add))
                    link(dve.tensor_tensor(gate[:, :, 0:E], gate[:, :, 0:E], raw[:, :, 0:E], ALU.add))
                    link(dve.tensor_reduce(r_small[:, 0, :], gate[:, :, 0:E], AX.X, ALU.max))
                    dve.tensor_tensor(gate[:, :, 0:E], gate[:, :, 0:E], spread(r_small[:, 0, :], 2, E),
                                      ALU.subtract).then_inc(sem(f"raw_shifted{l}"), 1)
                    dve.wait_ge(sem(f"raw_exp{l}"), 1)
                elif l == 2:
                    link(dve.tensor_tensor(gate[:, :, 0:E], raw[:, :, 0:E], hits, ALU.mult))
                else:
                    dve.tensor_tensor(gate[:, :, 0:E], raw[:, :, 0:E], hits, ALU.mult).then_inc(sem("gated"), 1)
                if l != 3:
                    link(dve.tensor_reduce(r_small[:, 1, :], gate[:, :, 0:E], AX.X, ALU.add))
                    if l == 2:
                        link(dve.tensor_scalar(r_small[:, 1, :], r_small[:, 1, :], 1e-20, None, ALU.add))
                    link(dve.reciprocal(r_small[:, 2, :], r_small[:, 1, :]))
                    dve.tensor_tensor(gate[:, :, 0:E], gate[:, :, 0:E], spread(r_small[:, 2, :], 2, E),
                                      ALU.mult).then_inc(sem("gated"), 1)
                dve.wait_ge(sem("gates_turned"), l + 1)
                link(dve.tensor_copy(gates_t[0:E, 0:NPAD], ps[0:E, 0:2, :].rearrange("p b n -> p (b n)")[:, 0:NPAD]))
                if l == 2:
                    link(dve.tensor_copy(chosen_t[0:E, 0:NPAD], ps[0:E, 2:4, :].rearrange("p b n -> p (b n)")[:, 0:NPAD]))
                    link(dve.memset(g_tail[0:E, 0:N], 0.0))
                    link(dve.tensor_tensor_scan(g_tail[0:E, 0:N], chosen_t[0:E, 0:N], g_tail[0:E, 0:N], 0.0, ALU.add, ALU.add))
                    link(dve.tensor_scalar(chosen_t[0:E, 0:N], g_tail[0:E, 0:N], float(CAPACITY), None, ALU.is_le))
                    link(dve.tensor_tensor(gates_t[0:E, 0:N], gates_t[0:E, 0:N], chosen_t[0:E, 0:N], ALU.mult))
                dve.memset(chosen_t[0:1, 0:N], 1.0).then_inc(sem("gates_ready"), 1)

            def experts(l):
                m = MOE[l]

                def split_weights(place, i):
                    slot = place % RING
                    dve.wait_ge(sem("w_hi_done"), m.chunks_at + i * RING + place + 1)
                    dve.tensor_tensor(w_lo[:, slot, 0:m.split_cols], w_ring[:, slot, 0:m.split_cols],
                                      w_hi[:, slot, 0:m.split_cols].bitcast(F32), ALU.subtract).then_inc(sem("w_lo_done"), 1)

                def low_part(i, u):
                    dve.wait_ge(sem("hid_hi_done"), m.at + i * (2 * RING) + u + 1)
                    dve.tensor_tensor(hid_lo[:, u % 2, :], hidden[:, u % 2, :], hid_hi[:, u % 2, :].bitcast(F32),
                                      ALU.subtract).then_inc(sem("hid_lo_done"), 1)

                def body(c, place, i):
                    slot = place % RING
                    whole = place < m.whole
                    gates = g_ring[:, slot, :] if whole else g_tail[:, :]
                    for t in range(2):
                        u = 2 * place + t
                        unit = m.at + i * (2 * RING) + u
                        cols = slice(t * HN, (t + 1) * HN)
                        if whole and t == 0:
                            dve.wait_ge(sem(f"gate_in{slot}"), i * 16 + 16 * (place // RING + 1 + m.gates_at[slot]))
                        elif place == m.whole and t == 0:
                            dve.wait_ge(sem(f"tail_in{l}"), 16 * m.e)
                        dve.wait_ge(sem("up_done"), unit + 1)
                        if m.glu:
                            if m.bias:
                                ins_ = dve.scalar_tensor_tensor(gated_u[:, t, :], ps[:, 5 + 2 * t, 0:HN],
                                                                w_ring[:, slot, 6 * P + 1:6 * P + 2], gates[:, cols],
                                                                ALU.add, ALU.mult)
                            else:
                                ins_ = dve.tensor_tensor(gated_u[:, t, :], ps[:, 5 + 2 * t, 0:HN], gates[:, cols], ALU.mult)
                            ins_.then_inc(sem("gated_u"), 1)
                            dve.wait_ge(sem("gated_u"), m.at_glu + i * (2 * RING) + u + 1)
                            other = gated_u[:, t, :]
                        else:
                            other = gates[:, cols]
                        dve.wait_ge(sem("act_done"), unit + 1)
                        if u >= 2:
                            dve.wait_ge(sem("hid_lo_done"), unit - 1)
                        dve.tensor_tensor(hidden[:, t, :], act_g[:, t, :], other, ALU.mult).then_inc(sem("hidden_done"), 1)
                        if u >= 1:
                            low_part(i, u - 1)
                        if t == 0 and place < m.chunks - 1:
                            split_weights(place + 1, i)

                split_weights(0, 0)
                chunk_walk(dve, m, body)
                low_part(0, 2 * m.chunks - 1)
                dve.wait_ge(sem("down_done"), m.at + 2 * m.chunks)
                if m.bias:
                    dve.wait_ge(sem(f"biased{l}"), 1)
                for d in range(KD):
                    for t in range(2):
                        cols = slice(t * HN, (t + 1) * HN)
                        src = ps[:, 2 * d + t, 0:HN]
                        if m.bias:
                            ins_ = dve.scalar_tensor_tensor(h[:, d, cols], src, vec("sb2", d), h[:, d, cols], ALU.add, ALU.add)
                        else:
                            ins_ = dve.tensor_tensor(h[:, d, cols], src, h[:, d, cols], ALU.add)
                        ins_.then_inc(sem(f"h_moe{l}"), 1)

            dve.wait_ge(sem("vecs_in"), 16)
            dve.wait_ge(sem("consts_in"), 16)
            link(dve.memset(small[:, :], 0.0))
            lam = vec("lambdas", 0, 32).rearrange("p (a b d) -> p a b d", a=2, b=2)
            link(dve.tensor_tensor(small[:, 16:32].rearrange("p (a d) -> p a d", a=2), lam[:, :, 0, :], lam[:, :, 1, :], ALU.mult))
            dve.tensor_reduce(small[:, 14:16], small[:, 16:32].rearrange("p (a d) -> p a d", a=2), AX.X,
                              ALU.add).then_inc(sem("lambda_sums"), 1)
            dve.tensor_scalar(small[:, 0:2], vec("q_b", 0, 2), 0.25, None, ALU.mult).then_inc(sem("q_bias_scaled"), 1)
            dve.tensor_scalar(small[:, 10:11], vec("rms_w"), 1.0 - LAMBDA_INIT, None, ALU.mult)
            dve.tensor_scalar(small[:, 8:10], const("sub"), float(8) ** -0.5, None, ALU.mult).then_inc(sem("sub_scaled"), 1)
            dve.wait_ge(sem("sub_scaled"), 1)

            norm(norm_of["patch"], "patches_normed")
            for m in range(KD):
                for t in range(2):
                    dve.wait_ge(sem("embedded"), 2 * m + t + 1)
                    dve.tensor_scalar(embed[:, m, t * HP:(t + 1) * HP], ps[:, 2 * m + t, 0:HP], vec("lin_b", m), None,
                                      ALU.add).then_inc(sem("embed_done"), 1)
            norm(norm_of["embed"], "embed_normed")
            dve.wait_ge(sem("embed_normed"), 2)
            pos = vec("pos", 0, 2 * T).rearrange("p (k t) -> p k t", k=KD)
            for m in range(KD):
                hm = h[:, m, :].rearrange("p (b t) -> p b t", b=B)
                dve.tensor_tensor(hm[:, :, 1:T], embed[:, m, :].rearrange("p (b t) -> p b t", b=B),
                                  spread(pos[:, m, 1:T], 1, B), ALU.add)
                link(dve.tensor_tensor(small[:, 4 + m:5 + m], vec("cls", m), pos[:, m, 0:1], ALU.add))
                link(dve.tensor_copy(hm[:, :, 0:1], spread(small[:, 4 + m:5 + m], 1, B)))
            dve.tensor_copy(small[:, 87:88], vec("beta")).then_inc(sem("h_embed"), 1)
            dve.wait_ge(sem("lambda_exp"), 1)
            link(dve.tensor_tensor(small[:, 11:12], small[:, 12:13], small[:, 13:14], ALU.subtract))
            link(dve.tensor_scalar(small[:, 11:12], small[:, 11:12], LAMBDA_INIT, None, ALU.add))
            dve.wait_ge(sem("logit_exp"), 1)
            for n in ("xn_pad", "probs_t_pad", "att_out_pad"):
                dve.wait_ge(sem(n), 1)
            for l in range(4):
                if last_stage < 2 * l + 1:
                    break
                norm(norm_of[f"att{l}"], f"normed_att{l}")
                if l == 0:
                    dve.wait_ge(sem("rel_in"), 32)
                    link(dve.tensor_reduce(bias0[:, :, :].rearrange("p h t -> p (h t)"), rel, AX.X, ALU.add))
                    link(dve.tensor_tensor(bias0[:, :, :], bias0[:, :, :], spread(const("causal37"), 1, H), ALU.add))
                if l < 3:
                    attention(l)
                else:
                    ema()
                residual(l, "proj_b" if l == 0 else None)
                if last_stage < 2 * l + 2:
                    break
                norm(norm_of[f"moe{l}"], f"normed_moe{l}")
                for t in range(2):
                    cols = slice(t * HN, (t + 1) * HN)
                    dve.wait_ge(sem("x_hi_done"), 2 * l + t + 1)
                    dve.tensor_tensor(x_lo[:, :, cols], xn[:, :, cols], x_hi[:, :, cols].bitcast(F32),
                                      ALU.subtract).then_inc(sem("x_split"), 1)
                route(l)
                experts(l)


def lay_out(x):
    f = {k: np.asarray(v) for k, v in x.items()}

    def cols(v):
        return v.reshape(-1, P).T

    def rows(w):
        return w.reshape(-1, P, w.shape[1]).transpose(1, 0, 2).reshape(P, -1)

    out = {}
    img = f["x"].reshape(B, 3, 6, 16, 6, 16).transpose(3, 5, 1, 0, 2, 4).reshape(PD, PB)
    out["patches"] = img.reshape(PK, P, PB).transpose(1, 0, 2)

    p = np.arange(P)
    c = np.zeros((P, CONSTS_W), np.float32)

    def put(arr, fields, name, val):
        at, w = fields[name]
        arr[:, at:at + w] = np.asarray(val).reshape(-1, w)

    tok = p % 64
    put(c, CONSTS, "ident", np.eye(P))
    put(c, CONSTS, "mean_d", np.full((P, P), 1.0 / D))
    put(c, CONSTS, "mean_pd", np.full((P, P), 1.0 / PD))
    put(c, CONSTS, "eps", np.full((P, 8), EPS))
    put(c, CONSTS, "head16", p[:, None] // 16 == np.arange(8))
    put(c, CONSTS, "head64", p[:, None] // 64 == np.arange(2))
    put(c, CONSTS, "sub", p[:, None] // 8 % 2 == np.arange(2))
    for s in (T, T + 1):
        put(c, CONSTS, f"stack{s}", (p[:, None] // 64 == np.arange(H) % 2) & (tok[:, None] < s))
        keys = np.arange(s)
        hidden = (keys > tok[:, None]) & (tok[:, None] < T) & (keys < T)
        put(c, CONSTS, f"causal{s}", np.where(hidden, MASKED, 0.0))
    out["consts"] = c

    v = np.zeros((P, VECS_W), np.float32)
    for name, src in (("ln1_w", "L0_tok_ln1_w"), ("ln1_b", "L0_tok_ln1_b"), ("lin_b", "L0_tok_lin_b"),
                      ("ln2_w", "L0_tok_ln2_w"), ("ln2_b", "L0_tok_ln2_b"), ("proj_b", "L0_attn_proj_b"),
                      ("gamma", "L3_attn_ln_gamma"), ("ln_beta", "L3_attn_ln_beta"), ("sb2", "L3_ffn_sb2")):
        put(v, VECS, name, cols(f[src]))
    put(v, VECS, "cls", cols(f["L0_tok_cls_token"].reshape(-1)))
    put(v, VECS, "pos", f["L0_tok_pos_embedding"][0, :T].T.reshape(KD, P, T).transpose(1, 0, 2).reshape(P, -1))
    for i, n in enumerate(("q_b", "k_b", "v_b")):
        put(v, VECS, n, cols(f["L0_attn_qkv_b"][i * D:(i + 1) * D]))
    lam = np.concatenate([f[f"L1_attn_{n}"] for n in ("lq1", "lk1", "lq2", "lk2")])
    put(v, VECS, "lambdas", np.tile(lam, (P, 1)))
    put(v, VECS, "rms_w", np.tile(f["L1_attn_rms_w"], 8)[:, None])
    put(v, VECS, "null_k", cols(f["L2_attn_null_k"].reshape(-1)))
    put(v, VECS, "null_v", cols(f["L2_attn_null_v"].reshape(-1)))
    put(v, VECS, "logit_scale", cols(np.repeat(f["L2_attn_logit_scale"], 64)))
    put(v, VECS, "beta", cols(np.repeat(f["L3_attn_beta"], 16)))
    biases = [f["L0_ffn_bs"], f["L1_ffn_expert_bias"], f["L2_ffn_expert_bias"], f["L3_ffn_gate_b"]]
    put(v, VECS, "router_b", np.tile(np.concatenate(biases), (P, 1)))
    out["vecs"] = v

    t = np.arange(T)
    back = (t[:, None] - t[None, :]) + 255
    rel = f["L0_attn_rel_pos_emb"].reshape(511, H, 16)[back]
    out["rel"] = rel.transpose(0, 2, 1, 3).reshape(T, H * T, 16)

    out["weights_lo"] = np.concatenate(
        [rows(f["L0_tok_lin_w"]), rows(f["L0_attn_qkv_w"].T), rows(f["L0_attn_proj_w"].T),
         rows(np.concatenate([f["L1_attn_Wq"], f["L1_attn_Wk"], f["L1_attn_Wv"]], 1)), rows(f["L1_attn_Wo"])], 1)
    out["weights_2"] = np.concatenate(
        [rows(np.concatenate([f["L2_attn_Wq"], f["L2_attn_Wk"], f["L2_attn_Wv"]], 1)), rows(f["L2_attn_Wo"])], 1)
    out["weights_3"] = np.concatenate(
        [rows(np.concatenate([f["L3_attn_Wq"].T, f["L3_attn_Wv"].T, f["L3_attn_Wg"].T], 1)), rows(f["L3_attn_Wo"].T)], 1)
    routers = [f["L0_ffn_Ws"], f["L1_ffn_gate_w"].T, f["L2_ffn_router_weight"].T, f["L3_ffn_gate_w"]]
    out["router_w"] = rows(np.concatenate(routers, 1)).reshape(P, KD, E_ALL)
    out["b2"] = f["L3_ffn_b2"]

    def chunk_rows(m, routed, shared):
        n = routed.shape[2]
        parts = []
        if m.shared:
            s = np.zeros((m.shared_chunks * P, n), np.float32)
            s[:m.shared] = shared
            parts.append(s.reshape(-1, P, n))
        cut = m.per_expert * P
        parts.append(routed[:, :cut].reshape(m.e, m.per_expert, P, n).transpose(1, 0, 2, 3).reshape(-1, P, n))
        if m.tails:
            r = routed[:, cut:].reshape(m.e, m.tails, m.tail_rows, n).transpose(1, 0, 2, 3)
            parts.append(r.reshape(-1, P, n))
        return np.concatenate(parts)

    def pack(l, ups, down, biases=()):
        m = MOE[l]
        cols_ = []
        for routed, shared in ups:
            r = chunk_rows(m, routed, shared)
            cols_.append(r.reshape(-1, P, KD, P).transpose(0, 3, 2, 1).reshape(-1, P, KD * P))
        cols_.append(chunk_rows(m, *down))
        for routed, shared in biases:
            cols_.append(chunk_rows(m, routed[:, :, None], None if shared is None else shared[:, None]))
        return np.concatenate(cols_, 2)

    sw = lambda a: a.transpose(0, 2, 1)
    out["experts0"] = pack(0, [(sw(f["L0_ffn_Wg"]), None), (sw(f["L0_ffn_Wu"]), None)], (f["L0_ffn_Wd"], None))
    out["experts1"] = pack(1, [(f["L1_ffn_w1"], f["L1_ffn_sw1"]), (f["L1_ffn_w3"], f["L1_ffn_sw3"])],
                           (sw(f["L1_ffn_w2"]), f["L1_ffn_sw2"].T))
    out["experts2"] = pack(2, [(sw(f["L2_ffn_w1"]), f["L2_ffn_sw1"])], (f["L2_ffn_w2"], f["L2_ffn_sw2"].T))
    out["experts3"] = pack(3, [(sw(f["L3_ffn_w1"]), f["L3_ffn_sw1"].T), (sw(f["L3_ffn_w3"]), f["L3_ffn_sw3"].T)],
                           (f["L3_ffn_w2"], f["L3_ffn_sw2"]),
                           [(f["L3_ffn_b1"], f["L3_ffn_sb1"]), (f["L3_ffn_b3"], f["L3_ffn_sb3"])])
    return {k: np.ascontiguousarray(a) for k, a in out.items()}


def kernel(**inputs):
    import concourse.bacc as _bacc
    from concourse.bass_utils import run_bass_kernel_spmd as _run

    nc = _bacc.Bacc("TRN2", target_bir_lowering=False, num_devices=1)
    arrays = {f"in_{k}": a for k, a in lay_out(inputs).items()}
    ins = {k[3:]: nc.dram_tensor(k, a.shape, mybir.dt.from_np(a.dtype), kind="ExternalInput").ap()
           for k, a in arrays.items()}
    out = nc.dram_tensor("out_tokens", (P, KD, N), F32, kind="ExternalOutput").ap()
    vit_tower(nc, ins, out)
    r = _run(nc, [arrays], core_ids=[0])
    got = r.results[0]["out_tokens"]
    return np.ascontiguousarray(got.transpose(2, 1, 0).reshape(B, T, D))
```

```python
from contextlib import ExitStack

import numpy as np

import concourse.bass as bass
from concourse import mybir

ALU = mybir.AluOpType
ACT = mybir.ActivationFunctionType
AX = mybir.AxisListType
F32 = mybir.dt.float32
F32R = mybir.dt.float32r


BF16 = mybir.dt.bfloat16

P = 128
B, T, D = 16, 37, 256
N = B * T
HN = N // 2
NPAD = 640
TT = NPAD // P
PB = B * (T - 1)
HP = PB // 2
PD = 768
PK = PD // P
KD = D // P
H = 16
OFFSETS = 2 * T - 1
EPS = 1e-5
BANK = 512
MASKED = -1.0e30
SENTINEL = -3.0e38
TAKEN = -2.0e38
LAMBDA_INIT = 0.8 - 0.6 * float(np.exp(-0.3 * 12))
RING = 4

CAPACITY = 2 * ((512 * 6 + 63) // 64)


class AttentionPlan:

    def __init__(self, dv, keys, subs, before):
        self.dv, self.keys, self.subs = dv, keys, subs
        self.chunks = H * dv // P
        self.hpc = P // dv
        self.order = [(kind, m) for kind in (1, 0, 2) for m in range(self.chunks)]
        self.rounds = 2 * self.chunks // 4
        self.parts = 2 if self.rounds > 1 else 1
        self.steps = [(p, i) for p in range(B // 2) for i in range(subs)]
        self.group = B // 8 if subs == 2 else 1
        self.groups = B // 2 // self.group
        self.turn_at = [(g + 1) * self.group * subs - 1 for g in range(self.groups - 1)]
        self.out_lag = 2 if subs == 2 else 1
        self.at = sum(len(a.steps) for a in before)
        self.groups_at = sum(a.groups for a in before)


ATT = []
for dv_, keys_, subs_ in ((16, T, 1), (16, T, 2), (64, T + 1, 1)):
    ATT.append(AttentionPlan(dv_, keys_, subs_, list(ATT)))


class ExpertPlan:

    def __init__(self, e, k, f, shared, glu, bias, before):
        self.e, self.k, self.f, self.shared, self.glu, self.bias = e, k, f, shared, glu, bias
        self.shared_chunks = -(-shared // P)
        self.per_expert = f // P
        self.tail_rows = P // e if f % P else 0
        self.tails = (f % P) * e // P
        self.whole = self.shared_chunks + self.per_expert * e
        self.chunks = self.whole + self.tails
        self.width = (6 if glu else 4) * P + (2 if bias else 0)
        self.col = sum(m.e for m in before)
        peeled = max(1, -(-self.shared_chunks // RING)) * RING
        self.peeled = peeled
        self.segments = [(0, peeled, False)]
        for start, end, final in ((peeled, self.whole, not self.tails), (self.whole, self.chunks, True)):
            looped = max(0, end - start - (1 if final else 0)) // RING * RING
            if looped:
                self.segments.append((start, looped, True))
            if end - start - looped > 0:
                self.segments.append((start + looped, end - start - looped, False))
        self.ungated = [-(-max(0, self.shared_chunks - s) // RING) for s in range(RING)]
        self.up_cols = (4 if glu else 2) * P
        self.split_cols = self.up_cols + 2 * P
        self.lag = 2 if glu else 3
        self.slots = 2 if glu else 4
        self.at = sum(2 * m.chunks for m in before)
        self.chunks_at = sum(m.chunks for m in before)
        self.at_glu = sum(2 * (m.chunks - m.shared_chunks) for m in before if m.glu)
        self.gates_at = [sum(-(-(m.whole - s) // RING) - m.ungated[s] for m in before) for s in range(RING)]
        self.weights_at = [sum(-(-(m.chunks - s) // RING) for m in before) for s in range(RING)]


MOE = []
for fields_ in ((8, 2, 688, 0, True, False), (16, 4, 256, 256, True, False),
                (64, 6, 128, 512, False, False), (16, 2, 352, 704, True, True)):
    MOE.append(ExpertPlan(*fields_, list(MOE)))
E_ALL = sum(m.e for m in MOE)
W_MAX = max(m.width for m in MOE)


class NormPlan:

    def __init__(self, n, src, out, after, cols=N, kc=KD, ones="mean_d", w=None):
        self.n, self.src, self.out, self.after, self.cols = n, src, out, after, cols
        self.kc, self.ones, self.w = kc, ones, w
        self.hc = cols // 2
        self.kc_sq = 1 if kc > KD else kc
        self.tiles = [(t, min(P, cols - t * P)) for t in range(TT)]
        self.pieces = [(0, 0, self.hc, 7, 0), (1, self.hc, 3 * P - self.hc, 7, self.hc),
                       (1, 3 * P, cols - 3 * P, 6, P)]


def packed(fields):
    at, out = 0, {}
    for name, width in fields:
        out[name] = (at, width)
        at += width
    return out, at


CONSTS, CONSTS_W = packed([
    ("ident", P), ("mean_d", P), ("mean_pd", P), ("eps", 8), ("head16", 8), ("head64", 2), ("sub", 2), ("shift", 104),
    ("stack37", H), ("stack38", H), ("causal37", T), ("causal38", T + 1)])
VECS, VECS_W = packed([
    ("ln1_w", 6), ("ln1_b", 6), ("lin_b", 2), ("ln2_w", 2), ("ln2_b", 2), ("cls", 2), ("pos", 2 * T),
    ("q_b", 2), ("k_b", 2), ("v_b", 2), ("proj_b", 2), ("lambdas", 32), ("rms_w", 1),
    ("null_k", 8), ("null_v", 8), ("logit_scale", 8), ("beta", 2), ("gamma", 2), ("ln_beta", 2),
    ("sb2", 2), ("router_b", E_ALL)])
WEIGHTS_LO, WEIGHTS_LO_W = packed([("lin", PK * D), ("qkv0", KD * 3 * D), ("o0", KD * D),
                                   ("qkv1", KD * 3 * D), ("o1", KD * D)])
WEIGHTS_2, WEIGHTS_2_W = packed([("qkv2", KD * 3 * 1024), ("o2", 8 * D)])
WEIGHTS_3, WEIGHTS_3_W = packed([("qkv3", KD * 3 * D), ("o3", KD * D)])


def vit_tower(nc, ins, out):
    ctx = ExitStack()
    with ctx:
        sems = {}

        def sem(name):
            if name not in sems:
                sems[name] = ctx.enter_context(nc.semaphore(name))
            return sems[name]

        def sb(name, shape):
            return ctx.enter_context(nc.sbuf_tensor(name, shape, F32))

        def over(name, shape, at, base=None):
            return nc.alloc_sbuf_tensor_at(name, shape, F32R, offset=(arena_at if base is None else base) + at)

        def spread(ap, axis, n):
            ap = ap.unsqueeze(axis)
            shape = list(ap.shape)
            shape[axis] = n
            return ap.broadcast_to(shape)

        ps = ctx.enter_context(nc.psum_tensor("ps", [P, 8, BANK], F32))

        consts = sb("consts", [P, CONSTS_W])
        vecs = sb("vecs", [P, VECS_W])
        weights = sb("weights", [P, max(WEIGHTS_LO_W, WEIGHTS_2_W, WEIGHTS_3_W)])
        router_w = sb("router_w", [P, KD, E_ALL])
        b2 = sb("b2", [H, D])
        h = sb("h", [P, KD, N])
        xn = sb("xn", [P, KD, NPAD])
        arena_at = nc.sbuf_base
        arena = sb("arena", [P, 8 * 2 * B * (T + 1)])
        x_hi, x_lo = (over(n, [P, KD, N], 4 * KD * N * i) for i, n in enumerate(("x_hi", "x_lo")))
        split = {}
        for glu, slots, cols in ((True, 2, 6 * P), (False, 4, 4 * P)):
            split[glu] = [over(f"{n}{slots}", [P, slots, HN], 4 * (2 * KD * N + slots * HN * i))
                          for i, n in enumerate(("hid_hi", "hid_lo"))]
            split[glu] += [over(f"{n}{slots}", [P, RING, cols], 4 * (2 * KD * N + 2 * slots * HN + RING * cols * i))
                           for i, n in enumerate(("w_hi", "w_lo"))]
        q_raw = sb("q_raw", [P, 8 * NPAD])
        v_raw = sb("v_raw", [P, 8 * B * (T + 1)])
        v_stack = sb("v_stack", [P, 4, H * 65])
        scores_at = nc.sbuf_base
        scores = sb("scores", [P, 2, H * (T + 1)])
        probs = sb("probs", [P, 2, H * 64])
        row_max = sb("row_max", [P, 2, H])
        probs_t = sb("probs_t", [P, 8 * 2 * T + 27])
        sums_r = sb("sums_r", [P, 2, H])
        att_out_at = nc.sbuf_base
        att_out = sb("att_out", [P, H * 64])
        att_tmp = sb("att_tmp", [P, H * 16])
        bias0 = sb("bias0", [P, H, T])
        small = sb("small", [P, 96])
        std = sb("std", [P, TT])
        rstd = sb("rstd", [P, TT])
        rms = sb("rms", [P, B // 8 * H])
        act_scratch = sb("act_scratch", [P, 1])
        w_ring = sb("w_ring", [P, RING, W_MAX])
        g_ring_at = nc.sbuf_base
        g_ring = sb("g_ring", [P, RING, N])
        x2_hi, x2_lo = (over(n, [P, KD, N], 4 * KD * N * i, g_ring_at) for i, n in enumerate(("x2_hi", "x2_lo")))
        w2_hi = over("w2_hi", [P, RING, KD * P], 0, scores_at)
        w2_lo = over("w2_lo", [P, RING, KD * P], 0, att_out_at)
        g_tail = sb("g_tail", [P, N])
        router = {n: sb(f"r_{n}", [P, TT, 72]) for n in ("raw", "logit", "hit", "gate")}
        top8 = sb("top8", [P, TT, 8])
        r_small = sb("r_small", [P, 3, TT])
        gates_t = sb("gates_t", [P, NPAD])
        chosen_t = sb("chosen_t", [P, NPAD])

        def const(name):
            at, w = CONSTS[name]
            return consts[:, at:at + w]

        def vec(name, i=0, n=1):
            at = VECS[name][0] + i
            return vecs[:, at:at + n]

        def region(fields, name, k):
            at, w = fields[name]
            return weights[:, at:at + w].rearrange("p (k n) -> p k n", k=k)

        att_w = {0: (region(WEIGHTS_LO, "qkv0", KD), region(WEIGHTS_LO, "o0", KD)),
                 1: (region(WEIGHTS_LO, "qkv1", KD), region(WEIGHTS_LO, "o1", KD)),
                 2: (region(WEIGHTS_2, "qkv2", KD), region(WEIGHTS_2, "o2", 8)),
                 3: (region(WEIGHTS_3, "qkv3", KD), region(WEIGHTS_3, "o3", KD))}
        lin_w = region(WEIGHTS_LO, "lin", PK)
        lin_scaled = v_stack[:, :, :].rearrange("p i n -> p (i n)")[:, 0:PK * D].rearrange("p (k n) -> p k n", k=PK)
        ident = const("ident")
        eps_col = const("eps")[:, 0:1]

        patches = arena[:, 0:PK * PB].rearrange("p (k n) -> p k n", k=PK)
        embed = arena[:, PK * PB:PK * PB + KD * PB].rearrange("p (k n) -> p k n", k=KD)
        rel_at = PK * PB + KD * PB
        rel = arena[0:OFFSETS, rel_at:rel_at + D]
        rel_sums = arena[0:OFFSETS, rel_at + D:rel_at + D + H]
        rstd_rows = scores[:, :, :].rearrange("p i n -> p (i n)")[:, 0:PB]
        mixed = arena[:, 0:KD * N].rearrange("p (k n) -> p k n", k=KD)
        v_flat = arena[:, KD * N:2 * KD * N].rearrange("p (k n) -> p k n", k=KD)
        decay = arena[:, 2 * KD * N:3 * KD * N].rearrange("p (k n) -> p k n", k=KD)
        state = arena[:, 3 * KD * N:4 * KD * N].rearrange("p (k n) -> p k n", k=KD)
        gate3 = arena[:, 4 * KD * N:5 * KD * N].rearrange("p (k n) -> p k n", k=KD)
        normed3 = arena[:, 5 * KD * N:6 * KD * N].rearrange("p (k n) -> p k n", k=KD)
        q_all = q_raw[:, :].rearrange("p (m n) -> p m n", m=8)
        act_g = scores[:, 0:2, 0:HN]
        gated_u = scores[:, 0:2, HN:2 * HN]
        hidden = probs[:, 0:2, 0:HN]

        def v_view(a):
            return v_raw[:, 0:a.chunks * B * a.keys].rearrange("p (m b s) -> p m b s", m=a.chunks, b=B)

        def kblk_view(a):
            return arena[:, 0:H * B * a.keys].rearrange("p (m j b s) -> p m j b s", m=a.chunks, j=a.hpc, b=B)

        v_raw_free = v_raw[:, 2 * B * (T + 1):]

        def stack_view(a, slot):
            return v_stack[:, slot, 0:H * (a.dv + 1)].rearrange("p (h d) -> p h d", h=H)

        def stack_parts(a, p, r, odd):
            S, slot = a.keys, 2 * (p % 2)
            rows = slice(64 * odd, 64 * odd + S)
            if a.chunks == 2:
                src = ps[0:S, 4, :].rearrange("p (i h e d) -> p i h e d", i=2, e=2, d=a.dv)[:, :, :, odd, :]
                dst = v_stack[:, slot:slot + 2, 0:H * (a.dv + 1)].rearrange("p i (h e d) -> p i h e d", e=2, d=a.dv + 1)
                return src, dst[rows, :, :, odd, 0:a.dv]
            img, half = divmod(r, 2)
            src = ps[0:S, 4, :].rearrange("p (h e d) -> p h e d", e=2, d=a.dv)[:, :, odd, :]
            dst = stack_view(a, slot + img).rearrange("p (h e) d -> p h e d", e=2)
            return src, dst[rows, 4 * half:4 * half + 4, odd, 0:a.dv]

        def out_view(l, p):
            if l == 1:
                return g_ring[:, :, :].rearrange("p r n -> p (r n)")[:, p * D:(p + 1) * D]
            return att_out[:, 0:ATT[l].chunks * P]

        out_bank = {0: 7, 1: 6, 2: 2}

        def value_banks(l, s):
            return 5 + s % 2 if l == 0 else 5

        def head_mask(a):
            return const("head16" if a.dv == 16 else "head64")

        def stack_mask(a):
            return const("stack37" if a.keys == T else "stack38")

        gate_rows = {l: nc.dram_tensor(f"gate_rows{l}", [m.whole + H, N], F32, kind="Internal").ap()
                     for l, m in enumerate(MOE)}

        def chunk_walk(eng, m, body):
            for first, count, looped in m.segments:
                if looped:
                    with eng.Fori(0, count // RING) as i:
                        for j in range(RING):
                            body(i * RING + (first + j), first + j, i)
                else:
                    for c in range(first, first + count):
                        body(c, c, 0)

        norms = [NormPlan("patch", patches, None, ("patches_in1", 16), PB, PK, "mean_pd"),
                 NormPlan("embed", embed, None, ("embed_done", 4), PB)]
        for l in range(4):
            norms.append(NormPlan(f"att{l}", h, xn, ("h_embed", 1) if l == 0 else (f"h_moe{l - 1}", 4)))
            if l == 3:
                norms.append(NormPlan("ema", mixed, normed3, ("mixed", 1), w="gamma"))
            norms.append(NormPlan(f"moe{l}", h, xn, (f"h_att{l}", 4)))
        for at, s in enumerate(norms):
            s.index = at
            s.at = 2 * at
            s.cen = q_raw[:, 0:s.kc * s.cols].rearrange("p (k n) -> p k n", k=s.kc)
            s.sq = v_raw[:, 0:s.kc * s.cols].rearrange("p (k n) -> p k n", k=s.kc)
        norm_of = {s.n: s for s in norms}

        block = ctx.enter_context(nc.Block())

        @block.sync
        def _(sp):
            sp.dma_start(rel, ins["rel"]).then_inc(sem("rel_in"), 16)
            sp.dma_start(consts[:, :], ins["consts"]).then_inc(sem("consts_in"), 16)
            for part in range(2):
                ks = slice(part * PK // 2, (part + 1) * PK // 2)
                sp.dma_start(patches[:, ks, :], ins["patches"][:, ks, :]).then_inc(sem(f"patches_in{part}"), 16)
            sp.dma_start(vecs[:, :], ins["vecs"]).then_inc(sem("vecs_in"), 16)
            lin_cols = PK * D
            sp.dma_start(weights[:, 0:lin_cols], ins["weights_lo"][:, 0:lin_cols]).then_inc(sem("lin_w_in"), 16)
            sp.dma_start(weights[:, lin_cols:WEIGHTS_LO_W], ins["weights_lo"][:, lin_cols:]).then_inc(sem("att_w0"), 16)
            sp.dma_start(router_w[:, :, :], ins["router_w"]).then_inc(sem("router_w_in"), 16)
            sp.dma_start(b2[:, :], ins["b2"]).then_inc(sem("router_w_in"), 16)
            for l, m in enumerate(MOE):
                w_in = ins[f"experts{l}"]

                def load_weights(c, place, i):
                    slot = place % RING
                    sp.dma_start(w_ring[:, slot, 0:m.width], w_in[c]).then_inc(sem(f"w_in{slot}"), 16)

                def load_gate(c, place, i):
                    if place < m.whole:
                        slot = place % RING
                        row = gate_rows[l][bass.ds(c, 1), :].broadcast_to([P, N])
                        sp.dma_start(g_ring[:, slot, :], row).then_inc(sem(f"gate_in{slot}"), 16)

                if l >= 1:
                    sp.wait_ge(sem("down_done"), m.at)
                for c in range(RING):
                    load_weights(c, c, 0)
                def load_next(c, place, i):
                    sp.wait_ge(sem("down_done"), m.at + i * (2 * RING) + 2 * (place - RING) + 2)
                    load_weights(c, place, i)

                for c in range(RING, m.shared_chunks):
                    load_next(c, c, 0)
                sp.wait_ge(sem("gates_ready"), l + 1)
                rows = gate_rows[l][m.shared_chunks:m.whole, :].rearrange("(f e) n -> e f n", e=m.e)
                sp.dma_start(rows, spread(gates_t[0:m.e, 0:N], 1, m.per_expert)).then_inc(sem(f"rows_out{l}"), 16)
                sp.wait_ge(sem(f"rows_out{l}"), 16)
                for c in range(m.shared_chunks, RING):
                    load_gate(c, c, 0)
                def stream(c, place, i):
                    if place >= max(RING, m.shared_chunks):
                        load_next(c, place, i)
                        load_gate(c, place, i)
                    if l == 2 and place == m.peeled - 1:
                        sp.wait_ge(sem("out_proj"), 4 * (l + 1))
                        sp.dma_start(weights[:, 0:WEIGHTS_3_W], ins["weights_3"]).then_inc(sem("att_w3"), 16)
                    if m.tails and place == m.peeled - 1:
                        rows = gate_rows[l][m.shared_chunks:m.shared_chunks + m.e, :]
                        sp.dma_start(g_tail[:, :],
                                     spread(rows, 1, m.tail_rows)).then_inc(sem(f"tail_in{l}"), 16)

                chunk_walk(sp, m, stream)
                if l == 1:
                    sp.dma_start(weights[:, 0:WEIGHTS_2_W], ins["weights_2"]).then_inc(sem("att_w2"), 16)
            for t in range(2):
                cols = slice(t * HN, (t + 1) * HN)
                sp.wait_ge(sem("h_moe3"), 2 * t + 2)
                sp.dma_start(out[:, :, cols], h[:, :, cols]).then_inc(sem("out_stored"), 16)
            sp.wait_ge(sem("out_stored"), 32)

        @block.tensor
        def _(pe):
            def keep_busy(bank, n):
                busy = consts[:, 0:2 * P].bitcast(BF16)
                for _ in range(n):
                    pe.matmul(ps[:, bank, 0:BANK], busy[:, 0:P], busy, start=True, stop=True)

            def norm(s, free=3):
                means(s)
                if free is not None:
                    keep_busy(free, 4)
                variances(s, free)

            def means(s):
                for t in range(2):
                    pe.wait_ge(sem(s.after[0]), s.after[1] if s.src is not h else max(1, s.after[1] * (t + 1) // 2))
                    for k in range(s.kc):
                        mm = pe.matmul(ps[:, 4 + t, 0:s.hc], const(s.ones), s.src[:, k, t * s.hc:(t + 1) * s.hc],
                                       start=(k == 0), stop=(k == s.kc - 1))
                    mm.then_inc(sem("mean"), 1)
            def variances(s, free):
                for t, rows in s.tiles:
                    if s.kc_sq == s.kc and t in (0, 2):
                        pe.wait_ge(sem("square"), s.at + (1 if t == 0 else 2))
                    for k in range(s.kc_sq):
                        mm = pe.matmul(ps[0:rows, 6, t:t + 1], s.sq[:, k, t * P:t * P + rows], const(s.ones)[:, 0:1],
                                       start=(k == 0), stop=(k == s.kc_sq - 1))
                mm.then_inc(sem("var"), 1)
                if free is not None:
                    keep_busy(free, 5)
                pe.wait_ge(sem("rstd_ready"), s.index + 1)
                for t, rows in s.tiles:
                    bank, col = (7, t * P) if t < 3 else (6, (t - 2) * P)
                    mm = pe.matmul(ps[:, bank, col:col + rows], rstd[0:rows, t:t + 1].broadcast_to([rows, P]),
                                   ident[0:rows, 0:rows], start=True, stop=True)
                    if t in (2, TT - 1):
                        mm.then_inc(sem("rstd_spread"), 1)

            def project(l, w, chunks):
                pe.wait_ge(sem(f"att_w{0 if l == 1 else l}"), 16)
                j = 0
                order = ATT[l].order if l < 3 else [divmod(n, chunks) for n in range(3 * chunks)]
                for n, (kind, m) in enumerate(order):
                    m += kind * chunks
                    for t in range(2):
                        if n == 0:
                            pe.wait_ge(sem(f"normed_att{l}"), t + 1)
                        if j >= 8:
                            pe.wait_ge(sem(f"proj_out{l}_{j % 2}"), (j - 8) // 2 + 1)
                        for k in range(KD):
                            cols = slice(t * HN, (t + 1) * HN)
                            if l == 2:
                                if t == k == 0:
                                    pe.wait_ge(sem("w2_lo_done"), n + 1)
                                if n == k == 0:
                                    pe.wait_ge(sem("x2_lo_done"), t + 1)
                                wh, wl = (a_[:, n % RING, k * P:(k + 1) * P] for a_ in (w2_hi, w2_lo))
                                pe.matmul(ps[:, j % 8, 0:HN], wh, x2_hi[:, k, cols], start=(k == 0), stop=False)
                                pe.matmul(ps[:, j % 8, 0:HN], wh, x2_lo[:, k, cols], start=False, stop=False)
                                mm = pe.matmul(ps[:, j % 8, 0:HN], wl, x2_hi[:, k, cols], start=False, stop=(k == KD - 1))
                                continue
                            mm = pe.matmul(ps[:, j % 8, 0:HN], w[:, k, m * P:(m + 1) * P],
                                           xn[:, k, cols], start=(k == 0), stop=(k == KD - 1))
                        mm.then_inc(sem(f"proj{l}"), 1)
                        j += 1

            def attention(l):
                a = ATT[l]
                w_qkv, w_o = att_w[l]
                project(l, w_qkv, a.chunks)
                kb, vv, S = kblk_view(a), v_view(a), a.keys
                pe.wait_ge(sem("q_pad"), l + 1)
                for par in range(2):
                    pe.wait_ge(sem(f"proj_out{l}_{par}"), 3 * a.chunks)

                keep_busy(2, 10 if l < 2 else 1)
                def score(s):
                    p, i = a.steps[s]
                    if s >= 1:
                        pe.wait_ge(sem("scored"), a.at + s)
                    for img in range(2):
                        tok = (2 * p + img) * T
                        for m in range(a.chunks):
                            head = m * a.hpc
                            dst = ps[64 * img:64 * img + 64, head // 8,
                                     (head % 8) * S:(head % 8 + a.hpc) * S]
                            mm = pe.matmul(dst, q_all[:, i * a.chunks + m, tok:tok + 64],
                                           kb[:, m, :, 2 * p + img, :], start=(head % 8 == 0),
                                           stop=(head % 8 + a.hpc == 8), skip_group_check=True)
                    mm.then_inc(sem("score"), 1)

                def stack(p, r):
                    if p * a.rounds + r >= 1:
                        pe.wait_ge(sem(f"stacked_even{l}"), p * a.rounds + r)
                        pe.wait_ge(sem(f"stacked_odd{l}"), p * a.rounds + r)
                    for n in range(4):
                        img, m = divmod(4 * r + n, a.chunks)
                        mm = pe.transpose(ps[0:S, 4, n * P:(n + 1) * P], vv[:, m, 2 * p + img, :], ident)
                    mm.then_inc(sem(f"stack{l}"), 1)

                def turn_out(g):
                    if l == 1:
                        pe.wait_ge(sem("rms_normed"), g + 1)
                    else:
                        pe.wait_ge(sem("summed"), a.at + g + 1)
                    if g:
                        pe.wait_ge(sem("out_copied"), a.groups_at + g)
                    for n in range(a.group):
                        for m in range(a.chunks):
                            dst = ps[:, out_bank[l] + n // 2 + m // 4, (2 * n % 4 + m % 4) * P:(2 * n % 4 + m % 4 + 1) * P]
                            mm = pe.transpose(dst, out_view(l, g * a.group + n)[:, m * P:(m + 1) * P], ident)
                    mm.then_inc(sem("turned"), 1)

                def turn_probs(s):
                    p, i = a.steps[s]
                    pe.wait_ge(sem("exped"), a.at + s + 1)
                    if s >= 1:
                        pe.wait_ge(sem("probs_copied"), a.at + s)
                    if l == 2 and s >= 2:
                        pe.wait_ge(sem("out_copied"), a.groups_at + s - 1)
                    for g in range(8):
                        mm = pe.transpose(ps[:, 2 + g // 4, (g % 4) * P:(g % 4 + 1) * P],
                                          probs[:, s % 2, g * P:(g + 1) * P], ident)
                    mm.then_inc(sem("probs_turned"), 1)

                def values(s, part):
                    p, i = a.steps[s]
                    if part == 0:
                        ahead = 2 if l == 0 else 1
                        if s >= ahead:
                            pe.wait_ge(sem("summed"), a.at + s - ahead + 1)
                        keep_busy(value_banks(l, s), 1 if l == 2 else 2)
                        pe.wait_ge(sem("probs_copied"), a.at + s + 1)
                        pe.wait_ge(sem(f"stacked_even{l}"), (p + 1) * a.rounds)
                        pe.wait_ge(sem(f"stacked_odd{l}"), (p + 1) * a.rounds)
                    d1 = a.dv + 1
                    each = 16 // a.parts
                    for n in range(part * each, (part + 1) * each):
                        img, g = divmod(n, 8)
                        st = stack_view(a, 2 * (p % 2) + img)
                        if l == 2:
                            bank, col = 5 + g // 3, (g % 3) * 2 * d1
                        else:
                            bank, col = value_banks(l, s), g * 2 * d1
                        at = (g * 2 + img) * T
                        mm = pe.matmul(ps[64 * img:64 * img + 64, bank, col:col + 2 * d1], probs_t[:, at:at + 64],
                                       st[:, 2 * g:2 * g + 2, :].rearrange("p h d -> p (h d)"),
                                       start=(col == 0), stop=True, skip_group_check=True)
                    if part == a.parts - 1:
                        mm.then_inc(sem("valued"), 1)

                pe.wait_ge(sem("stack_ones"), l + 1)
                score(0)
                if l == 2:
                    pe.wait_ge(sem("null_v_ready"), 1)
                for r in range(a.rounds):
                    stack(0, r)
                    keep_busy(7, 2)
                score(1)
                for s, (p, i) in enumerate(a.steps):
                    stacks = s + 1 < len(a.steps) and a.steps[s + 1][1] == 0
                    if s == len(a.steps) - 1:
                        pe.wait_ge(sem("out_copied"), a.groups_at + a.groups // 2)
                        pe.wait_ge(sem("scored"), a.at + s + 1)
                        if l == 2:
                            out_job(w_o, a.chunks, q_all, 0, 0)
                    turn_probs(s)
                    if s == len(a.steps) - 1:
                        out_job(w_o, a.chunks, q_all, 1 if l == 2 else 0, 0)
                    if stacks and a.rounds > 1:
                        stack(p + 1, 0)
                    if s + 2 < len(a.steps):
                        score(s + 2)
                    if stacks:
                        stack(p + 1, 1 if a.rounds > 1 else 0)
                    values(s, 0)
                    if s - a.out_lag in a.turn_at:
                        turn_out(a.turn_at.index(s - a.out_lag))
                    if a.rounds > 1:
                        if stacks:
                            stack(p + 1, 2)
                        values(s, 1)
                        if stacks:
                            stack(p + 1, 3)
                if l < 2:
                    out_job(w_o, a.chunks, q_all, 1, 0)
                keep_busy(4, (0, 4, 4)[l])
                turn_out(a.groups - 1)
                keep_busy(4, 3)
                pe.wait_ge(sem("out_copied"), a.groups_at + a.groups)
                for m in range(KD):
                    out_job(w_o, a.chunks, q_all, m, 1)

            def out_job(w_o, chunks, src, m, t):
                for k in range(chunks):
                    mm = pe.matmul(ps[:, 6 * t + m, 0:HN], w_o[:, k, m * P:(m + 1) * P],
                                   src[:, k, t * HN:(t + 1) * HN], start=(k == 0), stop=(k == chunks - 1))
                mm.then_inc(sem("out_proj"), 1)

            def route(l):
                m = MOE[l]
                pe.wait_ge(sem(f"normed_moe{l}"), 2)
                if l == 0:
                    pe.wait_ge(sem("router_w_in"), 32)
                for t in range(TT):
                    for k in range(KD):
                        mm = pe.matmul(ps[:, 0, t * m.e:(t + 1) * m.e], xn[:, k, t * P:(t + 1) * P],
                                       router_w[:, k, m.col:m.col + m.e], start=(k == 0), stop=(k == KD - 1))
                mm.then_inc(sem("logits"), 1)

            def turn_gates(l):
                m = MOE[l]
                keep_busy(3, 13 if l == 2 else 0)
                pe.wait_ge(sem("gated"), l + 1)
                for n, src in enumerate([router["gate"], router["hit"]][:2 if l == 2 else 1]):
                    for t in range(TT):
                        mm = pe.transpose(ps[0:m.e, 2 * n + t // 4, (t % 4) * P:(t % 4 + 1) * P],
                                          src[:, t, 0:m.e], ident)
                mm.then_inc(sem("gates_turned"), 1)

            def experts(l):
                m = MOE[l]
                hid_hi, hid_lo, w_hi, w_lo = split[m.glu]
                total = 2 * m.chunks

                def bank_of(place, t):
                    return 4 + 2 * t if m.glu else 4 + 2 * (place % 2) + t

                def split_product(dst, w_at, slot, xh, xl, first, last, **kw):
                    wh, wl = w_hi[:, slot, w_at:w_at + P], w_lo[:, slot, w_at:w_at + P]
                    pe.matmul(dst, wh, xh, start=first, stop=False, **kw)
                    pe.matmul(dst, wh, xl, start=False, stop=False, **kw)
                    return pe.matmul(dst, wl, xh, start=False, stop=last, **kw)

                def up(place, i, t):
                    slot = place % RING
                    if t == 0:
                        pe.wait_ge(sem("w_lo_done"), m.chunks_at + i * RING + place + 1)
                    u = 2 * place + t
                    if m.glu and u >= 2:
                        pe.wait_ge(sem("act_done"), m.at + i * (2 * RING) + u - 1)
                        if u - 2 < 2 * m.shared_chunks:
                            pe.wait_ge(sem("hidden_done"), m.at + u - 1)
                        else:
                            pe.wait_ge(sem("gated_u"), m.at_glu + i * (2 * RING) + u - 1 - 2 * m.shared_chunks)
                    elif u >= 4:
                        pe.wait_ge(sem("act_done"), m.at + i * (2 * RING) + u - 3)
                    for n in range(2 if m.glu else 1):
                        for k in range(KD):
                            cols = slice(t * HN, (t + 1) * HN)
                            mm = split_product(ps[:, bank_of(place, t) + n, 0:HN], (n * KD + k) * P, slot,
                                               x_hi[:, k, cols], x_lo[:, k, cols], k == 0, k == KD - 1)
                    mm.then_inc(sem("up_done"), 1)

                def down(place, i, t):
                    slot = place % RING
                    hid = (2 * place + t) % m.slots
                    if 2 * place + t == 0:
                        pe.wait_ge(sem("gates_ready"), l + 1)
                    pe.wait_ge(sem("hid_lo_done"), m.at + i * (2 * RING) + 2 * place + t + 1)
                    for d in range(KD):
                        mm = split_product(ps[:, 2 * d + t, 0:HN], m.up_cols + d * P, slot, hid_hi[:, hid, :],
                                           hid_lo[:, hid, :], place == 0,
                                           2 * place + t >= total - 2, skip_group_check=True)
                    mm.then_inc(sem("down_done"), 1)

                def down_of(place, t, i):
                    u = 2 * place + t - m.lag
                    if u >= 0:
                        down(u // 2, i, u % 2)

                def body(c, place, i):
                    for t in range(2):
                        up(place, i, t)
                        if 2 * place + t == m.lag - 1:
                            turn_gates(l)
                            if not m.shared_chunks:
                                pe.wait_ge(sem("gates_ready"), l + 1)
                                keep_busy(1, 18)
                            elif not m.glu:
                                keep_busy(7, 8)
                        down_of(place, t, i)
                    if m.bias and place == m.peeled - 1:
                        for d in range(KD):
                            for t in range(2):
                                pe.matmul(ps[:, 2 * d + t, 0:HN], b2[0:m.e, d * P:(d + 1) * P],
                                          gates_t[0:m.e, t * HN:(t + 1) * HN], start=False, stop=False,
                                          skip_group_check=True)

                pe.wait_ge(sem("x_split"), 2 * l + 2)
                chunk_walk(pe, m, body)
                for u in range(total - m.lag, total):
                    down(u // 2, 0, u % 2)

            pe.wait_ge(sem("consts_in"), 16)
            keep_busy(3, 12)
            s = norm_of["patch"]
            for k in range(PK):
                if k % (PK // 2) == 0:
                    pe.wait_ge(sem(f"patches_in{k // (PK // 2)}"), 16)
                for t in range(2):
                    mm = pe.matmul(ps[:, 4 + t, 0:s.hc], const(s.ones), s.src[:, k, t * s.hc:(t + 1) * s.hc],
                                   start=(k == 0), stop=(k == PK - 1))
                    if k == PK - 1:
                        mm.then_inc(sem("mean"), 1)
            pe.wait_ge(sem("rel_summed"), 1)
            for key in range(T):
                at = T - 1 - key
                mm = pe.matmul(ps[0:64, 6 + key // 32, key % 32 * H:(key % 32 + 1) * H], const("shift")[0:OFFSETS, at:at + 64],
                               rel_sums, start=True, stop=True)
            mm.then_inc(sem("rel_turned"), 1)
            pe.wait_ge(sem("lin_w_scaled"), 1)
            for t in range(2):
                pe.wait_ge(sem("centred"), t + 1)
                for m in range(KD):
                    for k in range(PK):
                        mm = pe.matmul(ps[:, 2 * m + t, 0:HP], lin_scaled[:, k, m * P:(m + 1) * P],
                                       s.cen[:, k, t * HP:(t + 1) * HP], start=(k == 0), stop=(k == PK - 1))
            mm.then_inc(sem("embedded"), 1)
            pe.wait_ge(sem("bias0_ready"), 2)
            for m in range(KD):
                for k in range(PK):
                    mm = pe.matmul(ps[:, 7, m:m + 1], lin_w[:, k, m * P:(m + 1) * P], vec("ln1_b", k),
                                   start=(k == 0), stop=(k == PK - 1))
            mm.then_inc(sem("bias_embedded"), 1)
            pe.wait_ge(sem("squares_summed"), 1)
            variances(s, 5)
            keep_busy(5, 6)
            norm(norm_of["embed"])
            keep_busy(3, 14)
            for l in range(4):
                norm(norm_of[f"att{l}"])
                if l < 3:
                    attention(l)
                else:
                    project(3, att_w[3][0], KD)
                    pe.wait_ge(sem("proj_out3_0"), 6)
                    pe.wait_ge(sem("gate_out3"), KD)
                    keep_busy(3, 1)
                    norm(norm_of["ema"])
                    keep_busy(3, 14)
                    pe.wait_ge(sem("ema_gated"), 1)
                    for t in range(2):
                        for m in range(KD):
                            out_job(att_w[3][1], KD, mixed, m, t)
                norm(norm_of[f"moe{l}"])
                route(l)
                experts(l)

        @block.scalar
        def _(act):
            loaded = [0]

            def load_table(func):
                if loaded[0]:
                    act.wait_ge(sem("table_loaded"), loaded[0])
                loaded[0] += 1
                act.activation(act_scratch[:, :], ident[:, 0:1], func).then_inc(sem("table_loaded"), 1)

            def norm(s, after=None):
                load_table(ACT.Sqrt)
                squares(s)
                deviations(s)
                if after is not None:
                    load_table(after)

            def squares(s):
                for t in range(2):
                    act.wait_ge(sem("centred"), s.at + t + 1)
                    cols = slice(t * s.hc, (t + 1) * s.hc)
                    act.activation(s.sq[:, :, cols], s.cen[:, :, cols], ACT.Square).then_inc(sem("square"), 1)

            def deviations(s):
                act.wait_ge(sem("var"), s.index + 1)
                rows = s.tiles[-1][1]
                act.activation(std[:, 0:TT - 1], ps[:, 6, 0:TT - 1], ACT.Sqrt, bias=eps_col)
                act.activation(std[0:rows, TT - 1:TT], ps[0:rows, 6, TT - 1:TT], ACT.Sqrt,
                               bias=eps_col[0:rows]).then_inc(sem("std"), 1)

            def from_proj(l, j):
                act.wait_ge(sem(f"proj{l}"), j + 1)

            def attention(l):
                a = ATT[l]
                S = a.keys
                if l == 0:
                    act.wait_ge(sem("sub_scaled"), 1)

                def high_weights(n):
                    kind, m = a.order[n]
                    m += kind * a.chunks
                    if n == 0:
                        act.wait_ge(sem("att_w2"), 16)
                    if n >= RING:
                        act.wait_ge(sem("proj2"), 2 * (n - RING + 1))
                    act.activation(w2_hi[:, n % RING, :].rearrange("p (k n) -> p k n", k=KD),
                                   att_w[2][0][:, :, m * P:(m + 1) * P], ACT.Copy).then_inc(sem("w2_hi_done"), 1)

                if l == 2:
                    for n in range(RING - 1):
                        high_weights(n)
                    for t in range(2):
                        cols = slice(t * HN, (t + 1) * HN)
                        act.wait_ge(sem("normed_att2"), t + 1)
                        act.activation(x2_hi[:, :, cols], xn[:, :, cols], ACT.Copy).then_inc(sem("x2_hi_done"), 1)
                for j in range(0, 6 * a.chunks, 2):
                    kind, m = a.order[j // 2]
                    if l == 2 and 1 <= j // 2 <= 3 * a.chunks - RING + 1:
                        high_weights(j // 2 + RING - 2)
                    from_proj(l, j)
                    src = ps[:, j % 8, 0:HN]
                    imgs = src.rearrange("p (b s) -> p b s", b=B // 2)
                    done = sem(f"proj_out{l}_0")
                    if kind == 0 and l == 0:
                        act.activation(q_all[:, m, 0:HN], src, ACT.Identity, bias=small[:, m:m + 1],
                                       scale=0.25).then_inc(done, 1)
                    elif kind == 0 and l == 1:
                        act.activation(q_all[:, m, 0:HN], src, ACT.Identity, scale=small[:, 8:9])
                        act.activation(q_all[:, 2 + m, 0:HN], src, ACT.Identity, scale=small[:, 9:10]).then_inc(done, 1)
                    elif kind == 0:
                        if m == 0:
                            act.wait_ge(sem("logit_scale_ready"), 1)
                        act.activation(q_all[:, m, 0:HN], src, ACT.Identity, scale=small[:, 24 + m:25 + m]).then_inc(done, 1)
                    elif kind == 1:
                        for jh in range(a.hpc):
                            bias = small[:, 48 + 8 * m + jh:49 + 8 * m + jh] if l == 0 else 0.0
                            ins_ = act.activation(kblk_view(a)[:, m, jh, 0:B // 2, 0:T], imgs, ACT.Identity, bias=bias,
                                                  scale=head_mask(a)[:, jh:jh + 1])
                        ins_.then_inc(done, 1)
                    else:
                        bias = vec("v_b", m) if l == 0 else 0.0
                        act.activation(v_view(a)[:, m, 0:B // 2, 0:T], imgs, ACT.Identity, bias=bias).then_inc(done, 1)

                def stack_even(p, rounds):
                    for r in rounds:
                        act.wait_ge(sem(f"stack{l}"), p * a.rounds + r + 1)
                        if p >= 2:
                            act.wait_ge(sem("valued"), a.at + (p - 1) * a.subs)
                        src, dst = stack_parts(a, p, r, 0)
                        act.activation(dst, src, ACT.Copy).then_inc(sem(f"stacked_even{l}"), 1)

                def exponentials(s):
                    act.wait_ge(sem("shifted"), a.at + s + 1)
                    if s >= 2:
                        act.wait_ge(sem("probs_turned"), a.at + s - 1)
                    act.activation(probs[:, s % 2, :].rearrange("p (h k) -> p h k", h=H)[:, :, 0:S],
                                   scores[:, s % 2, 0:H * S].rearrange("p (h s) -> p h s", h=H),
                                   ACT.Exp).then_inc(sem("exped"), 1)

                act.wait_ge(sem("stack_ones"), l + 1)
                stack_even(0, range(a.rounds))
                exponentials(0)
                for s, (p, i) in enumerate(a.steps):
                    stacks = s + 1 < len(a.steps) and a.steps[s + 1][1] == 0
                    if s + 1 < len(a.steps):
                        exponentials(s + 1)
                    if stacks:
                        stack_even(p + 1, range(1))
                    act.wait_ge(sem("probs_turned"), a.at + s + 1)
                    if s >= 1:
                        act.wait_ge(sem("valued"), a.at + s)
                    pt = probs_t[:, 0:16 * T].rearrange("p (g i t) -> p g i t", g=8, i=2)
                    src = ps[:, 2:4, :].rearrange("p b (g i t) -> p (b g) i t", g=4, i=2)
                    act.activation(pt, src[:, :, :, 0:T], ACT.Copy).then_inc(sem("probs_copied"), 1)
                    if l == 1 and s - 1 in a.turn_at:
                        root_mean_square(a.turn_at.index(s - 1))
                    if stacks:
                        stack_even(p + 1, range(1, min(2, a.rounds)))
                    if s - a.out_lag in a.turn_at:
                        copy_out(l, a, a.turn_at.index(s - a.out_lag))
                    if stacks:
                        stack_even(p + 1, range(2, a.rounds))
                if l == 1:
                    load_table(ACT.Sqrt)
                    root_mean_square(a.groups - 1)
                copy_out(l, a, a.groups - 1)

            def root_mean_square(g):
                act.wait_ge(sem("mean_square"), g + 1)
                act.activation(rms[:, :], rms[:, :], ACT.Sqrt).then_inc(sem("rms_ready"), 1)

            def copy_out(l, a, g):
                act.wait_ge(sem("turned"), a.groups_at + g + 1)
                for n in range(a.group):
                    p = g * a.group + n
                    bank = out_bank[l] + n // 2
                    src = ps[:, bank:bank + a.chunks // 4 + 1, :].rearrange("p b (m i t) -> p (b m) i t", m=4, i=2)
                    at = 2 * n % 4
                    src = src[:, at:at + a.chunks, :, 0:T]
                    dst = q_all[:, 0:a.chunks, 2 * p * T:2 * (p + 1) * T].rearrange("p m (i t) -> p m i t", i=2)
                    ins_ = act.activation(dst, src, ACT.Copy, scale=small[:, 10:11] if l == 1 else 1.0)
                ins_.then_inc(sem("out_copied"), 1)

            def route(l):
                m = MOE[l]
                if l == 2:
                    act.wait_ge(sem("logits"), l + 1)
                    src = ps[:, 0, 0:TT * m.e].rearrange("p (t e) -> p t e", t=TT)
                    act.activation(router["raw"][:, :, 0:m.e], src, ACT.Sigmoid).then_inc(sem("sigmoid2"), 1)
                else:
                    act.wait_ge(sem(f"raw_shifted{l}"), 1)
                    act.activation(router["gate"][:, :, 0:m.e], router["gate"][:, :, 0:m.e], ACT.Exp).then_inc(sem(f"raw_exp{l}"), 1)

            def split_weights(l, place, i):
                m = MOE[l]
                w_hi = split[m.glu][2]
                slot = place % RING
                act.wait_ge(sem(f"w_in{slot}"), i * 16 + 16 * (place // RING + 1 + m.weights_at[slot]))
                if place >= RING:
                    act.wait_ge(sem("down_done"), m.at + i * (2 * RING) + 2 * (place - RING) + 2)
                act.activation(w_hi[:, slot, 0:m.split_cols], w_ring[:, slot, 0:m.split_cols],
                               ACT.Copy).then_inc(sem("w_hi_done"), 1)

            def experts(l):
                m = MOE[l]
                func = ACT.Silu if m.glu else ACT.Gelu_apprx_tanh
                hid_hi = split[m.glu][0]

                def high_part(i, u):
                    unit = m.at + i * (2 * RING) + u
                    act.wait_ge(sem("hidden_done"), unit + 1)
                    if u >= m.slots:
                        act.wait_ge(sem("down_done"), unit - m.slots + 1)
                    act.activation(hid_hi[:, u % m.slots, :], hidden[:, u % 2, :], ACT.Copy).then_inc(sem("hid_hi_done"), 1)

                def body(c, place, i):
                    for t in range(2):
                        u = 2 * place + t
                        unit = m.at + i * (2 * RING) + u
                        act.wait_ge(sem("up_done"), unit + 1)
                        if u >= 2:
                            act.wait_ge(sem("hidden_done"), unit - 1)
                        bias = w_ring[:, place % RING, 6 * P:6 * P + 1] if m.bias else 0.0
                        bank = 4 + 2 * t if m.glu else 4 + 2 * (place % 2) + t
                        act.activation(act_g[:, t, :], ps[:, bank, 0:HN], func, bias=bias).then_inc(sem("act_done"), 1)
                        if u >= 1:
                            high_part(i, u - 1)
                        if t == 0 and 1 <= place < m.chunks - 1:
                            split_weights(l, place + 1, i)

                chunk_walk(act, m, body)
                high_part(0, 2 * m.chunks - 1)

            act.wait_ge(sem("consts_in"), 16)
            load_table(ACT.Sqrt)
            act.wait_ge(sem("lin_w_in"), 16)
            act.wait_ge(sem("vecs_in"), 16)
            for k in range(PK):
                ins_ = act.activation(lin_scaled[:, k, :], lin_w[:, k, :], ACT.Copy, scale=vec("ln1_w", k))
            ins_.then_inc(sem("lin_w_scaled"), 1)
            s = norm_of["patch"]
            squares(s)
            deviations(s)
            for n, (t, at, width, bank, col) in enumerate(s.pieces):
                act.wait_ge(sem("rstd_spread"), t + 1)
                act.activation(rstd_rows[:, at:at + width], ps[:, bank, col:col + width], ACT.Copy).then_inc(sem("rstd_out"), 1)
            for n in range(2 * KD):
                t, m = divmod(n, KD)
                act.wait_ge(sem("embed_scaled"), n + 1)
                act.wait_ge(sem("lin_bias_ready"), 1)
                part = embed[:, m, t * HP:(t + 1) * HP]
                act.activation(part, part, ACT.Identity, bias=small[:, 44 + m:45 + m]).then_inc(sem("embed_done"), 1)
            norm(norm_of["embed"], ACT.Exp)
            act.wait_ge(sem("lambda_sums"), 1)
            act.activation(small[:, 12:14], small[:, 14:16], ACT.Exp).then_inc(sem("lambda_exp"), 1)
            act.activation(small[:, 32:40], vec("logit_scale", 0, 8), ACT.Exp).then_inc(sem("logit_exp"), 1)
            act.activation(small[:, 40:42], vec("beta", 0, 2), ACT.Sigmoid).then_inc(sem("rates_ready"), 1)
            for l in range(4):
                norm(norm_of[f"att{l}"], ACT.Exp if l < 3 else ACT.Silu)
                if l < 3:
                    attention(l)
                else:
                    for j in range(0, 12, 2):
                        kind, m = divmod(j // 2, KD)
                        from_proj(3, j)
                        dst = (q_all, v_flat, gate3)[kind]
                        act.activation(dst[:, m, 0:HN], ps[:, j % 8, 0:HN],
                                       ACT.Silu if kind == 2 else ACT.Copy).then_inc(sem("proj_out3_0"), 1)
                    for m in range(KD):
                        j = 9 + 2 * m
                        from_proj(3, j)
                        act.activation(gate3[:, m, HN:N], ps[:, j % 8, 0:HN], ACT.Silu).then_inc(sem("gate_out3"), 1)
                    norm(norm_of["ema"])
                norm(norm_of[f"moe{l}"], ACT.Sigmoid if l == 2 else ACT.Exp)
                for t in range(2):
                    cols = slice(t * HN, (t + 1) * HN)
                    act.wait_ge(sem(f"normed_moe{l}"), t + 1)
                    act.activation(x_hi[:, :, cols], xn[:, :, cols], ACT.Copy).then_inc(sem("x_hi_done"), 1)
                for c in range(2):
                    split_weights(l, c, 0)
                route(l)
                load_table(ACT.Silu if MOE[l].glu else ACT.Gelu_apprx_tanh)
                experts(l)

        @block.gpsimd
        def _(pool):
            pool.memset(xn[:, :, N:NPAD], 0.0).then_inc(sem("xn_pad"), 1)
            pool.memset(probs_t[:, :], 1.0).then_inc(sem("probs_t_pad"), 1)
            pool.memset(att_out[:, :], 0.0).then_inc(sem("att_out_pad"), 1)
            s = norm_of["patch"]
            pool.wait_ge(sem("square"), 2)
            for k in range(1, PK):
                if k > 1:
                    pool.wait_ge(sem("squares_added"), k - 1)
                pool.tensor_tensor(s.sq[:, 0, :], s.sq[:, 0, :], s.sq[:, k, :],
                                   ALU.add).then_inc(sem("squares_summed" if k == PK - 1 else "squares_added"), 1)
            for l in range(4):
                a = ATT[l] if l < 3 else None
                if a:
                    if l:
                        pool.wait_ge(sem(f"h_moe{l - 1}"), 4)
                    else:
                        pool.wait_ge(sem("embedded"), 1)
                    pool.memset(v_stack[:, :, :], 0.0).then_inc(sem("att_zeroed"), 1)
                    pool.memset(probs[:, :, :], 0.0).then_inc(sem("att_zeroed"), 1)
                if l == 3:
                    pool.wait_ge(sem("rates_ready"), 1)
                    pool.wait_ge(sem("h_moe2"), 4)
                    pool.tensor_copy(decay, spread(small[:, 40:42], 2, N)).then_inc(sem("decay_filled"), 1)
                    pool.wait_ge(sem("decay_filled"), 1)
                    pool.memset(decay.rearrange("p k (b t) -> p k b t", b=B)[:, :, :, 0:1], 0.0).then_inc(sem("decay_ready"), 1)
                if l == 2:
                    pool.wait_ge(sem("normed_att2"), 2)
                    for m in range(a.chunks):
                        ins_ = pool.tensor_copy(v_view(a)[:, m, :, T:T + 1], spread(vec("null_v", m), 1, B))
                    ins_.then_inc(sem("null_v_ready"), 1)
                for s in range(len(a.steps) if a else 0):
                    S = a.keys
                    pool.wait_ge(sem("maxed"), a.at + s + 1)
                    sc = scores[:, s % 2, 0:H * S].rearrange("p (h s) -> p h s", h=H)
                    pool.tensor_tensor(sc, sc, spread(row_max[:, s % 2, :], 2, S), ALU.subtract).then_inc(sem("shifted"), 1)

        @block.vector
        def _(dve):
            chain = [0]

            def link(ins_):
                chain[0] += 1
                ins_.then_inc(sem("vector_chain"), 1)
                dve.wait_ge(sem("vector_chain"), chain[0])

            def centre(s):
                dve.wait_ge(sem(s.after[0]), s.after[1])
                for t in range(2):
                    cols = slice(t * s.hc, (t + 1) * s.hc)
                    dve.wait_ge(sem("mean"), s.at + t + 1)
                    dve.tensor_tensor(s.cen[:, :, cols], s.src[:, :, cols], spread(ps[:, 4 + t, 0:s.hc], 1, s.kc),
                                      ALU.subtract).then_inc(sem("centred"), 1)

            def reciprocals(s):
                rows = s.tiles[-1][1]
                dve.wait_ge(sem("std"), s.index + 1)
                dve.reciprocal(rstd[:, 0:TT - 1], std[:, 0:TT - 1])
                dve.reciprocal(rstd[0:rows, TT - 1:TT], std[0:rows, TT - 1:TT]).then_inc(sem("rstd_ready"), 1)

            def norm(s, done):
                centre(s)
                reciprocals(s)
                dve.wait_ge(sem("centred"), s.at + 2)
                for t, at, width, bank, col in s.pieces:
                    cols = slice(at, at + width)
                    dve.wait_ge(sem("rstd_spread"), s.at + t + 1)
                    if s.w:
                        for k in range(s.kc):
                            ins_ = dve.scalar_tensor_tensor(s.out[:, k, cols], s.cen[:, k, cols], vec(s.w, k),
                                                            ps[:, bank, col:col + width], ALU.mult, ALU.mult)
                    else:
                        ins_ = dve.tensor_tensor(s.out[:, :, cols], s.cen[:, :, cols],
                                                 spread(ps[:, bank, col:col + width], 1, s.kc), ALU.mult)
                    if at != s.hc:
                        ins_.then_inc(sem(done), 1)

            def attention(l):
                a = ATT[l]
                S = a.keys
                def low_weights(n):
                    kind, m = a.order[n]
                    m += kind * a.chunks
                    dve.wait_ge(sem("w2_hi_done"), n + 1)
                    dve.tensor_tensor(w2_lo[:, n % RING, :].rearrange("p (k n) -> p k n", k=KD),
                                      att_w[2][0][:, :, m * P:(m + 1) * P],
                                      w2_hi[:, n % RING, :].bitcast(F32).rearrange("p (k n) -> p k n", k=KD),
                                      ALU.subtract).then_inc(sem("w2_lo_done"), 1)

                if l == 2:
                    low_weights(0)
                    for t in range(2):
                        cols = slice(t * HN, (t + 1) * HN)
                        dve.wait_ge(sem("x2_hi_done"), t + 1)
                        dve.tensor_tensor(x2_lo[:, :, cols], xn[:, :, cols], x2_hi[:, :, cols].bitcast(F32),
                                          ALU.subtract).then_inc(sem("x2_lo_done"), 1)
                    for n in range(1, RING - 1):
                        low_weights(n)
                dve.wait_ge(sem(f"normed_att{l}"), 2)
                dve.memset(q_all[:, 0:a.subs * a.chunks, N:NPAD], 0.0).then_inc(sem("q_pad"), 1)
                dve.wait_ge(sem("att_zeroed"), 2 * l + 2)
                ones = v_stack[:, :, 0:H * (a.dv + 1)].rearrange("p i (h d) -> p i h d", h=H)[:, :, :, a.dv]
                dve.tensor_copy(ones, spread(stack_mask(a), 1, 4)).then_inc(sem("stack_ones"), 1)
                if l == 2:
                    link(dve.tensor_scalar(small[:, 24:32], small[:, 32:40], 0.125, None, ALU.mult))
                    dve.tensor_copy(small[:, 92:93], small[:, 24:25]).then_inc(sem("logit_scale_ready"), 1)
                for j in range(1, 6 * a.chunks, 2):
                    kind, m = a.order[j // 2]
                    if l == 2 and 1 <= j // 2 <= 3 * a.chunks - RING + 1:
                        low_weights(j // 2 + RING - 2)
                    dve.wait_ge(sem(f"proj{l}"), j + 1)
                    src = ps[:, j % 8, 0:HN]
                    imgs = src.rearrange("p (b s) -> p b s", b=B // 2)
                    done = sem(f"proj_out{l}_1")
                    if kind == 0 and l == 0:
                        dve.tensor_scalar(q_all[:, m, HN:N], src, vec("q_b", m), 0.25, ALU.add, ALU.mult).then_inc(done, 1)
                    elif kind == 0 and l == 1:
                        for i in range(2):
                            ins_ = dve.tensor_scalar(q_all[:, 2 * i + m, HN:N], src, small[:, 8 + i:9 + i], None, ALU.mult)
                        ins_.then_inc(done, 1)
                    elif kind == 0:
                        dve.tensor_scalar(q_all[:, m, HN:N], src, small[:, 24 + m:25 + m], None, ALU.mult).then_inc(done, 1)
                    elif kind == 1:
                        for jh in range(a.hpc):
                            mask = head_mask(a)[:, jh:jh + 1]
                            dst = kblk_view(a)[:, m, jh, B // 2:B, 0:T]
                            if l == 2:
                                dve.tensor_scalar(kblk_view(a)[:, m, jh, :, T:S], spread(vec("null_k", m), 1, B), mask,
                                                  None, ALU.mult)
                            if l == 0:
                                ins_ = dve.tensor_scalar(dst, imgs, vec("k_b", m), mask, ALU.add, ALU.mult)
                            else:
                                ins_ = dve.tensor_scalar(dst, imgs, mask, None, ALU.mult)
                        ins_.then_inc(done, 1)
                    else:
                        dst = v_view(a)[:, m, B // 2:B, 0:T]
                        if l == 0:
                            dve.tensor_scalar(dst, imgs, vec("v_b", m), None, ALU.add).then_inc(done, 1)
                        else:
                            dve.tensor_copy(dst, imgs).then_inc(done, 1)


                def scored(s):
                    dve.wait_ge(sem("score"), a.at + s + 1)
                    if s >= 2:
                        dve.wait_ge(sem("exped"), a.at + s - 1)
                    src = ps[:, 0:2, 0:8 * S].rearrange("p b (h s) -> p b h s", h=8)
                    dst = scores[:, s % 2, 0:H * S].rearrange("p (b h s) -> p b h s", b=2, h=8)
                    if l == 0:
                        bias = bias0[:, :, :].rearrange("p (b h) s -> p b h s", b=2)
                    else:
                        bias = spread(spread(const("causal37" if S == T else "causal38"), 1, 8), 1, 2)
                    dve.tensor_tensor(dst, src, bias, ALU.add).then_inc(sem("scored"), 1)
                    dve.wait_ge(sem("scored"), a.at + s + 1)
                    dve.tensor_reduce(row_max[:, s % 2, :], scores[:, s % 2, 0:H * S].rearrange("p (h s) -> p h s", h=H),
                                      AX.X, ALU.max).then_inc(sem("maxed"), 1)

                def stack_odd(p, rounds):
                    for r in rounds:
                        dve.wait_ge(sem(f"stacked_even{l}"), p * a.rounds + r + 1)
                        if p >= 2:
                            dve.wait_ge(sem("valued"), a.at + (p - 1) * a.subs)
                        src, dst = stack_parts(a, p, r, 1)
                        dve.tensor_copy(dst, src).then_inc(sem(f"stacked_odd{l}"), 1)

                def summed(s):
                    p, i = a.steps[s]
                    d1 = a.dv + 1
                    dve.wait_ge(sem("valued"), a.at + s + 1)
                    if l != 1 and s >= 1:
                        dve.wait_ge(sem("turned"), a.groups_at + s)
                    if l == 2:
                        parts = [(ps[:, 5 + b, 0:n * d1].rearrange("p (h d) -> p h d", h=n), 6 * b, n)
                                 for b, n in enumerate((6, 6, 4))]
                    else:
                        parts = [(ps[:, value_banks(l, s), 0:H * d1].rearrange("p (h d) -> p h d", h=H), 0, H)]
                    for src, h0, n in parts:
                        ins_ = dve.reciprocal(sums_r[:, i, h0:h0 + n], src[:, :, a.dv])
                    link(ins_)
                    if i == 1:
                        link(dve.tensor_scalar(sums_r[:, 1, :], sums_r[:, 1, :], small[:, 11:12], None, ALU.mult))
                    out_p = out_view(l, p)
                    dst = (att_tmp[:, :] if i == 1 else out_p).rearrange("p (h d) -> p h d", h=H)
                    for n_, (src, h0, n) in enumerate(parts):
                        ins_ = dve.tensor_tensor(dst[:, h0:h0 + n, :], src[:, :, 0:a.dv],
                                                 spread(sums_r[:, i, h0:h0 + n], 2, a.dv), ALU.mult)
                    ins_.then_inc(sem("summed"), 1)
                    if i == 1:
                        dve.wait_ge(sem("summed"), a.at + s + 1)
                        link(dve.tensor_tensor(out_p, out_p, att_tmp[:, :], ALU.subtract))

                def group_view(g):
                    return g_ring[:, :, :].rearrange("p r n -> p (r n)")[:, g * a.group * D:(g + 1) * a.group * D]

                def mean_square(g):
                    o = group_view(g)
                    sq = v_raw_free[:, 0:a.group * D]
                    link(dve.tensor_tensor(sq, o, o, ALU.mult))
                    link(dve.tensor_reduce(rms[:, :], sq.rearrange("p (h d) -> p h d", d=a.dv), AX.X, ALU.add))
                    dve.tensor_scalar(rms[:, :], rms[:, :], 1.0 / a.dv, EPS, ALU.mult, ALU.add).then_inc(sem("mean_square"), 1)

                def rms_norm(g):
                    o = group_view(g).rearrange("p (h d) -> p h d", d=a.dv)
                    dve.wait_ge(sem("rms_ready"), g + 1)
                    link(dve.reciprocal(rms[:, :], rms[:, :]))
                    dve.tensor_tensor(o, o, spread(rms[:, :], 2, a.dv), ALU.mult).then_inc(sem("rms_normed"), 1)

                scored(0)
                stack_odd(0, range(a.rounds))
                scored(1)
                for s, (p, i) in enumerate(a.steps):
                    stacks = s + 1 < len(a.steps) and a.steps[s + 1][1] == 0
                    if stacks and a.rounds > 1:
                        stack_odd(p + 1, range(1))
                    if s + 2 < len(a.steps):
                        scored(s + 2)
                    if stacks:
                        stack_odd(p + 1, range(a.rounds)[1 if a.rounds > 1 else 0:])
                    if l == 1 and s - 2 in a.turn_at:
                        rms_norm(a.turn_at.index(s - 2))
                    summed(s)
                    if l == 1 and s in a.turn_at:
                        mean_square(a.turn_at.index(s))
                if l == 1:
                    mean_square(a.groups - 1)
                    rms_norm(a.groups - 1)

            def residual(l, bias):
                for t in range(2):
                    for m in range(KD):
                        cols = slice(t * HN, (t + 1) * HN)
                        dve.wait_ge(sem("out_proj"), 4 * l + 2 * t + m + 1)
                        src = ps[:, 6 * t + m, 0:HN]
                        if bias:
                            ins_ = dve.scalar_tensor_tensor(h[:, m, cols], src, vec(bias, m), h[:, m, cols], ALU.add, ALU.add)
                        else:
                            ins_ = dve.tensor_tensor(h[:, m, cols], src, h[:, m, cols], ALU.add)
                        ins_.then_inc(sem(f"h_att{l}"), 1)

            def ema():
                for j in range(1, 8, 2):
                    kind, m = divmod(j // 2, KD)
                    dve.wait_ge(sem("proj3"), j + 1)
                    dve.tensor_copy((q_all, v_flat)[kind][:, m, HN:N], ps[:, j % 8, 0:HN]).then_inc(sem("proj_out3_1"), 1)
                dve.wait_ge(sem("decay_ready"), 1)
                dve.wait_ge(sem("proj_out3_0"), 4)
                dve.wait_ge(sem("proj_out3_1"), 4)
                for m in range(KD):
                    link(dve.tensor_tensor_scan(state[:, m, :], decay[:, m, :], v_flat[:, m, :], 0.0, ALU.mult, ALU.add))
                dve.tensor_tensor(mixed, q_all[:, 0:KD, 0:N], state, ALU.mult).then_inc(sem("mixed"), 1)
                norm(norm_of["ema"], "normed_ema")
                dve.wait_ge(sem("normed_ema"), 2)
                dve.wait_ge(sem("proj_out3_0"), 6)
                dve.wait_ge(sem("gate_out3"), 2)
                for k in range(KD):
                    ins_ = dve.scalar_tensor_tensor(mixed[:, k, :], normed3[:, k, :], vec("ln_beta", k), gate3[:, k, :],
                                                    ALU.add, ALU.mult)
                ins_.then_inc(sem("ema_gated"), 1)

            def route(l):
                m = MOE[l]
                E, K = m.e, m.k
                raw, logit, hit, gate = (router[n] for n in ("raw", "logit", "hit", "gate"))
                src = ps[:, 0, 0:TT * E].rearrange("p (t e) -> p t e", t=TT)
                bias = spread(vec("router_b", m.col, E), 1, TT)
                if l == 2:
                    link(dve.memset(gates_t[0:E, 0:N], 0.0))
                dve.wait_ge(sem("logits"), l + 1)
                link(dve.memset(logit[:, :, E:E + 8], SENTINEL))
                if l == 2:
                    dve.wait_ge(sem("sigmoid2"), 1)
                    link(dve.tensor_tensor(logit[:, :, 0:E], raw[:, :, 0:E], bias, ALU.add))
                elif l == 1:
                    link(dve.tensor_copy(raw[:, :, 0:E], src))
                    link(dve.tensor_tensor(logit[:, :, 0:E], raw[:, :, 0:E], bias, ALU.add))
                elif l == 0:
                    link(dve.tensor_tensor(logit[:, :, 0:E], src, bias, ALU.add))
                    link(dve.tensor_copy(raw[:, :, 0:E], logit[:, :, 0:E]))
                else:
                    link(dve.tensor_tensor(raw[:, :, 0:E], src, bias, ALU.add))
                    link(dve.tensor_reduce(r_small[:, 0, :], raw[:, :, 0:E], AX.X, ALU.max))
                    dve.tensor_tensor(gate[:, :, 0:E], raw[:, :, 0:E], spread(r_small[:, 0, :], 2, E),
                                      ALU.subtract).then_inc(sem("raw_shifted3"), 1)
                    dve.wait_ge(sem("raw_exp3"), 1)
                    link(dve.tensor_reduce(r_small[:, 1, :], gate[:, :, 0:E], AX.X, ALU.add))
                    link(dve.reciprocal(r_small[:, 2, :], r_small[:, 1, :]))
                    link(dve.tensor_tensor(raw[:, :, 0:E], gate[:, :, 0:E], spread(r_small[:, 2, :], 2, E), ALU.mult))
                    link(dve.tensor_copy(logit[:, :, 0:E], raw[:, :, 0:E]))
                for t in range(TT):
                    ins_ = dve.max(top8[:, t, :], logit[:, t, 0:E])
                link(ins_)
                link(dve.memset(top8[:, :, K:8], SENTINEL))
                for t in range(TT):
                    ins_ = dve.match_replace(hit[:, t, 0:E + 8], top8[:, t, :], logit[:, t, 0:E + 8], TAKEN)
                link(ins_)
                link(dve.tensor_scalar(hit[:, :, 0:E], hit[:, :, 0:E], TAKEN, None, ALU.is_equal))
                hits = hit[:, :, 0:E]
                if l in (0, 1):
                    link(dve.tensor_scalar(gate[:, :, 0:E], hits, -MASKED, MASKED, ALU.mult, ALU.add))
                    link(dve.tensor_tensor(gate[:, :, 0:E], gate[:, :, 0:E], raw[:, :, 0:E], ALU.add))
                    link(dve.tensor_reduce(r_small[:, 0, :], gate[:, :, 0:E], AX.X, ALU.max))
                    dve.tensor_tensor(gate[:, :, 0:E], gate[:, :, 0:E], spread(r_small[:, 0, :], 2, E),
                                      ALU.subtract).then_inc(sem(f"raw_shifted{l}"), 1)
                    dve.wait_ge(sem(f"raw_exp{l}"), 1)
                elif l == 2:
                    link(dve.tensor_tensor(gate[:, :, 0:E], raw[:, :, 0:E], hits, ALU.mult))
                else:
                    dve.tensor_tensor(gate[:, :, 0:E], raw[:, :, 0:E], hits, ALU.mult).then_inc(sem("gated"), 1)
                if l != 3:
                    link(dve.tensor_reduce(r_small[:, 1, :], gate[:, :, 0:E], AX.X, ALU.add))
                    if l == 2:
                        link(dve.tensor_scalar(r_small[:, 1, :], r_small[:, 1, :], 1e-20, None, ALU.add))
                    link(dve.reciprocal(r_small[:, 2, :], r_small[:, 1, :]))
                    dve.tensor_tensor(gate[:, :, 0:E], gate[:, :, 0:E], spread(r_small[:, 2, :], 2, E),
                                      ALU.mult).then_inc(sem("gated"), 1)

            def spread_gates(l):
                E = MOE[l].e
                dve.wait_ge(sem("gates_turned"), l + 1)
                turned = lambda first: ps[0:E, first:first + 2, :].rearrange("p b n -> p (b n)")[:, 0:NPAD]
                if l != 2:
                    dve.tensor_copy(gates_t[0:E, 0:NPAD], turned(0)).then_inc(sem("gates_ready"), 1)
                else:
                    link(dve.tensor_copy(chosen_t[0:E, 0:NPAD], turned(2)))
                    link(dve.tensor_tensor_scan(g_tail[0:E, 0:N], chosen_t[0:E, 0:N], gates_t[0:E, 0:N], 0.0, ALU.add, ALU.add))
                    dve.scalar_tensor_tensor(gates_t[0:E, 0:N], g_tail[0:E, 0:N], float(CAPACITY), turned(0)[:, 0:N],
                                             ALU.is_le, ALU.mult).then_inc(sem("gates_ready"), 1)

            def split_weights(l, place, i):
                m = MOE[l]
                w_hi, w_lo = split[m.glu][2:]
                slot = place % RING
                dve.wait_ge(sem("w_hi_done"), m.chunks_at + i * RING + place + 1)
                dve.tensor_tensor(w_lo[:, slot, 0:m.split_cols], w_ring[:, slot, 0:m.split_cols],
                                  w_hi[:, slot, 0:m.split_cols].bitcast(F32), ALU.subtract).then_inc(sem("w_lo_done"), 1)

            def experts(l):
                m = MOE[l]
                hid_hi, hid_lo = split[m.glu][:2]

                def low_part(i, u):
                    dve.wait_ge(sem("hid_hi_done"), m.at + i * (2 * RING) + u + 1)
                    dve.tensor_tensor(hid_lo[:, u % m.slots, :], hidden[:, u % 2, :], hid_hi[:, u % m.slots, :].bitcast(F32),
                                      ALU.subtract).then_inc(sem("hid_lo_done"), 1)

                def body(c, place, i):
                    slot = place % RING
                    whole = place < m.whole
                    gates = g_ring[:, slot, :] if whole else g_tail[:, :]
                    for t in range(2):
                        u = 2 * place + t
                        unit = m.at + i * (2 * RING) + u
                        cols = slice(t * HN, (t + 1) * HN)
                        shared = place < m.shared_chunks
                        if whole and t == 0 and not shared:
                            dve.wait_ge(sem(f"gate_in{slot}"),
                                        i * 16 + 16 * (place // RING + 1 - m.ungated[slot] + m.gates_at[slot]))
                        elif place == m.whole and t == 0:
                            dve.wait_ge(sem(f"tail_in{l}"), 16)
                        dve.wait_ge(sem("up_done"), unit + 1)
                        if shared:
                            other = ps[:, 5 + 2 * t, 0:HN]
                        elif m.glu:
                            if m.bias:
                                ins_ = dve.scalar_tensor_tensor(gated_u[:, t, :], ps[:, 5 + 2 * t, 0:HN],
                                                                w_ring[:, slot, 6 * P + 1:6 * P + 2], gates[:, cols],
                                                                ALU.add, ALU.mult)
                            else:
                                ins_ = dve.tensor_tensor(gated_u[:, t, :], ps[:, 5 + 2 * t, 0:HN], gates[:, cols], ALU.mult)
                            ins_.then_inc(sem("gated_u"), 1)
                            dve.wait_ge(sem("gated_u"), m.at_glu + i * (2 * RING) + u + 1 - 2 * m.shared_chunks)
                            other = gated_u[:, t, :]
                        else:
                            other = gates[:, cols]
                        dve.wait_ge(sem("act_done"), unit + 1)
                        if u >= 2:
                            dve.wait_ge(sem("hid_lo_done"), unit - 1)
                        if shared and not m.glu:
                            ins_ = dve.tensor_copy(hidden[:, t, :], act_g[:, t, :])
                        elif shared and m.bias:
                            ins_ = dve.scalar_tensor_tensor(hidden[:, t, :], other, w_ring[:, slot, 6 * P + 1:6 * P + 2],
                                                            act_g[:, t, :], ALU.add, ALU.mult)
                        else:
                            ins_ = dve.tensor_tensor(hidden[:, t, :], act_g[:, t, :], other, ALU.mult)
                        ins_.then_inc(sem("hidden_done"), 1)
                        if u >= 1:
                            low_part(i, u - 1)
                        if t == 0 and 1 <= place < m.chunks - 1:
                            split_weights(l, place + 1, i)
                        if u == 0 and shared:
                            spread_gates(l)

                if not m.shared_chunks:
                    spread_gates(l)
                chunk_walk(dve, m, body)
                low_part(0, 2 * m.chunks - 1)
                for t in range(2):
                    dve.wait_ge(sem("down_done"), m.at + 2 * m.chunks - 1 + t)
                    for d in range(KD):
                        cols = slice(t * HN, (t + 1) * HN)
                        src = ps[:, 2 * d + t, 0:HN]
                        if m.bias:
                            ins_ = dve.scalar_tensor_tensor(h[:, d, cols], src, vec("sb2", d), h[:, d, cols], ALU.add, ALU.add)
                        else:
                            ins_ = dve.tensor_tensor(h[:, d, cols], src, h[:, d, cols], ALU.add)
                        ins_.then_inc(sem(f"h_moe{l}"), 1)

            dve.wait_ge(sem("rel_in"), 16)
            dve.tensor_reduce(rel_sums, rel.rearrange("p (h d) -> p h d", h=H), AX.X, ALU.add).then_inc(sem("rel_summed"), 1)
            dve.wait_ge(sem("consts_in"), 16)
            dve.wait_ge(sem("vecs_in"), 16)
            link(dve.memset(small[:, :], 0.0))
            lam = vec("lambdas", 0, 32).rearrange("p (a b d) -> p a b d", a=2, b=2)
            link(dve.tensor_tensor(small[:, 16:32].rearrange("p (a d) -> p a d", a=2), lam[:, :, 0, :], lam[:, :, 1, :], ALU.mult))
            dve.tensor_reduce(small[:, 14:16], small[:, 16:32].rearrange("p (a d) -> p a d", a=2), AX.X,
                              ALU.add).then_inc(sem("lambda_sums"), 1)
            for m in range(KD):
                dve.tensor_scalar(small[:, 48 + 8 * m:56 + 8 * m], const("head16"), vec("k_b", m), None, ALU.mult)
            dve.tensor_scalar(small[:, 0:2], vec("q_b", 0, 2), 0.25, None, ALU.mult)
            dve.tensor_scalar(small[:, 10:11], vec("rms_w"), 1.0 - LAMBDA_INIT, None, ALU.mult)
            dve.tensor_scalar(small[:, 8:10], const("sub"), float(8) ** -0.5, None, ALU.mult).then_inc(sem("sub_scaled"), 1)
            dve.wait_ge(sem("sub_scaled"), 1)

            s = norm_of["patch"]
            centre(s)
            dve.wait_ge(sem("rel_turned"), 1)
            for img in range(2):
                rows = slice(64 * img, 64 * img + 64)
                for first, n in ((0, 32), (32, T - 32)):
                    causal = spread(const("causal37")[rows, first:first + n], 2, H)
                    ins_ = dve.tensor_tensor(bias0[rows, :, first:first + n].rearrange("p h t -> p t h"),
                                             ps[0:64, 6 + first // 32, 0:n * H].rearrange("p (t h) -> p t h", h=H),
                                             causal, ALU.add)
                ins_.then_inc(sem("bias0_ready"), 1)
            pos = vec("pos", 0, 2 * T).rearrange("p (k t) -> p k t", k=KD)
            for m in range(KD):
                first = h[:, m, :].rearrange("p (b t) -> p b t", b=B)[:, :, 0:1]
                link(dve.tensor_tensor(small[:, 4 + m:5 + m], vec("cls", m), pos[:, m, 0:1], ALU.add))
                dve.tensor_copy(first, spread(small[:, 4 + m:5 + m], 1, B))
                link(dve.tensor_scalar(pos[:, m, :], pos[:, m, :], vec("ln2_b", m), None, ALU.add))
            dve.wait_ge(sem("bias_embedded"), 1)
            dve.tensor_tensor(small[:, 44:46], ps[:, 7, 0:KD], vec("lin_b", 0, KD), ALU.add).then_inc(sem("lin_bias_ready"), 1)
            reciprocals(s)
            dve.wait_ge(sem("embedded"), 1)
            for t in range(2):
                dve.wait_ge(sem("rstd_out"), 2 * t + 1)
                for m in range(KD):
                    cols = slice(t * HP, (t + 1) * HP)
                    dve.tensor_tensor(embed[:, m, cols], ps[:, 2 * m + t, 0:HP], rstd_rows[:, cols],
                                      ALU.mult).then_inc(sem("embed_scaled"), 1)
            s = norm_of["embed"]
            centre(s)
            reciprocals(s)
            dve.wait_ge(sem("centred"), s.at + 2)
            for t, at, width, bank, col in s.pieces:
                dve.wait_ge(sem("rstd_spread"), s.at + t + 1)
                for m in range(KD):
                    cols = slice(at, at + width)
                    ins_ = dve.scalar_tensor_tensor(embed[:, m, cols], s.cen[:, m, cols], vec("ln2_w", m),
                                                    ps[:, bank, col:col + width], ALU.mult, ALU.mult)
            link(ins_)
            for m in range(KD):
                ins_ = dve.tensor_tensor(h[:, m, :].rearrange("p (b t) -> p b t", b=B)[:, :, 1:T],
                                         embed[:, m, :].rearrange("p (b t) -> p b t", b=B),
                                         spread(pos[:, m, 1:T], 1, B), ALU.add)
            link(ins_)
            dve.tensor_copy(small[:, 87:88], vec("beta")).then_inc(sem("h_embed"), 1)
            dve.wait_ge(sem("lambda_exp"), 1)
            link(dve.tensor_tensor(small[:, 11:12], small[:, 12:13], small[:, 13:14], ALU.subtract))
            link(dve.tensor_scalar(small[:, 11:12], small[:, 11:12], LAMBDA_INIT, None, ALU.add))
            dve.wait_ge(sem("logit_exp"), 1)
            for n in ("xn_pad", "probs_t_pad", "att_out_pad"):
                dve.wait_ge(sem(n), 1)
            for l in range(4):
                norm(norm_of[f"att{l}"], f"normed_att{l}")
                if l < 3:
                    attention(l)
                else:
                    ema()
                residual(l, "proj_b" if l == 0 else None)
                norm(norm_of[f"moe{l}"], f"normed_moe{l}")
                for t in range(2):
                    cols = slice(t * HN, (t + 1) * HN)
                    dve.wait_ge(sem("x_hi_done"), 2 * l + t + 1)
                    dve.tensor_tensor(x_lo[:, :, cols], xn[:, :, cols], x_hi[:, :, cols].bitcast(F32),
                                      ALU.subtract).then_inc(sem("x_split"), 1)
                for c in range(2):
                    split_weights(l, c, 0)
                route(l)
                experts(l)


def lay_out(x):
    f = {k: np.asarray(v) for k, v in x.items()}

    def cols(v):
        return v.reshape(-1, P).T

    def rows(w):
        return w.reshape(-1, P, w.shape[1]).transpose(1, 0, 2).reshape(P, -1)

    out = {}
    img = f["x"].reshape(B, 3, 6, 16, 6, 16).transpose(3, 5, 1, 0, 2, 4).reshape(PD, PB)
    out["patches"] = img.reshape(PK, P, PB).transpose(1, 0, 2)

    p = np.arange(P)
    c = np.zeros((P, CONSTS_W), np.float32)

    def put(arr, fields, name, val):
        at, w = fields[name]
        arr[:, at:at + w] = np.asarray(val).reshape(-1, w)

    tok = p % 64
    put(c, CONSTS, "ident", np.eye(P))
    put(c, CONSTS, "mean_d", np.full((P, P), 1.0 / D))
    put(c, CONSTS, "mean_pd", np.full((P, P), 1.0 / PD))
    put(c, CONSTS, "eps", np.full((P, 8), EPS))
    put(c, CONSTS, "head16", p[:, None] // 16 == np.arange(8))
    put(c, CONSTS, "head64", p[:, None] // 64 == np.arange(2))
    put(c, CONSTS, "shift", p[:, None] == np.arange(104))
    put(c, CONSTS, "sub", p[:, None] // 8 % 2 == np.arange(2))
    for s in (T, T + 1):
        put(c, CONSTS, f"stack{s}", (p[:, None] // 64 == np.arange(H) % 2) & (tok[:, None] < s))
        keys = np.arange(s)
        hidden = (keys > tok[:, None]) & (tok[:, None] < T) & (keys < T)
        put(c, CONSTS, f"causal{s}", np.where(hidden, MASKED, 0.0))
    out["consts"] = c

    v = np.zeros((P, VECS_W), np.float32)
    for name, src in (("ln1_w", "L0_tok_ln1_w"), ("ln1_b", "L0_tok_ln1_b"), ("lin_b", "L0_tok_lin_b"),
                      ("ln2_w", "L0_tok_ln2_w"), ("ln2_b", "L0_tok_ln2_b"), ("proj_b", "L0_attn_proj_b"),
                      ("gamma", "L3_attn_ln_gamma"), ("ln_beta", "L3_attn_ln_beta"), ("sb2", "L3_ffn_sb2")):
        put(v, VECS, name, cols(f[src]))
    put(v, VECS, "cls", cols(f["L0_tok_cls_token"].reshape(-1)))
    put(v, VECS, "pos", f["L0_tok_pos_embedding"][0, :T].T.reshape(KD, P, T).transpose(1, 0, 2).reshape(P, -1))
    for i, n in enumerate(("q_b", "k_b", "v_b")):
        put(v, VECS, n, cols(f["L0_attn_qkv_b"][i * D:(i + 1) * D]))
    lam = np.concatenate([f[f"L1_attn_{n}"] for n in ("lq1", "lk1", "lq2", "lk2")])
    put(v, VECS, "lambdas", np.tile(lam, (P, 1)))
    put(v, VECS, "rms_w", np.tile(f["L1_attn_rms_w"], 8)[:, None])
    put(v, VECS, "null_k", cols(f["L2_attn_null_k"].reshape(-1)))
    put(v, VECS, "null_v", cols(f["L2_attn_null_v"].reshape(-1)))
    put(v, VECS, "logit_scale", cols(np.repeat(f["L2_attn_logit_scale"], 64)))
    put(v, VECS, "beta", cols(np.repeat(f["L3_attn_beta"], 16)))
    biases = [f["L0_ffn_bs"], f["L1_ffn_expert_bias"], f["L2_ffn_expert_bias"], f["L3_ffn_gate_b"]]
    put(v, VECS, "router_b", np.tile(np.concatenate(biases), (P, 1)))
    out["vecs"] = v

    out["rel"] = f["L0_attn_rel_pos_emb"][255 - (T - 1):255 + T]

    out["weights_lo"] = np.concatenate(
        [rows(f["L0_tok_lin_w"]), rows(f["L0_attn_qkv_w"].T), rows(f["L0_attn_proj_w"].T),
         rows(np.concatenate([f["L1_attn_Wq"], f["L1_attn_Wk"], f["L1_attn_Wv"]], 1)), rows(f["L1_attn_Wo"])], 1)
    out["weights_2"] = np.concatenate(
        [rows(np.concatenate([f["L2_attn_Wq"], f["L2_attn_Wk"], f["L2_attn_Wv"]], 1)), rows(f["L2_attn_Wo"])], 1)
    out["weights_3"] = np.concatenate(
        [rows(np.concatenate([f["L3_attn_Wq"].T, f["L3_attn_Wv"].T, f["L3_attn_Wg"].T], 1)), rows(f["L3_attn_Wo"].T)], 1)
    routers = [f["L0_ffn_Ws"], f["L1_ffn_gate_w"].T, f["L2_ffn_router_weight"].T, f["L3_ffn_gate_w"]]
    out["router_w"] = rows(np.concatenate(routers, 1)).reshape(P, KD, E_ALL)
    out["b2"] = f["L3_ffn_b2"]

    def chunk_rows(m, routed, shared):
        n = routed.shape[2]
        parts = []
        if m.shared:
            s = np.zeros((m.shared_chunks * P, n), np.float32)
            s[:m.shared] = shared
            parts.append(s.reshape(-1, P, n))
        cut = m.per_expert * P
        parts.append(routed[:, :cut].reshape(m.e, m.per_expert, P, n).transpose(1, 0, 2, 3).reshape(-1, P, n))
        if m.tails:
            r = routed[:, cut:].reshape(m.e, m.tails, m.tail_rows, n).transpose(1, 0, 2, 3)
            parts.append(r.reshape(-1, P, n))
        return np.concatenate(parts)

    def pack(l, ups, down, biases=()):
        m = MOE[l]
        cols_ = []
        for routed, shared in ups:
            r = chunk_rows(m, routed, shared)
            cols_.append(r.reshape(-1, P, KD, P).transpose(0, 3, 2, 1).reshape(-1, P, KD * P))
        cols_.append(chunk_rows(m, *down))
        for routed, shared in biases:
            cols_.append(chunk_rows(m, routed[:, :, None], None if shared is None else shared[:, None]))
        return np.concatenate(cols_, 2)

    sw = lambda a: a.transpose(0, 2, 1)
    out["experts0"] = pack(0, [(sw(f["L0_ffn_Wg"]), None), (sw(f["L0_ffn_Wu"]), None)], (f["L0_ffn_Wd"], None))
    out["experts1"] = pack(1, [(f["L1_ffn_w1"], f["L1_ffn_sw1"]), (f["L1_ffn_w3"], f["L1_ffn_sw3"])],
                           (sw(f["L1_ffn_w2"]), f["L1_ffn_sw2"].T))
    out["experts2"] = pack(2, [(sw(f["L2_ffn_w1"]), f["L2_ffn_sw1"])], (f["L2_ffn_w2"], f["L2_ffn_sw2"].T))
    out["experts3"] = pack(3, [(sw(f["L3_ffn_w1"]), f["L3_ffn_sw1"].T), (sw(f["L3_ffn_w3"]), f["L3_ffn_sw3"].T)],
                           (f["L3_ffn_w2"], f["L3_ffn_sw2"]),
                           [(f["L3_ffn_b1"], f["L3_ffn_sb1"]), (f["L3_ffn_b3"], f["L3_ffn_sb3"])])
    return {k: np.ascontiguousarray(a) for k, a in out.items()}


def kernel(**inputs):
    import concourse.bacc as _bacc
    from concourse.bass_utils import run_bass_kernel_spmd as _run

    nc = _bacc.Bacc("TRN2", target_bir_lowering=False, num_devices=1)
    arrays = {f"in_{k}": a for k, a in lay_out(inputs).items()}
    ins = {k[3:]: nc.dram_tensor(k, a.shape, mybir.dt.from_np(a.dtype), kind="ExternalInput").ap()
           for k, a in arrays.items()}
    out = nc.dram_tensor("out_tokens", (P, KD, N), F32, kind="ExternalOutput").ap()
    vit_tower(nc, ins, out)
    r = _run(nc, [arrays], core_ids=[0])
    got = r.results[0]["out_tokens"]
    return np.ascontiguousarray(got.transpose(2, 1, 0).reshape(B, T, D))
```
